# Optimizing a Trainium2 kernel written in Bass

```python
import numpy as np
import jax
import jax.numpy as jnp

def _softmax(x, axis=-1):
    return jax.nn.softmax(x, axis=axis)

def _gelu(x):
    return jax.nn.gelu(x, approximate=True)

def _silu(x):
    return jax.nn.silu(x)

def _sigmoid(x):
    return jax.nn.sigmoid(x)

def _layernorm(x, axis=-1, eps=1e-05):
    m = jnp.mean(x, axis=axis, keepdims=True)
    v = jnp.var(x, axis=axis, keepdims=True)
    return (x - m) / jnp.sqrt(v + eps)

def _scatter_add(tgt, idx, src, axis=0):
    return tgt.at[idx].add(src)

def _segment_sum(src, seg, n):
    return jax.ops.segment_sum(src, seg, n)
kernel_name = 'mk_flamingo_gated_d4_seqx_r8_e4e173'

def setup_inputs(seed: int=0):
    np.random.seed(seed)
    _w = jnp.asarray

    def _rec_inputs():
        import jax
        import jax.numpy as jnp
        _rk = jax.random.key(seed)
        x = 7.22e-05 + 1 * jax.random.normal(jax.random.fold_in(_rk, 1), (32, 128, 128), jnp.float32)
        _lenS = 128 - jax.random.randint(jax.random.fold_in(_rk, 7), (32,), 0, max(1, 128 // 4) + 1, jnp.int32)
        _lenS2 = 128 - jax.random.randint(jax.random.fold_in(_rk, 8), (32,), 0, max(1, 128 // 4) + 1, jnp.int32)
        _ctx_1024P = jax.random.normal(jax.random.fold_in(_rk, 11), (32, 16, 128), jnp.float32)
        _ctx_1024c = jax.random.dirichlet(jax.random.fold_in(_rk, 511), 0.3 * jnp.ones((16,), jnp.float32), (32, 128))
        _ctx_1024t = jnp.einsum('bsk,bkd->bsd', _ctx_1024c, _ctx_1024P)
        _ctx_1024t = _ctx_1024t * jax.lax.rsqrt(jnp.mean(jnp.square(_ctx_1024t)) + 1e-12) * 0.953939
        ctx_1024 = -1.39393e-06 + 0.999914 * (_ctx_1024t + 0.3 * jax.random.normal(jax.random.fold_in(_rk, 611), (32, 128, 128), jnp.float32))
        _validS = jnp.arange(128)[None, :] < _lenS[:, None]
        _validS2 = jnp.arange(128)[None, :] < _lenS2[:, None]
        _causal = jnp.tril(jnp.ones((128, 128), dtype=bool))
        mask_BxS2_bf1 = jnp.ones((32, 128), dtype=bool)
        mask_Bx1x1xS2_ik0 = jnp.where(jnp.broadcast_to(_validS2[:, None, None, :], (32, 1, 1, 128)), 0, 1).astype(jnp.int32)
        _g = jax.random.normal(jax.random.fold_in(_rk, 9001), (2, 4), jnp.float32)
        _g = jnp.sign(_g) * jnp.maximum(jnp.abs(_g), 1.0) + (_g == 0) * 1.0
        g_xattn = _g[0]
        g_ffn = _g[1]
        return (x, ctx_1024, mask_BxS2_bf1, mask_Bx1x1xS2_ik0, g_xattn, g_ffn)
    x, ctx_1024, mask_BxS2_bf1, mask_Bx1x1xS2_ik0, g_xattn, g_ffn = _rec_inputs()

    def _L0_xattn_setup():
        import jax, jax.numpy as jnp
        import numpy as np
        HEADS = 16
        DIM_HEAD = 64
        SCALE = DIM_HEAD ** (-0.5)
        key = jax.random.key(seed)
        ks = jax.random.split(key, 6)
        B, Nq, Nkv, D = (4, 256, 128, 128)
        inner = HEADS * DIM_HEAD
        return {'x': jax.random.normal(ks[0], (B, Nq, D), dtype=jnp.float32), 'context': jax.random.normal(ks[1], (B, Nkv, D), dtype=jnp.float32), 'mask': jnp.ones((B, Nkv), dtype=bool), 'Wq': jax.random.normal(ks[2], (inner, D), dtype=jnp.float32) * D ** (-0.5), 'Wkv': jax.random.normal(ks[3], (2 * inner, D), dtype=jnp.float32) * D ** (-0.5), 'Wout': jax.random.normal(ks[4], (D, inner), dtype=jnp.float32) * inner ** (-0.5), 'b_out': jnp.zeros((D,), dtype=jnp.float32)}
    _L0_xattn_all = _L0_xattn_setup()
    _L0_xattn_in = {k: v for k, v in _L0_xattn_all.items() if k in ('Wq', 'Wkv', 'Wout', 'b_out')}
    del _L0_xattn_all

    def _L0_ffn_setup():
        import jax, jax.numpy as jnp
        import numpy as np
        HIDDEN = 128
        INNER = 512

        def _weight_quant(w):
            scale = 1.0 / jnp.clip(jnp.mean(jnp.abs(w)), 1e-05)
            wq = jnp.clip(jnp.round(w * scale), -1.0, 1.0) / scale
            return w + jax.lax.stop_gradient(wq - w)

        def _act_quant(x):
            scale = 127.0 / jnp.clip(jnp.max(jnp.abs(x), axis=-1, keepdims=True), 1e-05)
            xq = jnp.clip(jnp.round(x * scale), -128.0, 127.0) / scale
            return x + jax.lax.stop_gradient(xq - x)

        def _bitlinear(x, w):
            return jnp.einsum('bsi,oi->bso', _act_quant(x), _weight_quant(w))
        key = jax.random.key(seed)
        k0, k1, k2, k3 = jax.random.split(key, 4)
        x = jax.random.normal(k0, (4, 256, HIDDEN), dtype=jnp.float32)
        w_gate = jax.random.normal(k1, (INNER, HIDDEN), dtype=jnp.float32) / np.sqrt(HIDDEN)
        w_up = jax.random.normal(k2, (INNER, HIDDEN), dtype=jnp.float32) / np.sqrt(HIDDEN)
        w_down = jax.random.normal(k3, (HIDDEN, INNER), dtype=jnp.float32) / np.sqrt(INNER)
        return {'x': x, 'w_gate': w_gate, 'w_up': w_up, 'w_down': w_down}
    _L0_ffn_all = _L0_ffn_setup()
    _L0_ffn_in = {k: v for k, v in _L0_ffn_all.items() if k in ('w_gate', 'w_up', 'w_down')}
    del _L0_ffn_all

    def _L1_xattn_setup():
        import jax, jax.numpy as jnp
        import numpy as np
        D_MODEL = 128
        NUM_HEADS = 16
        D_K = D_MODEL // NUM_HEADS
        MAX_REL = 128
        key = jax.random.key(seed)
        ks = jax.random.split(key, 16)
        B, S = (4, 256)
        s = 1.0 / np.sqrt(D_MODEL)
        inp = {'query': jax.random.normal(ks[0], (B, S, D_MODEL), jnp.float32), 'key': jax.random.normal(ks[1], (B, S, D_MODEL), jnp.float32), 'value': jax.random.normal(ks[2], (B, S, D_MODEL), jnp.float32), 'mask': jax.random.randint(ks[3], (B, 1, 1, S), 0, 2, jnp.int32), 'Wq': jax.random.normal(ks[4], (D_MODEL, D_MODEL), jnp.float32) * s, 'bq': jax.random.normal(ks[5], (D_MODEL,), jnp.float32) * 0.02, 'Wk': jax.random.normal(ks[6], (D_MODEL, D_MODEL), jnp.float32) * s, 'bk': jax.random.normal(ks[7], (D_MODEL,), jnp.float32) * 0.02, 'Wv': jax.random.normal(ks[8], (D_MODEL, D_MODEL), jnp.float32) * s, 'bv': jax.random.normal(ks[9], (D_MODEL,), jnp.float32) * 0.02, 'Wo': jax.random.normal(ks[10], (D_MODEL, D_MODEL), jnp.float32) * s, 'bo': jax.random.normal(ks[11], (D_MODEL,), jnp.float32) * 0.02, 'rel_emb': jax.random.normal(ks[12], (2 * MAX_REL + 1, NUM_HEADS), jnp.float32) * 0.02}
        return inp
    _L1_xattn_all = _L1_xattn_setup()
    _L1_xattn_in = {k: v for k, v in _L1_xattn_all.items() if k in ('Wq', 'bq', 'Wk', 'bk', 'Wv', 'bv', 'Wo', 'bo', 'rel_emb')}
    del _L1_xattn_all

    def _L1_ffn_setup():
        import jax, jax.numpy as jnp
        import numpy as np
        B, L, D = (4, 64, 128)
        E, TOP_K = (16, 4)
        F = 4 * D
        key = jax.random.key(seed)
        ks = jax.random.split(key, 6)
        scale = 0.02
        return {'x': jax.random.normal(ks[0], (B, L, D), jnp.float32), 'keys': jax.random.normal(ks[1], (E, D), jnp.float32), 'w1': jax.random.normal(ks[2], (E, F, D), jnp.float32) * scale, 'b1': jnp.zeros((E, F), jnp.float32), 'w2': jax.random.normal(ks[3], (E, D, F), jnp.float32) * scale, 'b2': jnp.zeros((E, D), jnp.float32), 'rw': jax.random.normal(ks[4], (E, D), jnp.float32) * scale, 'rb': jnp.zeros((E,), jnp.float32)}
    _L1_ffn_all = _L1_ffn_setup()
    _L1_ffn_in = {k: v for k, v in _L1_ffn_all.items() if k in ('keys', 'w1', 'b1', 'w2', 'b2', 'rw', 'rb')}
    del _L1_ffn_all

    def _L2_xattn_setup():
        import jax, jax.numpy as jnp
        import numpy as np
        EPS = 1e-05

        def layer_norm(x, g, b):
            mu = jnp.mean(x, axis=-1, keepdims=True)
            var = jnp.var(x, axis=-1, keepdims=True)
            return (x - mu) * jax.lax.rsqrt(var + EPS) * g + b
        key = jax.random.key(seed)
        ks = jax.random.split(key, 8)
        dim, heads, dim_head = (128, 16, 64)
        inner = heads * dim_head
        b, n, m = (8, 512, 64)
        s = dim ** (-0.5)
        return {'x': jax.random.normal(ks[0], (b, n, dim), jnp.float32), 'latents': jax.random.normal(ks[1], (b, m, dim), jnp.float32), 'ln_m_g': jnp.ones((dim,), jnp.float32), 'ln_m_b': jnp.zeros((dim,), jnp.float32), 'ln_l_g': jnp.ones((dim,), jnp.float32), 'ln_l_b': jnp.zeros((dim,), jnp.float32), 'Wq': jax.random.normal(ks[2], (dim, inner), jnp.float32) * s, 'Wkv': jax.random.normal(ks[3], (dim, 2 * inner), jnp.float32) * s, 'Wout': jax.random.normal(ks[4], (inner, dim), jnp.float32) * s}
    _L2_xattn_all = _L2_xattn_setup()
    _L2_xattn_in = {k: v for k, v in _L2_xattn_all.items() if k in ('ln_m_g', 'ln_m_b', 'ln_l_g', 'ln_l_b', 'Wq', 'Wkv', 'Wout')}
    del _L2_xattn_all

    def _L2_ffn_setup():
        import jax, jax.numpy as jnp
        import numpy as np
        QB = 127.0
        EPS = 1e-05

        def _ste(x, q):
            return x + jax.lax.stop_gradient(q - x)

        def bitlinear(x, W, b):
            w_scale = jnp.clip(jnp.mean(jnp.abs(W)), EPS, None)
            Wq = _ste(W, jnp.clip(jnp.round(W / w_scale), -1.0, 1.0) * w_scale)
            x_scale = jnp.clip(jnp.max(jnp.abs(x), axis=-1, keepdims=True), EPS, None)
            xq = _ste(x, jnp.clip(jnp.round(x * (QB / x_scale)), -QB - 1.0, QB) * (x_scale / QB))
            return jnp.einsum('bnd,hd->bnh', xq, Wq) + b
        key = jax.random.key(seed)
        k0, k1, k2 = jax.random.split(key, 3)
        B, N, D = (8, 512, 128)
        H = int(D * 4.0)
        x = jax.random.normal(k0, (B, N, D), dtype=jnp.float32)
        W1 = jax.random.normal(k1, (H, D), dtype=jnp.float32) * 0.02
        b1 = jnp.zeros((H,), dtype=jnp.float32)
        W2 = jax.random.normal(k2, (D, H), dtype=jnp.float32) * 0.02
        b2 = jnp.zeros((D,), dtype=jnp.float32)
        return {'x': x, 'W1': W1, 'b1': b1, 'W2': W2, 'b2': b2}
    _L2_ffn_all = _L2_ffn_setup()
    _L2_ffn_in = {k: v for k, v in _L2_ffn_all.items() if k in ('W1', 'b1', 'W2', 'b2')}
    del _L2_ffn_all

    def _L3_xattn_setup():
        import jax, jax.numpy as jnp
        import numpy as np
        E = 128
        H = 16
        D = E // H
        B, S = (4, 256)

        def _split_heads(x):
            b, s, _ = x.shape
            return x.reshape(b, s, H, D).transpose(0, 2, 1, 3)
        key = jax.random.key(seed)
        ks = jax.random.split(key, 12)
        sc = 1.0 / np.sqrt(E)
        inp = {'query': jax.random.normal(ks[0], (B, S, E), jnp.float32), 'key': jax.random.normal(ks[1], (B, S, E), jnp.float32), 'value': jax.random.normal(ks[2], (B, S, E), jnp.float32), 'Wq': jax.random.normal(ks[3], (E, E), jnp.float32) * sc, 'bq': jax.random.normal(ks[4], (E,), jnp.float32) * sc, 'Wk': jax.random.normal(ks[5], (E, E), jnp.float32) * sc, 'bk': jax.random.normal(ks[6], (E,), jnp.float32) * sc, 'Wv': jax.random.normal(ks[7], (E, E), jnp.float32) * sc, 'bv': jax.random.normal(ks[8], (E,), jnp.float32) * sc, 'Wo': jax.random.normal(ks[9], (E, E), jnp.float32) * sc, 'bo': jax.random.normal(ks[10], (E,), jnp.float32) * sc}
        return inp
    _L3_xattn_all = _L3_xattn_setup()
    _L3_xattn_in = {k: v for k, v in _L3_xattn_all.items() if k in ('Wq', 'bq', 'Wk', 'bk', 'Wv', 'bv', 'Wo', 'bo')}
    del _L3_xattn_all

    def _L3_ffn_setup():
        import jax, jax.numpy as jnp
        import numpy as np
        B, T, D, E, H = (4, 128, 128, 8, 256)
        key = jax.random.key(seed)
        ks = jax.random.split(key, 5)
        bound_bank = 1.0 / np.sqrt(D)
        bound_down = 1.0 / np.sqrt(H)
        return {'x': jax.random.normal(ks[0], (B, T, D), dtype=jnp.float32), 'gate_w': jax.random.uniform(ks[1], (E, D), jnp.float32, -bound_bank, bound_bank), 'gate_bank': jax.random.uniform(ks[2], (E, D, H), jnp.float32, -bound_bank, bound_bank), 'up_bank': jax.random.uniform(ks[3], (E, D, H), jnp.float32, -bound_bank, bound_bank), 'down_bank': jax.random.uniform(ks[4], (E, H, D), jnp.float32, -bound_down, bound_down)}
    _L3_ffn_all = _L3_ffn_setup()
    _L3_ffn_in = {k: v for k, v in _L3_ffn_all.items() if k in ('gate_w', 'gate_bank', 'up_bank', 'down_bank')}
    del _L3_ffn_all
    return {'x': x, 'ctx_1024': ctx_1024, 'mask_BxS2_bf1': mask_BxS2_bf1, 'mask_Bx1x1xS2_ik0': mask_Bx1x1xS2_ik0, 'g_xattn': g_xattn, 'g_ffn': g_ffn, 'L0_xattn_Wq': _L0_xattn_in['Wq'], 'L0_xattn_Wkv': _L0_xattn_in['Wkv'], 'L0_xattn_Wout': _L0_xattn_in['Wout'], 'L0_xattn_b_out': _L0_xattn_in['b_out'], 'L0_ffn_w_gate': _L0_ffn_in['w_gate'], 'L0_ffn_w_up': _L0_ffn_in['w_up'], 'L0_ffn_w_down': _L0_ffn_in['w_down'], 'L1_xattn_Wq': _L1_xattn_in['Wq'], 'L1_xattn_bq': _L1_xattn_in['bq'], 'L1_xattn_Wk': _L1_xattn_in['Wk'], 'L1_xattn_bk': _L1_xattn_in['bk'], 'L1_xattn_Wv': _L1_xattn_in['Wv'], 'L1_xattn_bv': _L1_xattn_in['bv'], 'L1_xattn_Wo': _L1_xattn_in['Wo'], 'L1_xattn_bo': _L1_xattn_in['bo'], 'L1_xattn_rel_emb': _L1_xattn_in['rel_emb'], 'L1_ffn_keys': _L1_ffn_in['keys'], 'L1_ffn_w1': _L1_ffn_in['w1'], 'L1_ffn_b1': _L1_ffn_in['b1'], 'L1_ffn_w2': _L1_ffn_in['w2'], 'L1_ffn_b2': _L1_ffn_in['b2'], 'L1_ffn_rw': _L1_ffn_in['rw'], 'L1_ffn_rb': _L1_ffn_in['rb'], 'L2_xattn_ln_m_g': _L2_xattn_in['ln_m_g'], 'L2_xattn_ln_m_b': _L2_xattn_in['ln_m_b'], 'L2_xattn_ln_l_g': _L2_xattn_in['ln_l_g'], 'L2_xattn_ln_l_b': _L2_xattn_in['ln_l_b'], 'L2_xattn_Wq': _L2_xattn_in['Wq'], 'L2_xattn_Wkv': _L2_xattn_in['Wkv'], 'L2_xattn_Wout': _L2_xattn_in['Wout'], 'L2_ffn_W1': _L2_ffn_in['W1'], 'L2_ffn_b1': _L2_ffn_in['b1'], 'L2_ffn_W2': _L2_ffn_in['W2'], 'L2_ffn_b2': _L2_ffn_in['b2'], 'L3_xattn_Wq': _L3_xattn_in['Wq'], 'L3_xattn_bq': _L3_xattn_in['bq'], 'L3_xattn_Wk': _L3_xattn_in['Wk'], 'L3_xattn_bk': _L3_xattn_in['bk'], 'L3_xattn_Wv': _L3_xattn_in['Wv'], 'L3_xattn_bv': _L3_xattn_in['bv'], 'L3_xattn_Wo': _L3_xattn_in['Wo'], 'L3_xattn_bo': _L3_xattn_in['bo'], 'L3_ffn_gate_w': _L3_ffn_in['gate_w'], 'L3_ffn_gate_bank': _L3_ffn_in['gate_bank'], 'L3_ffn_up_bank': _L3_ffn_in['up_bank'], 'L3_ffn_down_bank': _L3_ffn_in['down_bank']}

def reference(x, ctx_1024, mask_BxS2_bf1, mask_Bx1x1xS2_ik0, g_xattn, g_ffn, L0_xattn_Wq, L0_xattn_Wkv, L0_xattn_Wout, L0_xattn_b_out, L0_ffn_w_gate, L0_ffn_w_up, L0_ffn_w_down, L1_xattn_Wq, L1_xattn_bq, L1_xattn_Wk, L1_xattn_bk, L1_xattn_Wv, L1_xattn_bv, L1_xattn_Wo, L1_xattn_bo, L1_xattn_rel_emb, L1_ffn_keys, L1_ffn_w1, L1_ffn_b1, L1_ffn_w2, L1_ffn_b2, L1_ffn_rw, L1_ffn_rb, L2_xattn_ln_m_g, L2_xattn_ln_m_b, L2_xattn_ln_l_g, L2_xattn_ln_l_b, L2_xattn_Wq, L2_xattn_Wkv, L2_xattn_Wout, L2_ffn_W1, L2_ffn_b1, L2_ffn_W2, L2_ffn_b2, L3_xattn_Wq, L3_xattn_bq, L3_xattn_Wk, L3_xattn_bk, L3_xattn_Wv, L3_xattn_bv, L3_xattn_Wo, L3_xattn_bo, L3_ffn_gate_w, L3_ffn_gate_bank, L3_ffn_up_bank, L3_ffn_down_bank):
    import jax
    import jax.numpy as jnp

    def _L0_xattn_ref(x, context, mask, Wq, Wkv, Wout, b_out):
        import jax, jax.numpy as jnp
        import numpy as np
        HEADS = 16
        DIM_HEAD = 64
        SCALE = DIM_HEAD ** (-0.5)
        B, Nq, _ = x.shape
        Nkv = context.shape[1]
        q = x @ Wq.T
        kv = context @ Wkv.T
        k, v = jnp.split(kv, 2, axis=-1)
        q = q.reshape(B, Nq, HEADS, DIM_HEAD).transpose(0, 2, 1, 3)
        k = k.reshape(B, Nkv, HEADS, DIM_HEAD).transpose(0, 2, 1, 3)
        v = v.reshape(B, Nkv, HEADS, DIM_HEAD).transpose(0, 2, 1, 3)
        sim = jnp.einsum('bhid,bhjd->bhij', q, k) * SCALE
        max_neg = -jnp.finfo(sim.dtype).max
        sim = jnp.where(mask[:, None, None, :], sim, max_neg)
        attn = jax.nn.softmax(sim, axis=-1)
        out = jnp.einsum('bhij,bhjd->bhid', attn, v)
        out = out.transpose(0, 2, 1, 3).reshape(B, Nq, HEADS * DIM_HEAD)
        return out @ Wout.T + b_out

    def _L0_ffn_ref(x, w_gate, w_up, w_down):
        import jax, jax.numpy as jnp
        import numpy as np
        HIDDEN = 128
        INNER = 512

        def _weight_quant(w):
            scale = 1.0 / jnp.clip(jnp.mean(jnp.abs(w)), 1e-05)
            wq = jnp.clip(jnp.round(w * scale), -1.0, 1.0) / scale
            return w + jax.lax.stop_gradient(wq - w)

        def _act_quant(x):
            scale = 127.0 / jnp.clip(jnp.max(jnp.abs(x), axis=-1, keepdims=True), 1e-05)
            xq = jnp.clip(jnp.round(x * scale), -128.0, 127.0) / scale
            return x + jax.lax.stop_gradient(xq - x)

        def _bitlinear(x, w):
            return jnp.einsum('bsi,oi->bso', _act_quant(x), _weight_quant(w))
        gate = jax.nn.silu(_bitlinear(x, w_gate))
        up = _bitlinear(x, w_up)
        return _bitlinear(gate * up, w_down)

    def _L1_xattn_ref(query, key, value, mask, Wq, bq, Wk, bk, Wv, bv, Wo, bo, rel_emb):
        import jax, jax.numpy as jnp
        import numpy as np
        D_MODEL = 128
        NUM_HEADS = 16
        D_K = D_MODEL // NUM_HEADS
        MAX_REL = 128
        B, S, D = query.shape
        H, dk = (NUM_HEADS, D_K)

        def proj(x, W, b):
            return (x @ W.T + b).reshape(B, S, H, dk).transpose(0, 2, 1, 3)
        Q = proj(query, Wq, bq)
        K = proj(key, Wk, bk)
        V = proj(value, Wv, bv)
        scores = jnp.einsum('bhqd,bhkd->bhqk', Q, K) / jnp.sqrt(jnp.float32(dk))
        pos = jnp.arange(S)
        rel = jnp.clip(pos[None, :] - pos[:, None], -MAX_REL, MAX_REL) + MAX_REL
        bias = rel_emb[rel].transpose(2, 0, 1)
        scores = scores + bias[None]
        scores = jnp.where(mask == 0, -jnp.inf, scores)
        weights = jax.nn.softmax(scores, axis=-1)
        weights = jnp.nan_to_num(weights, nan=0.0)
        context = jnp.einsum('bhqk,bhkd->bhqd', weights, V)
        context = context.transpose(0, 2, 1, 3).reshape(B, S, D)
        return context @ Wo.T + bo

    def _L1_ffn_ref(x, keys, w1, b1, w2, b2, rw, rb):
        import jax, jax.numpy as jnp
        import numpy as np
        B, L, D = (4, 64, 128)
        E, TOP_K = (16, 4)
        F = 4 * D
        diff = x[:, :, None, :] - keys
        dist2 = jnp.sum(diff * diff, axis=-1)
        logits = -dist2 + jnp.einsum('bld,ed->ble', x, rw) + rb
        topv, topi = jax.lax.top_k(logits, TOP_K)
        w = jax.nn.softmax(topv, axis=-1)
        hidden = jax.nn.gelu(jnp.einsum('bld,efd->blef', x, w1) + b1, approximate=False)
        exp_out = jnp.einsum('blef,edf->bled', hidden, w2) + b2
        sel = jnp.take_along_axis(exp_out, topi[..., None], axis=2)
        fused = jnp.sum(w[..., None] * sel, axis=2)
        return fused

    def _L2_xattn_ref(x, latents, ln_m_g, ln_m_b, ln_l_g, ln_l_b, Wq, Wkv, Wout):
        import jax, jax.numpy as jnp
        import numpy as np
        EPS = 1e-05

        def layer_norm(x, g, b):
            mu = jnp.mean(x, axis=-1, keepdims=True)
            var = jnp.var(x, axis=-1, keepdims=True)
            return (x - mu) * jax.lax.rsqrt(var + EPS) * g + b
        heads, dim_head = (16, 64)
        scale = dim_head ** (-0.5)
        x = layer_norm(x, ln_m_g, ln_m_b)
        lat = layer_norm(latents, ln_l_g, ln_l_b)
        b, m, _ = lat.shape
        q = lat @ Wq
        kv_input = jnp.concatenate([x, lat], axis=1)
        kv = kv_input @ Wkv
        k, v = jnp.split(kv, 2, axis=-1)

        def split_heads(t):
            return t.reshape(t.shape[0], t.shape[1], heads, dim_head).transpose(0, 2, 1, 3)
        q, k, v = (split_heads(q), split_heads(k), split_heads(v))
        dots = jnp.einsum('bhid,bhjd->bhij', q, k) * scale
        attn = jax.nn.softmax(dots, axis=-1)
        out = jnp.einsum('bhij,bhjd->bhid', attn, v)
        out = out.transpose(0, 2, 1, 3).reshape(b, m, heads * dim_head)
        return out @ Wout

    def _L2_ffn_ref(x, W1, b1, W2, b2):
        import jax, jax.numpy as jnp
        import numpy as np
        QB = 127.0
        EPS = 1e-05

        def _ste(x, q):
            return x + jax.lax.stop_gradient(q - x)

        def bitlinear(x, W, b):
            w_scale = jnp.clip(jnp.mean(jnp.abs(W)), EPS, None)
            Wq = _ste(W, jnp.clip(jnp.round(W / w_scale), -1.0, 1.0) * w_scale)
            x_scale = jnp.clip(jnp.max(jnp.abs(x), axis=-1, keepdims=True), EPS, None)
            xq = _ste(x, jnp.clip(jnp.round(x * (QB / x_scale)), -QB - 1.0, QB) * (x_scale / QB))
            return jnp.einsum('bnd,hd->bnh', xq, Wq) + b
        h = bitlinear(x, W1, b1)
        h = jax.nn.gelu(h, approximate=False)
        return bitlinear(h, W2, b2)

    def _L3_xattn_ref(query, key, value, Wq, bq, Wk, bk, Wv, bv, Wo, bo):
        import jax, jax.numpy as jnp
        import numpy as np
        E = 128
        H = 16
        D = E // H
        B, S = (4, 256)

        def _split_heads(x):
            b, s, _ = x.shape
            return x.reshape(b, s, H, D).transpose(0, 2, 1, 3)
        q = _split_heads(query @ Wq + bq)
        k = _split_heads(key @ Wk + bk)
        v = _split_heads(value @ Wv + bv)
        scale = 1.0 / jnp.sqrt(jnp.asarray(D, q.dtype))
        scores = jnp.einsum('bhqd,bhkd->bhqk', q, k) * scale
        probs = jax.nn.softmax(scores, axis=-1)
        attn = jnp.einsum('bhqk,bhkd->bhqd', probs, v)
        attn = attn.transpose(0, 2, 1, 3).reshape(query.shape[0], -1, E)
        return attn @ Wo + bo

    def _L3_ffn_ref(x, gate_w, gate_bank, up_bank, down_bank):
        import jax, jax.numpy as jnp
        import numpy as np
        B, T, D, E, H = (4, 128, 128, 8, 256)
        logits = jnp.einsum('btd,ed->bte', x, gate_w)
        selected = jnp.argmax(logits, axis=-1)
        u = jnp.einsum('btd,edh->bteh', x, up_bank)
        a = jnp.einsum('btd,edh->bteh', x, gate_bank)
        h = jax.nn.silu(a) * u
        y = jnp.einsum('bteh,ehd->bted', h, down_bank)
        idx = selected[:, :, None, None]
        out = jnp.take_along_axis(y, idx, axis=2)[:, :, 0, :]
        return out
    x = x + jnp.tanh(g_xattn[0]) * _L0_xattn_ref(_layernorm(x, axis=-1), ctx_1024, mask_BxS2_bf1, L0_xattn_Wq, L0_xattn_Wkv, L0_xattn_Wout, L0_xattn_b_out)
    x = x + jnp.tanh(g_ffn[0]) * _L0_ffn_ref(_layernorm(x, axis=-1), L0_ffn_w_gate, L0_ffn_w_up, L0_ffn_w_down)
    x = x + jnp.tanh(g_xattn[1]) * _L1_xattn_ref(_layernorm(x, axis=-1), ctx_1024, ctx_1024, mask_Bx1x1xS2_ik0, L1_xattn_Wq, L1_xattn_bq, L1_xattn_Wk, L1_xattn_bk, L1_xattn_Wv, L1_xattn_bv, L1_xattn_Wo, L1_xattn_bo, L1_xattn_rel_emb)
    x = x + jnp.tanh(g_ffn[1]) * _L1_ffn_ref(_layernorm(x, axis=-1), L1_ffn_keys, L1_ffn_w1, L1_ffn_b1, L1_ffn_w2, L1_ffn_b2, L1_ffn_rw, L1_ffn_rb)
    x = x + jnp.tanh(g_xattn[2]) * _L2_xattn_ref(ctx_1024, _layernorm(x, axis=-1), L2_xattn_ln_m_g, L2_xattn_ln_m_b, L2_xattn_ln_l_g, L2_xattn_ln_l_b, L2_xattn_Wq, L2_xattn_Wkv, L2_xattn_Wout)
    x = x + jnp.tanh(g_ffn[2]) * _L2_ffn_ref(_layernorm(x, axis=-1), L2_ffn_W1, L2_ffn_b1, L2_ffn_W2, L2_ffn_b2)
    x = x + jnp.tanh(g_xattn[3]) * _L3_xattn_ref(_layernorm(x, axis=-1), ctx_1024, ctx_1024, L3_xattn_Wq, L3_xattn_bq, L3_xattn_Wk, L3_xattn_bk, L3_xattn_Wv, L3_xattn_bv, L3_xattn_Wo, L3_xattn_bo)
    x = x + jnp.tanh(g_ffn[3]) * _L3_ffn_ref(_layernorm(x, axis=-1), L3_ffn_gate_w, L3_ffn_gate_bank, L3_ffn_up_bank, L3_ffn_down_bank)
    return x

_drawn_inputs = setup_inputs


def setup_inputs(seed=0):
    import zlib

    import numpy as np

    out = dict(_drawn_inputs(seed))
    spreads = {'L0_xattn_b_out': (0.0, 0.1),
     'L1_ffn_b1': (0.0, 0.44),
     'L1_ffn_b2': (0.0, 0.1),
     'L1_ffn_rb': (0.0, 2.0),
     'L2_xattn_ln_m_g': (1.0, 0.2),
     'L2_xattn_ln_m_b': (0.0, 0.1),
     'L2_xattn_ln_l_g': (1.0, 0.2),
     'L2_xattn_ln_l_b': (0.0, 0.1),
     'L2_ffn_b1': (0.0, 0.8),
     'L2_ffn_b2': (0.0, 0.1)}
    factors = {'g_ffn': 8.0,
     'L1_xattn_bq': 8.0,
     'L1_xattn_bk': 64.0,
     'L1_xattn_bv': 2.796,
     'L1_xattn_rel_emb': 8.0,
     'L1_ffn_rw': 8.0,
     'L2_ffn_W1': 4.413,
     'L2_ffn_W2': 3.803,
     'L3_xattn_bq': 5.322,
     'L3_xattn_bk': 64.0}
    for name, (base, spread) in spreads.items():
        noise = np.random.default_rng([zlib.crc32(name.encode()), seed]).standard_normal(out[name].shape)
        drawn = base * np.exp(spread * noise) if base else spread * noise
        out[name] = jnp.asarray(drawn.astype(out[name].dtype))
    for name, factor in factors.items():
        out[name] = (out[name] * factor).astype(out[name].dtype)
    return out
```

```python
from contextlib import ExitStack

import concourse.bass as bass
from concourse import mybir

P = 128
B = 32
D = 128
GB = 4
W = GB * P
NG = B // GB
UN = 2
DH = 64
HEADS = 16
NEG = -1.0e30
EPS = 1e-5
MAGIC = 12582912.0

ALU = mybir.AluOpType
ACT = mybir.ActivationFunctionType
BF16 = mybir.dt.bfloat16
F32 = mybir.dt.float32
I32 = mybir.dt.int32
U8 = mybir.dt.uint8
AX = mybir.AxisListType


class Signal:

    def __init__(self, sem, base, per, credit):
        self.sem, self.base, self.per, self.credit = sem, base, per, credit

    def at(self, t, n=1):
        return t * self.per + (self.base + self.credit + n)


class Signals:

    def __init__(self, nc, ctx):
        self.nc, self.ctx, self.sems, self.end = nc, ctx, {}, {}

    def new(self, name, per=1, credit=0, groups=NG, extra=0):
        if name not in self.sems:
            self.sems[name] = self.ctx.enter_context(self.nc.semaphore(name))
        base = self.end.get(name, 0)
        self.end[name] = base + credit + per * groups + extra
        return Signal(self.sems[name], base, per, credit)


class Core:
    pass


class Loads:

    def __init__(self, S, name, pairs):
        self.pairs = pairs
        self.landed = S.new(name, per=16 * len(pairs), groups=1)

    def start(self, sp):
        for dst, src in self.pairs:
            sp.dma_start(dst, src).then_inc(self.landed.sem, 16)

    def finish(self, sp):
        sp.wait_ge(self.landed.sem, self.landed.at(0, 16 * len(self.pairs)))


def ones_like(c, row):
    p = row.start_partition()
    return c.ones[p:p + 1, :]



class Norm:

    def __init__(self, nc, ctx, S, name, tag="", turns=True):
        def sb(n, shape):
            return ctx.enter_context(nc.sbuf_tensor(f"{name}_{n}{tag}", shape, F32))

        self.st = sb("ln_st", [P, GB, 6])
        self.mv = sb("ln_mv", [P, GB, 2])
        self.ve = sb("ln_ve", [P, GB])
        self.rs = sb("ln_rs", [P, GB])
        self.xn = sb("ln_xn", [P, GB, D])
        self.spare = sb("ln_spare", [P, 1])
        self.stats = S.new("ln_stats_done" + tag, groups=NG + 1)
        self.moments = S.new("ln_moments_done" + tag, groups=NG + 1)
        self.veps = S.new("ln_veps_done" + tag, groups=NG + 1)
        self.rstd = S.new("ln_rstd_done" + tag, groups=NG + 1)
        self.normed = S.new("ln_normed" + tag, groups=NG + 1)
        if not turns:
            return
        self.out = sb("ln_T", [P, UN, W])
        self.turned = S.new("ln_turned" + tag, groups=NG + 1)

    def stats_dve(self, nc, dve, t, src):
        for j in range(GB):
            ins = nc.vector.bn_stats(self.st[:, j, :], src(t, j))
        ins.then_inc(self.stats.sem, 1)
        dve.wait_ge(self.stats.sem, self.stats.at(t))
        nc.vector.memset(self.spare[:, :], 0.0)
        for j in range(GB):
            ins = nc.vector.bn_aggr(self.mv[:, j, :], self.st[:, j, :])
        ins.then_inc(self.moments.sem, 1)
        dve.wait_ge(self.moments.sem, self.moments.at(t))
        nc.vector.tensor_scalar(self.ve[:, :], self.mv[:, :, 1], EPS, None, ALU.add).then_inc(self.veps.sem, 1)

    def rstd_pool(self, nc, pool, t, minus_half):
        pool.wait_ge(self.veps.sem, self.veps.at(t))
        nc.gpsimd.tensor_tensor(self.rs[:, :], self.ve[:, :], minus_half[:, 0:GB], ALU.pow)\
            .then_inc(self.rstd.sem, 1)

    def apply_dve(self, nc, dve, t, src, first=False):
        dve.wait_ge(self.rstd.sem, self.rstd.at(t))
        if not first:
            dve.wait_ge(self.turned.sem, self.turned.at(t, 0))
        for j in range(GB):
            ins = nc.vector.tensor_scalar(self.xn[:, j, :], src(t, j), self.mv[:, j, 0:1], self.rs[:, j:j + 1],
                                          ALU.subtract, ALU.mult)
        ins.then_inc(self.normed.sem, 1)

    def turn_pe(self, nc, pe, t, bank, ident):
        pe.wait_ge(self.normed.sem, self.normed.at(t))
        for j in range(GB):
            ins = nc.tensor.transpose(bank[:, j * P:(j + 1) * P], self.xn[:, j, :], ident)
        ins.then_inc(self.turned.sem, 1)



def attention64(nc, c, S, name, NS, wq, wk, wv, wo, masked, affine, gate, bias_row, loads=None):
    M = HEADS // 2
    BQ = GB // NS
    QM = 2 * NS
    NQ = M * QM
    UP = 1 + 2 * NS
    UG = M * UP + NS
    TG = M * (QM + 1)
    KL = NS * P
    LNQ = NQ // 2
    SCALE = float(DH) ** -0.5

    def proj_use(m, k):
        return m * UP + k + (NS if QM * m - 1 > LNQ else 0)

    LN_USE = UP * sum(1 for m in range(M) if QM * m - 1 <= LNQ)

    def proj_bank(u, k):
        return (NS + u * UG + k) % 2

    def turn_step(m):
        return QM * (m + 1) + 1

    def probs_use(q):
        return q + sum(1 for m in range(M) if turn_step(m) < q)

    def out_use(m):
        return min(turn_step(m) + 1, NQ) + m

    with ExitStack() as ctx:
        def sb(n, shape, dt=F32):
            return ctx.enter_context(nc.sbuf_tensor(f"{name}_{n}", shape, dt))

        def ps(n):
            return ctx.enter_context(nc.psum_tensor(f"{name}_{n}", [P, W], F32))

        pj = [ps(f"proj{i}") for i in range(2)]
        sc = [ps(f"scores{i}") for i in range(2)]
        pt = [ps(f"turned{i}") for i in range(2)]
        po = ps("pv")
        acc = ps("acc")
        QT = sb("QT", [P, 2, W])
        KT = sb("KT", [P, 2, 2, GB, NS * P])
        V = sb("V", [P, 2, GB, NS, 2, DH + 1])
        prob = sb("prob", [P, 2, W])
        probT = sb("probT", [P, 2, W])
        mx = sb("mx", [P, 2, BQ])
        rs = sb("rs", [P, 2, BQ])
        on = sb("on", [P, 2, GB, P])
        onT = sb("onT", [P, 2, W])
        if masked:
            mask_row = sb("mask_row", [P, UN, W], BF16)
        nx = Norm(nc, ctx, S, name)
        if NS == 1:
            ctxT = sb("ctxT", [P, 2, W])
            norms = [nx]
            sources = [ctxT]
        else:
            ctx_tok = sb("ctx_tok", [P, 2, GB, D])
            nctx = Norm(nc, ctx, S, name, "_ctx")
            norms = [nctx, nx]
            sources = [nctx.out, nx.out]

        proj_ready = S.new("a_proj_ready", per=M * UP)
        proj_used = S.new("a_proj_used", per=UG, credit=2, extra=NS)
        scores_ready = S.new("a_scores_ready", per=NQ)
        max_done = S.new("a_max_done", per=NQ)
        shifted = S.new("a_shifted", per=NQ, credit=2)
        exp_done = S.new("a_exp_done", per=NQ)
        turned = S.new("a_turned", per=TG, credit=TG)
        turned_used = S.new("a_turned_used", per=TG, credit=2)
        pv_ready = S.new("a_pv_ready", per=NQ)
        recip_done = S.new("a_recip_done", per=NQ)
        head_out = S.new("a_head_out", per=NQ, credit=1)
        out_ready = S.new("a_out_ready")
        x_updated = S.new("a_x_updated", credit=1)
        ones_set = S.new("a_ones_set", groups=1)
        mask_ready = S.new("a_mask_ready", groups=NG + 1)
        load = [S.new(f"a_ctx_load{p}", per=16, groups=NG // UN + (NS == 2 and p == 0)) for p in range(UN)]

        def x_tile(t, j):
            return c.x[:, t * GB + j, :]

        with nc.Block() as block:
            @block.sync
            def _(sp):
                def load_group(t, p):
                    if NS == 1:
                        sp.dma_start(ctxT[:, p, :], c.ctxT_dram[:, bass.ds(t * W, W)]).then_inc(load[p].sem, 16)
                    else:
                        sp.dma_start(ctx_tok[:, p, :, :].rearrange("p b d -> p (b d)"),
                                     c.ctx_tok_dram[:, bass.ds(t * W, W)]).then_inc(load[p].sem, 16)

                for p in range(UN):
                    load_group(p, p)
                if loads:
                    loads.start(sp)
                with sp.Fori(0, NG // UN - 1) as i:
                    for u in range(UN):
                        if NS == 1:
                            sp.wait_ge(out_ready.sem, out_ready.at(i * UN + u))
                        else:
                            sp.wait_ge(nctx.normed.sem, nctx.normed.at(i * UN + u))
                        load_group((i + 1) * UN + u, u)
                if NS == 2:
                    sp.wait_ge(nctx.normed.sem, nctx.normed.at(NG - 2))
                    load_group(0, 0)
                    sp.wait_ge(load[0].sem, load[0].at(NG // UN, 16))
                if loads:
                    loads.finish(sp)

            @block.gpsimd
            def _(pool):
                for n in norms:
                    n.rstd_pool(nc, pool, 0, c.minus_half)
                if masked:
                    nc.gpsimd.tensor_copy(mask_row[:, 0, :], c.mask[:, 0:W]).then_inc(mask_ready.sem, 1)
                with pool.Fori(0, NG // UN) as i:
                    for u in range(UN):
                        t = i * UN + u
                        for n in norms:
                            n.rstd_pool(nc, pool, t + 1, c.minus_half)
                        if masked:
                            nc.gpsimd.tensor_copy(mask_row[:, 1 - u, :], c.mask[:, bass.ds((t + 1) * W, W)])\
                                .then_inc(mask_ready.sem, 1)

            @block.tensor
            def _(pe):
                def project(t, u, m):
                    k = proj_use(m, 0)
                    pe.wait_ge(proj_used.sem, proj_used.at(t, NS + k - 1))
                    nc.tensor.matmul(pj[proj_bank(u, k)][:, :], wq[:, m, :], nx.out[:, u, :],
                                     start=True, stop=True).then_inc(proj_ready.sem, 1)
                    for s in range(NS):
                        k += 1
                        pe.wait_ge(proj_used.sem, proj_used.at(t, NS + k - 1))
                        nc.tensor.matmul(pj[proj_bank(u, k)][:, :], wk[:, m, :], sources[s][:, u, :],
                                         start=True, stop=True).then_inc(proj_ready.sem, 1)
                    for s in range(NS):
                        k += 1
                        pe.wait_ge(proj_used.sem, proj_used.at(t, NS + k - 1))
                        for b in range(GB):
                            ins = nc.tensor.matmul(pj[proj_bank(u, k)][:, b * P:(b + 1) * P],
                                                   sources[s][:, u, b * P:(b + 1) * P], wv[:, m, :],
                                                   start=True, stop=True)
                        ins.then_inc(proj_ready.sem, 1)

                def scores(t, u, q):
                    m, h = q // QM, q % QM // NS
                    b0 = q % NS * BQ
                    if q % QM == 0:
                        pe.wait_ge(proj_used.sem, proj_used.at(t, NS + proj_use(m, UP)))
                    pe.wait_ge(shifted.sem, shifted.at(t, q - 1))
                    bank = sc[q % 2]
                    if masked:
                        nc.tensor.matmul(bank[:, :], c.pick[:, 0, :], mask_row[:, u, :],
                                         start=True, stop=False, skip_group_check=True)
                    for b in range(BQ):
                        ins = nc.tensor.matmul(bank[:, b * KL:(b + 1) * KL],
                                               QT[:, m % 2, (b0 + b) * P:(b0 + b + 1) * P],
                                               KT[:, m % 2, h, b0 + b, :],
                                               start=not masked, stop=True, skip_group_check=masked)
                    ins.then_inc(scores_ready.sem, 1)

                def turn_probs(t, u, q):
                    k = probs_use(q)
                    pe.wait_ge(exp_done.sem, exp_done.at(t, q + 1))
                    pe.wait_ge(turned_used.sem, turned_used.at(t, k - 1))
                    for b in range(GB):
                        ins = nc.tensor.transpose(pt[(u * TG + k) % 2][:, b * P:(b + 1) * P],
                                                  prob[:, q % 2, b * P:(b + 1) * P], c.ident[:, :])
                    ins.then_inc(turned.sem, 1)

                def pv(t, q):
                    m, h = q // QM, q % QM // NS
                    b0 = q % NS * BQ
                    pe.wait_ge(turned_used.sem, turned_used.at(t, probs_use(q) + 1))
                    pe.wait_ge(head_out.sem, head_out.at(t, q))
                    for b in range(BQ):
                        for s in range(NS):
                            col = (b * NS + s) * P
                            ins = nc.tensor.matmul(po[:, b * (DH + 1):(b + 1) * (DH + 1)],
                                                   probT[:, q % 2, col:col + P], V[:, m % 2, b0 + b, s, h, :],
                                                   start=s == 0, stop=s == NS - 1)
                    ins.then_inc(pv_ready.sem, 1)

                def turn_out(t, u, m):
                    k = out_use(m)
                    pe.wait_ge(head_out.sem, head_out.at(t, QM * (m + 1)))
                    pe.wait_ge(turned_used.sem, turned_used.at(t, k - 1))
                    for b in range(GB):
                        ins = nc.tensor.transpose(pt[(u * TG + k) % 2][:, b * P:(b + 1) * P],
                                                  on[:, m % 2, b, :], c.ident[:, :])
                    ins.then_inc(turned.sem, 1)

                def project_out(t, m):
                    if m == 0:
                        pe.wait_ge(x_updated.sem, x_updated.at(t, 0))
                        nc.tensor.matmul(acc[:, :], ones_like(c, bias_row), bias_row, start=True, stop=False,
                                         skip_group_check=True)
                    pe.wait_ge(turned_used.sem, turned_used.at(t, out_use(m) + 1))
                    for b in range(GB):
                        ins = nc.tensor.matmul(acc[:, b * P:(b + 1) * P], onT[:, m % 2, b * P:(b + 1) * P],
                                               wo[:, m, :], start=False, stop=m == M - 1, skip_group_check=True)
                    if m == M - 1:
                        ins.then_inc(out_ready.sem, 1)

                pe.sem_inc(turned.sem, turned.credit)
                for s, n in enumerate(norms):
                    pe.wait_ge(proj_used.sem, proj_used.at(0, s - 1))
                    n.turn_pe(nc, pe, 0, pj[s % 2], c.ident[:, :])
                pe.wait_ge(ones_set.sem, ones_set.at(0))
                with pe.Fori(0, NG // UN) as i:
                    for u in range(UN):
                        t = i * UN + u
                        if NS == 1:
                            pe.wait_ge(load[u].sem, load[u].at(i, 16))
                        if masked:
                            pe.wait_ge(mask_ready.sem, mask_ready.at(t))
                        pe.wait_ge(proj_used.sem, proj_used.at(t, NS))
                        project(t, u, 0)
                        scores(t, u, 0)
                        for q in range(NQ):
                            if q + 1 < NQ:
                                if (q + 1) % QM == 0:
                                    project(t, u, (q + 1) // QM)
                                scores(t, u, q + 1)
                            turn_probs(t, u, q)
                            if q >= 1:
                                pv(t, q - 1)
                            for m in range(M):
                                if turn_step(m) == q:
                                    turn_out(t, u, m)
                                if turn_step(m) + 1 == q:
                                    project_out(t, m)
                            if q == LNQ:
                                for s, n in enumerate(norms):
                                    k = LN_USE + s
                                    pe.wait_ge(proj_used.sem, proj_used.at(t, NS + k - 1))
                                    n.turn_pe(nc, pe, t + 1, pj[proj_bank(u, k)], c.ident[:, :])
                        pv(t, NQ - 1)
                        if turn_step(M - 2) + 1 >= NQ:
                            project_out(t, M - 2)
                        turn_out(t, u, M - 1)
                        project_out(t, M - 1)

            @block.scalar
            def _(act):
                def copy_projections(t, u, m):
                    k = proj_use(m, 0)
                    act.wait_ge(proj_ready.sem, proj_ready.at(t, m * UP + 1))
                    nc.scalar.copy(QT[:, m % 2, :], pj[proj_bank(u, k)][:, :]).then_inc(proj_used.sem, 1)
                    for s in range(NS):
                        k += 1
                        act.wait_ge(proj_ready.sem, proj_ready.at(t, m * UP + 2 + s))
                        for h in range(2):
                            rows = slice(h * DH, (h + 1) * DH)
                            ins = nc.scalar.copy(KT[rows, m % 2, h, :, s * P:(s + 1) * P],
                                                 pj[proj_bank(u, k)][rows, :].rearrange("p (b k) -> p b k", b=GB))
                        ins.then_inc(proj_used.sem, 1)
                    for s in range(NS):
                        k += 1
                        act.wait_ge(proj_ready.sem, proj_ready.at(t, m * UP + 2 + NS + s))
                        nc.scalar.copy(V[:, m % 2, :, s, :, 0:DH],
                                       pj[proj_bank(u, k)][:, :].rearrange("p (b h d) -> p b h d", b=GB, h=2))\
                            .then_inc(proj_used.sem, 1)

                def copy_norm(t, u, s, n, bank):
                    act.wait_ge(n.turned.sem, n.turned.at(t))
                    if affine is None:
                        nc.scalar.copy(n.out[:, u, :], bank[:, :]).then_inc(proj_used.sem, 1)
                    else:
                        nc.scalar.activation(n.out[:, u, :], bank[:, :], ACT.Identity, bias=affine[s][1],
                                             scale=affine[s][0]).then_inc(proj_used.sem, 1)

                def copy_turned(t, u, k, dst):
                    act.wait_ge(turned.sem, turned.at(t, k + 1))
                    nc.scalar.copy(dst, pt[(u * TG + k) % 2][:, :]).then_inc(turned_used.sem, 1)

                act.sem_inc(proj_used.sem, proj_used.credit)
                act.sem_inc(turned_used.sem, turned_used.credit)
                for s, n in enumerate(norms):
                    copy_norm(0, 0, s, n, pj[s % 2])
                with act.Fori(0, NG // UN) as i:
                    for u in range(UN):
                        t = i * UN + u
                        copy_projections(t, u, 0)
                        for q in range(NQ):
                            act.wait_ge(shifted.sem, shifted.at(t, q + 1))
                            nc.scalar.activation(prob[:, q % 2, :], prob[:, q % 2, :], ACT.Exp, scale=SCALE)\
                                .then_inc(exp_done.sem, 1)
                            if q + 1 < NQ and (q + 1) % QM == 0:
                                copy_projections(t, u, (q + 1) // QM)
                            copy_turned(t, u, probs_use(q), probT[:, q % 2, :])
                            for m in range(M):
                                if turn_step(m) == q:
                                    copy_turned(t, u, out_use(m), onT[:, m % 2, :])
                            if q == LNQ:
                                for s, n in enumerate(norms):
                                    copy_norm(t + 1, 1 - u, s, n, pj[proj_bank(u, LN_USE + s)])
                        copy_turned(t, u, out_use(M - 1), onT[:, (M - 1) % 2, :])

            @block.vector
            def _(dve):
                def shift(t, q):
                    dve.wait_ge(scores_ready.sem, scores_ready.at(t, q + 1))
                    view = sc[q % 2][:, :].rearrange("p (b k) -> p b k", b=BQ)
                    nc.vector.tensor_reduce(mx[:, q % 2, :], view, AX.X, ALU.max).then_inc(max_done.sem, 1)
                    dve.wait_ge(max_done.sem, max_done.at(t, q + 1))
                    dve.wait_ge(turned.sem, turned.at(t, probs_use(q - 2) + 1 if q >= 2 else
                                                      probs_use(NQ + q - 2) + 1 - TG))
                    nc.vector.tensor_tensor(prob[:, q % 2, :].rearrange("p (b k) -> p b k", b=BQ), view,
                                            mx[:, q % 2, :].unsqueeze(2).to_broadcast([P, BQ, KL]), ALU.subtract)\
                        .then_inc(shifted.sem, 1)

                def normalise(t, q):
                    m, h = q // QM, q % QM // NS
                    b0 = q % NS * BQ
                    dve.wait_ge(pv_ready.sem, pv_ready.at(t, q + 1))
                    out = po[:, 0:BQ * (DH + 1)].rearrange("p (b e) -> p b e", b=BQ)
                    nc.vector.reciprocal(rs[:, q % 2, :], out[:, :, DH]).then_inc(recip_done.sem, 1)
                    dve.wait_ge(recip_done.sem, recip_done.at(t, q + 1))
                    nc.vector.tensor_tensor(on[:, m % 2, b0:b0 + BQ, h * DH:(h + 1) * DH], out[:, :, 0:DH],
                                            rs[:, q % 2, :].unsqueeze(2).to_broadcast([P, BQ, DH]), ALU.mult)\
                        .then_inc(head_out.sem, 1)

                def ctx_tile(u):
                    return lambda t, j: ctx_tok[:, u, j, :]

                nc.vector.memset(KT[0:DH, :, 1, :, :], 0.0)
                nc.vector.memset(KT[DH:P, :, 0, :, :], 0.0)
                nc.vector.memset(V[:, :, :, :, :, DH:DH + 1], 1.0).then_inc(ones_set.sem, 1)
                dve.sem_inc(shifted.sem, shifted.credit)
                dve.sem_inc(head_out.sem, head_out.credit)
                dve.sem_inc(x_updated.sem, x_updated.credit)
                if NS == 2:
                    dve.wait_ge(load[0].sem, load[0].at(0, 16))
                    nctx.stats_dve(nc, dve, 0, ctx_tile(0))
                    nctx.apply_dve(nc, dve, 0, ctx_tile(0), first=True)
                nx.stats_dve(nc, dve, 0, x_tile)
                nx.apply_dve(nc, dve, 0, x_tile, first=True)
                with dve.Fori(0, NG // UN) as i:
                    for u in range(UN):
                        t = i * UN + u
                        shift(t, 0)
                        for q in range(NQ):
                            if q + 1 < NQ:
                                shift(t, q + 1)
                            if q >= 1:
                                normalise(t, q - 1)
                            if NS == 2 and q == LNQ // 2 - 3:
                                dve.wait_ge(load[1 - u].sem, load[1 - u].at(i + u, 16))
                                nctx.stats_dve(nc, dve, t + 1, ctx_tile(1 - u))
                            if NS == 2 and q == LNQ // 2 - 1:
                                nctx.apply_dve(nc, dve, t + 1, ctx_tile(1 - u))
                            if q == LNQ // 2 - 1:
                                nx.stats_dve(nc, dve, t + 1, x_tile)
                            if q == LNQ // 2 + 1:
                                nx.apply_dve(nc, dve, t + 1, x_tile)
                        normalise(t, NQ - 1)
                        dve.wait_ge(out_ready.sem, out_ready.at(t))
                        xg = c.x[:, bass.ds(t * GB, GB), :].rearrange("p b d -> p (b d)")
                        nc.vector.scalar_tensor_tensor(xg, acc[:, :], gate, xg, ALU.mult, ALU.add)\
                            .then_inc(x_updated.sem, 1)



def ternary_ffn(nc, c, S, name, gated, weights, gate, hidden_bias=None, out_bias=None, loads=None):
    F = 512
    FB = F // P
    NW = len(weights)
    with ExitStack() as ctx:
        def sb(n, shape, dt=F32):
            return ctx.enter_context(nc.sbuf_tensor(f"{name}_{n}", shape, dt))

        def ps(n, dt=F32):
            return ctx.enter_context(nc.psum_tensor(f"{name}_{n}", [P, W], dt))

        up_bank = [[ps(f"up{k}{i}") for i in range(2)] for k in range(NW - 1)]
        xt_bank = ps("xt", BF16)
        ht_bank = ps("ht", BF16)
        y_bank = ps("y")
        sum_bank = ps("sum")
        wt = sb("wt", [P, NW, F])
        wb = sb("wb", [P, NW, F], BF16)
        wsum = sb("wsum", [P, NW])
        wmean = sb("wmean", [P, NW])
        wtmp = sb("wtmp", [P, NW])
        winv = sb("winv", [P, NW])
        xam = sb("xam", [P, GB])
        xa = sb("xa", [P, GB])
        xs = sb("xs", [P, GB])
        xdq = sb("xdq", [P, UN, NW - 1, GB])
        xr = sb("xr", [P, GB, D])
        xq = sb("xq", [P, GB, D], BF16)
        xqT = sb("xqT", [P, UN, W], BF16)
        pre = sb("pre", [P, 2, F])
        h = sb("h", [P, 2, F])
        ham = sb("ham", [P, 2])
        ha = sb("ha", [P, 2])
        hs = sb("hs", [P, 2])
        hdq = sb("hdq", [P, GB])
        hr = sb("hr", [P, 2, F])
        hq = sb("hq", [P, 2, F], BF16)
        hqT = sb("hqT", [P, 2, F], BF16)
        wtg = sb("wtg", [P, 1])
        y = sb("y_sb", [P, GB, D])
        nx = Norm(nc, ctx, S, name, turns=False)

        w_step = S.new("b_weight_step", per=NW + 6, groups=1)
        w_total = S.new("b_weight_total", groups=1)
        x_step = S.new("b_x_step", per=5, groups=NG + 1)
        xq_ready = S.new("b_xq_ready", groups=NG + 1)
        x_turned = S.new("b_x_turned", groups=NG + 1)
        xT_ready = S.new("b_xT_ready", groups=NG + 1)
        up_ready = S.new("b_up_ready", per=GB)
        act_done = S.new("b_act_done", per=GB)
        a1_done = S.new("b_a1_done", per=GB, credit=2)
        am_done = S.new("b_am_done", per=GB)
        ha_done = S.new("b_ha_done", per=GB)
        hs_done = S.new("b_hs_done", per=GB)
        rounded = S.new("b_rounded", per=GB)
        hq_ready = S.new("b_hq_ready", per=GB)
        h_turned = S.new("b_h_turned", per=GB)
        hT_ready = S.new("b_hT_ready", per=GB, credit=1)
        y_ready = S.new("b_y_ready")
        y_done = S.new("b_y_done", per=0 if out_bias is None else 1)
        x_updated = S.new("b_x_updated", credit=1)
        hdq_done = S.new("b_hdq_done")

        def x_tile(t, j):
            return c.x[:, t * GB + j, :]

        with nc.Block() as block:
            if loads:
                @block.sync
                def _(sp):
                    loads.start(sp)
                    loads.finish(sp)

            @block.gpsimd
            def _(pool):
                nx.rstd_pool(nc, pool, 0, c.minus_half)
                with pool.Fori(0, NG // UN) as i:
                    for u in range(UN):
                        nx.rstd_pool(nc, pool, i * UN + u + 1, c.minus_half)

            @block.tensor
            def _(pe):
                def turn_x(t):
                    pe.wait_ge(xq_ready.sem, xq_ready.at(t))
                    for b in range(GB):
                        ins = nc.tensor.transpose(xt_bank[:, b * P:(b + 1) * P], xq[:, b, :], c.ident_bf[:, :])
                    ins.then_inc(x_turned.sem, 1)

                def up(t, u, b):
                    if b == 0:
                        pe.wait_ge(xT_ready.sem, xT_ready.at(t))
                    pe.wait_ge(a1_done.sem, a1_done.at(t, b - 1))
                    for k in range(NW - 1):
                        ins = nc.tensor.matmul(up_bank[k][b % 2][:, :], xqT[:, u, b * P:(b + 1) * P], wb[:, k, :],
                                               start=True, stop=True)
                    ins.then_inc(up_ready.sem, 1)

                def turn_h(t, b):
                    pe.wait_ge(hq_ready.sem, hq_ready.at(t, b + 1))
                    pe.wait_ge(hT_ready.sem, hT_ready.at(t, b))
                    for f in range(FB):
                        ins = nc.tensor.transpose(ht_bank[:, f * P:(f + 1) * P], hq[:, b % 2, f * P:(f + 1) * P],
                                                  c.ident_bf[:, :])
                    ins.then_inc(h_turned.sem, 1)

                def down(t, b):
                    if b == 0:
                        pe.wait_ge(x_updated.sem, x_updated.at(t, 0))
                    pe.wait_ge(hT_ready.sem, hT_ready.at(t, b + 1))
                    for f in range(FB):
                        ins = nc.tensor.matmul(y_bank[:, b * P:(b + 1) * P], hqT[:, b % 2, f * P:(f + 1) * P],
                                               wb[:, NW - 1, f * P:(f + 1) * P], start=f == 0, stop=f == FB - 1)
                    if b == GB - 1:
                        ins.then_inc(y_ready.sem, 1)

                pe.wait_ge(w_step.sem, w_step.at(0, NW))
                nc.tensor.matmul(sum_bank[:, 0:NW], c.ones[:, :], wsum[:, :], start=True, stop=True)\
                    .then_inc(w_total.sem, 1)
                turn_x(0)
                pe.wait_ge(w_step.sem, w_step.at(0, NW + 6))
                with pe.Fori(0, NG // UN) as i:
                    for u in range(UN):
                        t = i * UN + u
                        up(t, u, 0)
                        for b in range(GB):
                            if b + 1 < GB:
                                up(t, u, b + 1)
                            if b == 2:
                                turn_x(t + 1)
                            turn_h(t, b)
                            down(t, b)

            @block.scalar
            def _(act):
                def copy_x(t, u):
                    act.wait_ge(x_turned.sem, x_turned.at(t))
                    nc.scalar.copy(xqT[:, u, :], xt_bank[:, :]).then_inc(xT_ready.sem, 1)

                def activate(t, u, b):
                    if gated:
                        act.wait_ge(up_ready.sem, up_ready.at(t, b + 1))
                        nc.scalar.activation(pre[:, b % 2, :], up_bank[0][b % 2][:, :], ACT.Silu,
                                             scale=xdq[:, u, 0, b:b + 1]).then_inc(act_done.sem, 1)
                    else:
                        act.wait_ge(a1_done.sem, a1_done.at(t, b + 1))
                        nc.scalar.activation(h[:, b % 2, :], pre[:, b % 2, :], ACT.Gelu).then_inc(act_done.sem, 1)

                def round_up(t, b):
                    act.wait_ge(hs_done.sem, hs_done.at(t, b + 1))
                    nc.scalar.activation(hr[:, b % 2, :], h[:, b % 2, :], ACT.Identity, bias=c.magic[:, :],
                                         scale=hs[:, b % 2:b % 2 + 1]).then_inc(rounded.sem, 1)

                act.sem_inc(hT_ready.sem, hT_ready.credit)
                copy_x(0, 0)
                with act.Fori(0, NG // UN) as i:
                    for u in range(UN):
                        t = i * UN + u
                        activate(t, u, 0)
                        for b in range(GB):
                            if b + 1 < GB:
                                activate(t, u, b + 1)
                            round_up(t, b)
                            if b == 2:
                                copy_x(t + 1, 1 - u)
                            act.wait_ge(h_turned.sem, h_turned.at(t, b + 1))
                            nc.scalar.copy(hqT[:, b % 2, :], ht_bank[:, :]).then_inc(hT_ready.sem, 1)

            @block.vector
            def _(dve):
                def quantise_x(t, u):
                    dve.wait_ge(nx.normed.sem, nx.normed.at(t))
                    nc.vector.tensor_reduce(xam[:, :], nx.xn[:, :, :], AX.X, ALU.max, apply_absolute_value=True)\
                        .then_inc(x_step.sem, 1)
                    dve.wait_ge(x_step.sem, x_step.at(t, 1))
                    nc.vector.tensor_scalar(xa[:, :], xam[:, :], 1e-5, 1.0 / 127.0, ALU.max, ALU.mult)\
                        .then_inc(x_step.sem, 1)
                    dve.wait_ge(x_step.sem, x_step.at(t, 2))
                    nc.vector.reciprocal(xs[:, :], xa[:, :]).then_inc(x_step.sem, 1)
                    for k in range(NW - 1):
                        ins = nc.vector.tensor_scalar(xdq[:, u, k, :], xa[:, :], wmean[:, k:k + 1], None, ALU.mult)
                    ins.then_inc(x_step.sem, 1)
                    dve.wait_ge(x_step.sem, x_step.at(t, 4))
                    for b in range(GB):
                        ins = nc.vector.tensor_scalar(xr[:, b, :], nx.xn[:, b, :], xs[:, b:b + 1], MAGIC,
                                                      ALU.mult, ALU.add)
                    ins.then_inc(x_step.sem, 1)
                    dve.wait_ge(x_step.sem, x_step.at(t, 5))
                    if not isinstance(t, int):
                        dve.wait_ge(xT_ready.sem, xT_ready.at(t, 0))
                    nc.vector.tensor_scalar(xq[:, :, :], xr[:, :, :], MAGIC, 127.0, ALU.subtract, ALU.min)\
                        .then_inc(xq_ready.sem, 1)

                def hidden(t, u, b):
                    k = b % 2
                    if gated:
                        dve.wait_ge(act_done.sem, act_done.at(t, b + 1))
                        nc.vector.scalar_tensor_tensor(h[:, k, :], up_bank[1][k][:, :], xdq[:, u, 1, b:b + 1],
                                                       pre[:, k, :], ALU.mult, ALU.mult).then_inc(a1_done.sem, 1)
                    else:
                        dve.wait_ge(up_ready.sem, up_ready.at(t, b + 1))
                        nc.vector.scalar_tensor_tensor(pre[:, k, :], up_bank[0][k][:, :], xdq[:, u, 0, b:b + 1],
                                                       hidden_bias, ALU.mult, ALU.add).then_inc(a1_done.sem, 1)

                def scale_h(t, b):
                    k = b % 2
                    if gated:
                        dve.wait_ge(a1_done.sem, a1_done.at(t, b + 1))
                    else:
                        dve.wait_ge(act_done.sem, act_done.at(t, b + 1))
                    nc.vector.tensor_reduce(ham[:, k:k + 1], h[:, k, :], AX.X, ALU.max, apply_absolute_value=True)\
                        .then_inc(am_done.sem, 1)
                    dve.wait_ge(am_done.sem, am_done.at(t, b + 1))
                    nc.vector.tensor_scalar(ha[:, k:k + 1], ham[:, k:k + 1], 1e-5, 1.0 / 127.0, ALU.max, ALU.mult)\
                        .then_inc(ha_done.sem, 1)
                    dve.wait_ge(ha_done.sem, ha_done.at(t, b + 1))
                    nc.vector.reciprocal(hs[:, k:k + 1], ha[:, k:k + 1]).then_inc(hs_done.sem, 1)
                    ins = nc.vector.tensor_scalar(hdq[:, b:b + 1], ha[:, k:k + 1], wtg[:, :], None, ALU.mult)
                    if b == GB - 1:
                        ins.then_inc(hdq_done.sem, 1)

                def quantise_h(t, b):
                    dve.wait_ge(rounded.sem, rounded.at(t, b + 1))
                    nc.vector.tensor_scalar(hq[:, b % 2, :], hr[:, b % 2, :], MAGIC, 127.0, ALU.subtract, ALU.min)\
                        .then_inc(hq_ready.sem, 1)

                dve.sem_inc(a1_done.sem, a1_done.credit)
                dve.sem_inc(x_updated.sem, x_updated.credit)
                for k, w in enumerate(weights):
                    nc.vector.tensor_reduce(wsum[:, k:k + 1], w, AX.X, ALU.add, apply_absolute_value=True)\
                        .then_inc(w_step.sem, 1)
                nx.stats_dve(nc, dve, 0, x_tile)
                dve.wait_ge(w_total.sem, w_total.at(0))
                nc.vector.tensor_scalar(wmean[:, :], sum_bank[:, 0:NW], 1.0 / (P * F), 1e-5, ALU.mult, ALU.max)\
                    .then_inc(w_step.sem, 1)
                dve.wait_ge(w_step.sem, w_step.at(0, NW + 1))
                nc.vector.reciprocal(winv[:, :], wmean[:, :]).then_inc(w_step.sem, 1)
                nc.vector.tensor_tensor(wtg[:, :], wmean[:, NW - 1:NW], gate, ALU.mult).then_inc(w_step.sem, 1)
                dve.wait_ge(w_step.sem, w_step.at(0, NW + 3))
                for k, w in enumerate(weights):
                    ins = nc.vector.tensor_scalar(wt[:, k, :], w, winv[:, k:k + 1], MAGIC, ALU.mult, ALU.add)
                ins.then_inc(w_step.sem, 1)
                dve.wait_ge(w_step.sem, w_step.at(0, NW + 4))
                nc.vector.tensor_scalar(wt[:, :, :], wt[:, :, :], MAGIC, 1.0, ALU.subtract, ALU.min)\
                    .then_inc(w_step.sem, 1)
                dve.wait_ge(w_step.sem, w_step.at(0, NW + 5))
                nc.vector.tensor_scalar(wb[:, :, :], wt[:, :, :], -1.0, None, ALU.max).then_inc(w_step.sem, 1)
                nx.apply_dve(nc, dve, 0, x_tile, first=True)
                quantise_x(0, 0)
                with dve.Fori(0, NG // UN) as i:
                    for u in range(UN):
                        t = i * UN + u
                        hidden(t, u, 0)
                        for b in range(GB):
                            if not gated and b + 1 < GB:
                                hidden(t, u, b + 1)
                            scale_h(t, b)
                            if gated and b + 1 < GB:
                                hidden(t, u, b + 1)
                            if b == 0:
                                nx.stats_dve(nc, dve, t + 1, x_tile)
                            if b == 1:
                                nx.apply_dve(nc, dve, t + 1, x_tile, first=True)
                                quantise_x(t + 1, 1 - u)
                            quantise_h(t, b)
                        dve.wait_ge(y_ready.sem, y_ready.at(t))
                        dve.wait_ge(hdq_done.sem, hdq_done.at(t))
                        for b in range(GB):
                            xb = c.x[:, t * GB + b, :]
                            if out_bias is None:
                                ins = nc.vector.scalar_tensor_tensor(xb, y_bank[:, b * P:(b + 1) * P],
                                                                     hdq[:, b:b + 1], xb, ALU.mult, ALU.add)
                            else:
                                ins = nc.vector.scalar_tensor_tensor(y[:, b, :], y_bank[:, b * P:(b + 1) * P],
                                                                     hdq[:, b:b + 1], out_bias, ALU.mult, ALU.add)
                        if out_bias is not None:
                            ins.then_inc(y_done.sem, 1)
                            dve.wait_ge(y_done.sem, y_done.at(t))
                            xg = c.x[:, bass.ds(t * GB, GB), :]
                            ins = nc.vector.tensor_tensor(xg, y[:, :, :], xg, ALU.add)
                        ins.then_inc(x_updated.sem, 1)



def attention8(nc, c, S, name, wq, wk, wv, wo, bq, bk, bv_row, bo_row, gate, rel_bias=None, rel_flipped=None,
               mask=None, valid=None):
    DK = D // HEADS
    NR = 4
    NQ = HEADS
    HQ = 8
    TG = NQ + 1
    UG = 3
    SCALE = float(DK) ** -0.5
    TINY = 1e-30
    LNQ, PRQ = 5, 8

    with ExitStack() as ctx:
        def sb(n, shape, dt=F32):
            return ctx.enter_context(nc.sbuf_tensor(f"{name}_{n}", shape, dt))

        def ps(n):
            return ctx.enter_context(nc.psum_tensor(f"{name}_{n}", [P, W], F32))

        pj = [ps(f"proj{i}") for i in range(2)]
        sc = [ps(f"scores{i}") for i in range(2)]
        pt = [ps(f"turned{i}") for i in range(2)]
        po = ps("pv")
        va = ps("va")
        QT = sb("QT", [P, UN, NR, W])
        KT = sb("KT", [P, W])
        Kx = sb("Kx", [P, UN, NR, W])
        V = sb("V", [P, UN, GB, HEADS, DK + 1])
        bqs = sb("bqs", [P, 1])
        prob = sb("prob", [P, 2, W])
        probT = sb("probT", [P, 2, W])
        mx = sb("mx", [P, 2, GB])
        den = sb("den", [P, NQ // HQ, GB, HQ])
        rs = sb("rs", [P, NQ // HQ, GB, HQ])
        on = sb("on", [P, UN, GB, D])
        onT = sb("onT", [P, UN, W])
        ctxT = sb("ctxT", [P, UN, W])
        if mask is not None:
            mask_row = sb("mask_row", [P, UN, W], BF16)
            vg = sb("vg", [P, UN, GB])
        nx = Norm(nc, ctx, S, name)

        zeros_set = S.new("c_zeros_set", groups=1)
        q_scaled = S.new("c_bq_scaled", groups=1)
        proj_ready = S.new("c_proj_ready", per=2, extra=2)
        proj_used = S.new("c_proj_used", per=UG, credit=2, extra=UG)
        kx_ready = S.new("c_kx_ready", groups=NG + 1)
        v_ready = S.new("c_v_ready", groups=NG + 1)
        vg_ready = S.new("c_vg_ready", groups=NG + 1)
        va_used = S.new("c_va_used", per=2, extra=1, credit=1)
        scores_ready = S.new("c_scores_ready", per=NQ)
        biased = S.new("c_biased", per=NQ if rel_bias is not None else 0)
        max_done = S.new("c_max_done", per=NQ)
        shifted = S.new("c_shifted", per=NQ, credit=2)
        exp_done = S.new("c_exp_done", per=NQ)
        turned = S.new("c_turned", per=TG, credit=TG)
        turned_used = S.new("c_turned_used", per=TG, credit=2)
        pv_ready = S.new("c_pv_ready", per=NQ // HQ)
        den_done = S.new("c_den_done", per=NQ // HQ)
        recip_done = S.new("c_recip_done", per=NQ // HQ)
        head_out = S.new("c_head_out", per=NQ // HQ, credit=1)
        out_ready = S.new("c_out_ready")
        flip_ready = S.new("c_flip_ready", per=HEADS * P // W, groups=1)
        flip_used = S.new("c_flip_used", per=HEADS * P // W, groups=1)
        mask_ready = S.new("c_mask_ready", groups=NG + 1)
        load = [S.new(f"c_ctx_load{p}", per=16, groups=NG // UN + (p == 0)) for p in range(UN)]

        def x_tile(t, j):
            return c.x[:, t * GB + j, :]

        def group(t):
            return slice(t * GB, (t + 1) * GB) if isinstance(t, int) else bass.ds(t * GB, GB)

        with nc.Block() as block:
            @block.sync
            def _(sp):
                def load_group(t, p):
                    sp.dma_start(ctxT[:, p, :], c.ctxT_dram[:, bass.ds(t * W, W)]).then_inc(load[p].sem, 16)

                for p in range(UN):
                    load_group(p, p)
                with sp.Fori(0, NG // UN - 1) as i:
                    for u in range(UN):
                        sp.wait_ge(v_ready.sem, v_ready.at(i * UN + u))
                        load_group((i + 1) * UN + u, u)
                sp.wait_ge(v_ready.sem, v_ready.at(NG - 2))
                load_group(0, 0)
                sp.wait_ge(load[0].sem, load[0].at(NG // UN, 16))

            @block.gpsimd
            def _(pool):
                nc.gpsimd.memset(QT[:, :, :, :], 0.0).then_inc(zeros_set.sem, 1)
                nx.rstd_pool(nc, pool, 0, c.minus_half)
                if mask is not None:
                    nc.gpsimd.tensor_copy(mask_row[:, 0, :], mask[:, 0:W]).then_inc(mask_ready.sem, 1)
                with pool.Fori(0, NG // UN) as i:
                    for u in range(UN):
                        t = i * UN + u
                        nx.rstd_pool(nc, pool, t + 1, c.minus_half)
                        if mask is not None:
                            nc.gpsimd.tensor_copy(mask_row[:, 1 - u, :], mask[:, bass.ds((t + 1) * W, W)])\
                                .then_inc(mask_ready.sem, 1)

            @block.tensor
            def _(pe):
                def turn_norm(t, bank):
                    nx.turn_pe(nc, pe, t, bank, c.ident[:, :])

                def project(t, u, pb, i_load):
                    pe.wait_ge(proj_used.sem, pb[0][1])
                    nc.tensor.matmul(pb[0][0][:, :], wq, nx.out[:, u, :], start=True, stop=True)\
                        .then_inc(proj_ready.sem, 1)
                    pe.wait_ge(load[u].sem, load[u].at(i_load, 16))
                    pe.wait_ge(proj_used.sem, pb[1][1])
                    nc.tensor.matmul(pb[1][0][:, :], wk, ctxT[:, u, :], start=True, stop=True)\
                        .then_inc(proj_ready.sem, 1)

                def project_v(t, u, n):
                    pe.wait_ge(va_used.sem, n)
                    nc.tensor.matmul(va[:, :], ones_like(c, bv_row), bv_row, start=True, stop=False, skip_group_check=True)
                    for b in range(GB):
                        ins = nc.tensor.matmul(va[:, b * P:(b + 1) * P], ctxT[:, u, b * P:(b + 1) * P], wv,
                                               start=False, stop=True, skip_group_check=True)
                    ins.then_inc(v_ready.sem, 1)

                def scores(t, u, q):
                    r, j = q // NR, q % NR
                    if q == 0:
                        pe.wait_ge(kx_ready.sem, kx_ready.at(t))
                        if mask is not None:
                            pe.wait_ge(mask_ready.sem, mask_ready.at(t))
                    pe.wait_ge(shifted.sem, shifted.at(t, q - 1))
                    bank = sc[q % 2]
                    if mask is not None:
                        nc.tensor.matmul(bank[:, :], c.pick[:, 1, :], mask_row[:, u, :], start=True, stop=False,
                                         skip_group_check=True)
                    for b in range(GB):
                        ins = nc.tensor.matmul(bank[:, b * P:(b + 1) * P],
                                               QT[:, u, j, b * P:(b + 1) * P], Kx[:, u, r, b * P:(b + 1) * P],
                                               start=mask is None, stop=True, skip_group_check=mask is not None)
                    ins.then_inc(scores_ready.sem, 1)

                def turn_probs(t, u, q):
                    pe.wait_ge(exp_done.sem, exp_done.at(t, q + 1))
                    pe.wait_ge(turned_used.sem, turned_used.at(t, q - 1))
                    for b in range(GB):
                        ins = nc.tensor.transpose(pt[(u * TG + q) % 2][:, b * P:(b + 1) * P],
                                                  prob[:, q % 2, b * P:(b + 1) * P], c.ident[:, :])
                    ins.then_inc(turned.sem, 1)

                def pv(t, u, q):
                    r, j = q // NR, q % NR
                    pe.wait_ge(turned_used.sem, turned_used.at(t, q + 1))
                    if q % HQ == 0:
                        pe.wait_ge(head_out.sem, head_out.at(t, q // HQ))
                    for b in range(GB):
                        col = (b * HQ + q % HQ) * (DK + 1)
                        ins = nc.tensor.matmul(po[:, col:col + DK + 1], probT[:, q % 2, b * P:(b + 1) * P],
                                               V[:, u, b, 4 * j + r, :], start=True, stop=True)
                    if q % HQ == HQ - 1:
                        ins.then_inc(pv_ready.sem, 1)

                pe.sem_inc(turned.sem, turned.credit)
                if rel_bias is not None:
                    for k in range(HEADS * P // W):
                        if k >= 2:
                            pe.wait_ge(flip_used.sem, flip_used.at(0, k - 1))
                        nc.tensor.matmul(sc[k % 2][:, :], c.flip[:, :], rel_flipped[:, k * 4:(k + 1) * 4, :],
                                         start=True, stop=True).then_inc(flip_ready.sem, 1)
                    pe.wait_ge(flip_used.sem, flip_used.at(0, HEADS * P // W))
                pe.wait_ge(proj_used.sem, proj_used.at(0, -1))
                turn_norm(0, pj[0])
                project(0, 0, [(pj[1], proj_used.at(0, 1)), (pj[0], proj_used.at(0, 1))], 0)
                project_v(0, 0, va_used.at(0, 0))
                with pe.Fori(0, NG // UN) as i:
                    for u in range(UN):
                        t = i * UN + u
                        banks = [pj[(UG + u * UG + k) % 2] for k in range(UG)]
                        scores(t, u, 0)
                        for q in range(NQ):
                            if q + 1 < NQ:
                                scores(t, u, q + 1)
                            turn_probs(t, u, q)
                            if q >= 1:
                                pv(t, u, q - 1)
                            if q == LNQ:
                                pe.wait_ge(proj_used.sem, proj_used.at(t, UG - 1))
                                turn_norm(t + 1, banks[0])
                            if q == PRQ:
                                project(t + 1, 1 - u, [(banks[1], proj_used.at(t, UG + 1)),
                                                       (banks[2], proj_used.at(t, UG + 1))], i + u)
                                project_v(t + 1, 1 - u, va_used.at(t, 1))
                        pv(t, u, NQ - 1)
                        pe.wait_ge(head_out.sem, head_out.at(t, NQ // HQ))
                        pe.wait_ge(turned_used.sem, turned_used.at(t, NQ - 1))
                        for b in range(GB):
                            ins = nc.tensor.transpose(pt[(u * TG + NQ) % 2][:, b * P:(b + 1) * P], on[:, u, b, :],
                                                      c.ident[:, :])
                        ins.then_inc(turned.sem, 1)
                        pe.wait_ge(va_used.sem, va_used.at(t, 2))
                        nc.tensor.matmul(va[:, :], ones_like(c, bo_row), bo_row, start=True, stop=False,
                                         skip_group_check=True)
                        pe.wait_ge(turned_used.sem, turned_used.at(t, NQ + 1))
                        for b in range(GB):
                            ins = nc.tensor.matmul(va[:, b * P:(b + 1) * P], onT[:, u, b * P:(b + 1) * P], wo,
                                                   start=False, stop=True, skip_group_check=True)
                        ins.then_inc(out_ready.sem, 1)

            @block.scalar
            def _(act):
                def copy_norm(t, u, bank):
                    act.wait_ge(nx.turned.sem, nx.turned.at(t))
                    nc.scalar.copy(nx.out[:, u, :], bank[:, :]).then_inc(proj_used.sem, 1)

                def copy_qk(n, u, banks, kx_before):
                    act.wait_ge(proj_ready.sem, n)
                    for j in range(NR):
                        quadrant = slice(32 * j, 32 * j + 32)
                        ins = nc.scalar.activation(QT[quadrant, u, j, :], banks[0][quadrant, :], ACT.Identity,
                                                   bias=bqs[quadrant, :], scale=SCALE)
                    ins.then_inc(proj_used.sem, 1)
                    act.wait_ge(proj_ready.sem, n + 1)
                    if kx_before is not None:
                        act.wait_ge(kx_ready.sem, kx_before)
                    nc.scalar.activation(KT[:, :], banks[1][:, :], ACT.Identity, bias=bk)\
                        .then_inc(proj_used.sem, 1)

                def copy_turned(t, u, k, dst):
                    act.wait_ge(turned.sem, turned.at(t, k + 1))
                    nc.scalar.copy(dst, pt[(u * TG + k) % 2][:, :]).then_inc(turned_used.sem, 1)

                act.sem_inc(proj_used.sem, proj_used.credit)
                act.sem_inc(turned_used.sem, turned_used.credit)
                if rel_bias is not None:
                    for k in range(HEADS * P // W):
                        act.wait_ge(flip_ready.sem, flip_ready.at(0, k + 1))
                        nc.scalar.copy(rel_bias[:, k * 4:(k + 1) * 4, :].rearrange("p h k -> p (h k)"),
                                       sc[k % 2][:, :]).then_inc(flip_used.sem, 1)
                copy_norm(0, 0, pj[0])
                act.wait_ge(zeros_set.sem, zeros_set.at(0))
                act.wait_ge(q_scaled.sem, q_scaled.at(0))
                copy_qk(proj_ready.at(0, 1), 0, [pj[1], pj[0]], None)
                with act.Fori(0, NG // UN) as i:
                    for u in range(UN):
                        t = i * UN + u
                        banks = [pj[(UG + u * UG + k) % 2] for k in range(UG)]
                        for q in range(NQ):
                            act.wait_ge(shifted.sem, shifted.at(t, q + 1))
                            nc.scalar.activation(prob[:, q % 2, :], prob[:, q % 2, :], ACT.Exp)\
                                .then_inc(exp_done.sem, 1)
                            copy_turned(t, u, q, probT[:, q % 2, :])
                            if q == LNQ:
                                copy_norm(t + 1, 1 - u, banks[0])
                            if q == PRQ:
                                copy_qk(proj_ready.at(t, 3), 1 - u, banks[1:], kx_ready.at(t))
                        copy_turned(t, u, NQ, onT[:, u, :])

            @block.vector
            def _(dve):
                def keys_and_values(t, u, n):
                    dve.wait_ge(proj_used.sem, n)
                    for r in range(NR):
                        ins = nc.vector.tensor_scalar(Kx[:, u, r, :], KT[:, :], c.headmask[:, r:r + 1], None, ALU.mult)
                    ins.then_inc(kx_ready.sem, 1)
                    view = va[:, :].rearrange("p (b h d) -> p b h d", b=GB, h=HEADS)
                    if valid is None:
                        dve.wait_ge(v_ready.sem, v_ready.at(t))
                        ins = nc.vector.tensor_copy(V[:, u, :, :, 0:DK], view)
                    else:
                        nc.vector.tensor_copy(vg[:, u, :], valid[:, group(t)]).then_inc(vg_ready.sem, 1)
                        dve.wait_ge(vg_ready.sem, vg_ready.at(t))
                        nc.vector.tensor_copy(V[:, u, :, :, DK], vg[:, u, :].unsqueeze(2).to_broadcast([P, GB, HEADS]))
                        dve.wait_ge(v_ready.sem, v_ready.at(t))
                        for b in range(GB):
                            ins = nc.vector.tensor_scalar(V[:, u, b, :, 0:DK], view[:, b, :, :], vg[:, u, b:b + 1],
                                                          None, ALU.mult)
                    ins.then_inc(va_used.sem, 1)

                def shift(t, u, q):
                    h = 4 * (q % NR) + q // NR
                    dve.wait_ge(scores_ready.sem, scores_ready.at(t, q + 1))
                    view = sc[q % 2][:, :].rearrange("p (b k) -> p b k", b=GB)
                    dst = prob[:, q % 2, :].rearrange("p (b k) -> p b k", b=GB)
                    before = turned.at(t, q - 1 if q >= 2 else NQ + q - 1 - TG)
                    if rel_bias is not None:
                        dve.wait_ge(turned.sem, before)
                        nc.vector.tensor_tensor(dst, view, rel_bias[:, h, :].unsqueeze(1).to_broadcast([P, GB, P]),
                                                ALU.add).then_inc(biased.sem, 1)
                        view = dst
                        dve.wait_ge(biased.sem, biased.at(t, q + 1))
                    nc.vector.tensor_reduce(mx[:, q % 2, :], view, AX.X, ALU.max).then_inc(max_done.sem, 1)
                    dve.wait_ge(max_done.sem, max_done.at(t, q + 1))
                    if rel_bias is None:
                        dve.wait_ge(turned.sem, before)
                    nc.vector.tensor_tensor(dst, view, mx[:, q % 2, :].unsqueeze(2).to_broadcast([P, GB, P]),
                                            ALU.subtract).then_inc(shifted.sem, 1)

                def normalise(t, u, half):
                    dve.wait_ge(pv_ready.sem, pv_ready.at(t, half + 1))
                    out = po[:, 0:GB * HQ * (DK + 1)].rearrange("p (b r j e) -> p b r j e", b=GB, r=HQ // NR, j=NR)
                    flat = po[:, 0:GB * HQ * (DK + 1)].rearrange("p (b l e) -> p b l e", b=GB, l=HQ)
                    nc.vector.tensor_scalar(den[:, half, :, :], flat[:, :, :, DK], TINY, None, ALU.max)\
                        .then_inc(den_done.sem, 1)
                    dve.wait_ge(den_done.sem, den_done.at(t, half + 1))
                    nc.vector.reciprocal(rs[:, half, :, :], den[:, half, :, :]).then_inc(recip_done.sem, 1)
                    dve.wait_ge(recip_done.sem, recip_done.at(t, half + 1))
                    for r2 in range(HQ // NR):
                        r = half * (HQ // NR) + r2
                        dst = on[:, u, :, :].rearrange("p b (j r d) -> p b j r d", j=NR, r=NR)[:, :, :, r, :]
                        ins = nc.vector.tensor_tensor(
                            dst, out[:, :, r2, :, 0:DK],
                            rs[:, half, :, r2 * NR:(r2 + 1) * NR].unsqueeze(3).to_broadcast([P, GB, NR, DK]), ALU.mult)
                    ins.then_inc(head_out.sem, 1)

                dve.sem_inc(shifted.sem, shifted.credit)
                dve.sem_inc(head_out.sem, head_out.credit)
                dve.sem_inc(va_used.sem, va_used.credit)
                nc.vector.tensor_scalar(bqs[:, :], bq, SCALE, None, ALU.mult).then_inc(q_scaled.sem, 1)
                if valid is None:
                    nc.vector.memset(V[:, :, :, :, DK:DK + 1], 1.0)
                nx.stats_dve(nc, dve, 0, x_tile)
                nx.apply_dve(nc, dve, 0, x_tile, first=True)
                keys_and_values(0, 0, proj_used.at(0, UG))
                with dve.Fori(0, NG // UN) as i:
                    for u in range(UN):
                        t = i * UN + u
                        shift(t, u, 0)
                        for q in range(NQ):
                            if q + 1 < NQ:
                                shift(t, u, q + 1)
                            if q == 1:
                                nx.stats_dve(nc, dve, t + 1, x_tile)
                            if q == 3:
                                nx.apply_dve(nc, dve, t + 1, x_tile)
                            if q == PRQ:
                                keys_and_values(t + 1, 1 - u, proj_used.at(t + 1, UG))
                            if q == HQ:
                                normalise(t, u, 0)
                        normalise(t, u, 1)
                        dve.wait_ge(out_ready.sem, out_ready.at(t))
                        xg = c.x[:, bass.ds(t * GB, GB), :].rearrange("p b d -> p (b d)")
                        nc.vector.scalar_tensor_tensor(xg, va[:, :], gate, xg, ALU.mult, ALU.add)\
                            .then_inc(va_used.sem, 1)



def experts_ffn(nc, c, S, name, E, FB, TOP, gated, w_up, w_down, keys, gate, b_up=None, b_down=None,
                rw=None, rb=None, loads=None):
    NU = E * FB
    R = 2 if gated else 4
    SENT = -3.0e38
    if gated:
        AT = dict(stats=0, apply=1, turn=2, logits=3, choose=3, exp=3, weights=3, wt=4, bias=4, add=4)
    else:
        AT = dict(stats=1, apply=2, turn=3, logits=5, choose=5, exp=6, weights=7, wt=8, bias=9, add=10)
    with ExitStack() as ctx:
        def sb(n, shape, dt=F32):
            return ctx.enter_context(nc.sbuf_tensor(f"{name}_{n}", shape, dt))

        def ps(n):
            return ctx.enter_context(nc.psum_tensor(f"{name}_{n}", [P, W], F32))

        up_bank = [[ps(f"up{k}{i}") for i in range(R)] for k in range(len(w_up))]
        y_bank = [ps(f"y{i}") for i in range(2)]
        ln_bank = ps("ln")
        lg_bank = ps("lg")
        hT = sb("hT", [P, 2, FB, W])
        sil = sb("sil", [P, 2, W]) if gated else None
        lg = sb("lg_sb", [P, GB, E + 8])
        rep = sb("rep", [P, GB, E + 8])
        m8 = sb("m8", [P, GB, 8])
        sel = sb("sel", [P, GB, E])
        ex = sb("ex", [P, GB, E])
        wsum = sb("wsum", [P, GB])
        wrec = sb("wrec", [P, GB])
        wts = sb("wts", [P, UN, GB, E])
        nx = Norm(nc, ctx, S, name)
        if not gated:
            xsq = sb("xsq", [P, W])
            k2 = sb("k2", [P, E])
            ksq = sb("ksq", [P, E])
            minus = sb("minus", [P, E])
            crow = sb("crow", [1, E])
            wT = sb("wT", [E, W])

        up_ready = S.new("m_up_ready", per=NU)
        sil_done = S.new("m_sil_done", per=NU if gated else 0)
        h_ready = S.new("m_h_ready", per=NU, credit=R)
        y_ready = S.new("m_y_ready", per=E)
        y_added = S.new("m_y_added", per=E, credit=2)
        xT_ready = S.new("m_xT_ready", groups=NG + 1)
        logits_ready = S.new("m_logits_ready", groups=NG + 1)
        step = S.new("m_choice_step", per=5, groups=NG + 1)
        shifted = S.new("m_shifted", groups=NG + 1)
        ex_done = S.new("m_exp_done", groups=NG + 1 if not gated else 0)
        wstep = S.new("m_weight_step", per=3, groups=NG + 1)
        wts_ready = S.new("m_wts_ready", groups=NG + 1)
        wT_turned = S.new("m_wT_turned", groups=NG + 1)
        wT_ready = S.new("m_wT_ready", groups=NG + 1)
        bias_ready = S.new("m_bias_ready", groups=NG + 1)
        bias_added = S.new("m_bias_added", groups=NG + 1)
        kstep = S.new("m_key_step", per=3, groups=1)
        ksum = S.new("m_key_sum", groups=1)

        def x_tile(t, j):
            return c.x[:, t * GB + j, :]

        def x_group(t):
            return c.x[:, t * GB:(t + 1) * GB, :] if isinstance(t, int) else c.x[:, bass.ds(t * GB, GB), :]

        with nc.Block() as block:
            if loads:
                @block.sync
                def _(sp):
                    loads.start(sp)
                    loads.finish(sp)

            @block.gpsimd
            def _(pool):
                nx.rstd_pool(nc, pool, 0, c.minus_half)
                with pool.Fori(0, NG // UN) as i:
                    for u in range(UN):
                        nx.rstd_pool(nc, pool, i * UN + u + 1, c.minus_half)

            @block.tensor
            def _(pe):
                def up(t, u, e):
                    for f in range(FB):
                        k = e * FB + f
                        pe.wait_ge(h_ready.sem, h_ready.at(t, k - R + 1))
                        for j, w in enumerate(w_up):
                            ins = nc.tensor.matmul(up_bank[j][k % R][:, :], w[:, e, f * P:(f + 1) * P],
                                                   nx.out[:, u, :], start=True, stop=True)
                        ins.then_inc(up_ready.sem, 1)

                def down(t, e):
                    pe.wait_ge(y_added.sem, y_added.at(t, e - 1))
                    pe.wait_ge(h_ready.sem, h_ready.at(t, (e + 1) * FB))
                    for b in range(GB):
                        for f in range(FB):
                            ins = nc.tensor.matmul(y_bank[e % 2][:, b * P:(b + 1) * P],
                                                   hT[:, e % 2, f, b * P:(b + 1) * P], w_down[:, e, f, :],
                                                   start=f == 0, stop=f == FB - 1)
                    ins.then_inc(y_ready.sem, 1)

                def logits(t, u):
                    pe.wait_ge(xT_ready.sem, xT_ready.at(t))
                    for b in range(GB):
                        cols = slice(b * P, (b + 1) * P)
                        dst = lg_bank[:, b * E:(b + 1) * E]
                        ins = nc.tensor.matmul(dst, nx.out[:, u, cols], keys if gated else k2[:, :],
                                               start=True, stop=gated)
                        if not gated:
                            nc.tensor.matmul(dst, xsq[:, cols], minus[:, :], start=False, stop=False)
                            ins = nc.tensor.matmul(dst, c.ones[0:1, :], crow[0:1, :], start=False, stop=True)
                    ins.then_inc(logits_ready.sem, 1)

                def turn_weights(t, u):
                    pe.wait_ge(wts_ready.sem, wts_ready.at(t))
                    for b in range(GB):
                        ins = nc.tensor.transpose(ln_bank[0:E, b * P:(b + 1) * P], wts[:, u, b, :], c.ident[:, :])
                    ins.then_inc(wT_turned.sem, 1)

                def add_bias(t):
                    pe.wait_ge(wT_ready.sem, wT_ready.at(t))
                    for b in range(GB):
                        ins = nc.tensor.matmul(ln_bank[:, b * P:(b + 1) * P], wT[:, b * P:(b + 1) * P], b_down,
                                               start=True, stop=True)
                    ins.then_inc(bias_ready.sem, 1)

                def prepare(t, u, e):
                    if e in (None, AT["turn"]):
                        nx.turn_pe(nc, pe, t, ln_bank, c.ident[:, :])
                    if e in (None, AT["logits"]):
                        logits(t, u)
                    if not gated and e in (None, AT["wt"]):
                        turn_weights(t, u)
                    if not gated and e in (None, AT["bias"]):
                        add_bias(t)

                if not gated:
                    pe.wait_ge(kstep.sem, kstep.at(0, 2))
                    nc.tensor.matmul(lg_bank[0:1, 0:E], minus[:, 0:1], ksq[:, :], start=True, stop=True)\
                        .then_inc(ksum.sem, 1)
                    pe.wait_ge(kstep.sem, kstep.at(0, 3))
                prepare(0, 0, None)
                with pe.Fori(0, NG // UN) as i:
                    for u in range(UN):
                        t = i * UN + u
                        up(t, u, 0)
                        for e in range(E):
                            if e + 1 < E:
                                up(t, u, e + 1)
                            down(t, e)
                            prepare(t + 1, 1 - u, e)

            @block.scalar
            def _(act):
                def activate(t, e):
                    for f in range(FB):
                        k = e * FB + f
                        act.wait_ge(up_ready.sem, up_ready.at(t, k + 1))
                        if gated:
                            nc.scalar.activation(sil[:, k % 2, :], up_bank[0][k % R][:, :], ACT.Silu)\
                                .then_inc(sil_done.sem, 1)
                        else:
                            nc.scalar.activation(hT[:, e % 2, f, :], up_bank[0][k % R][:, :], ACT.Gelu,
                                                 bias=b_up[:, e * FB + f:e * FB + f + 1]).then_inc(h_ready.sem, 1)

                def prepare(t, u, e):
                    if e in (None, AT["turn"]):
                        act.wait_ge(nx.turned.sem, nx.turned.at(t))
                        ins = nc.scalar.copy(nx.out[:, u, :], ln_bank[:, :])
                        if not gated:
                            ins = nc.scalar.activation(xsq[:, :], ln_bank[:, :], ACT.Square)
                        ins.then_inc(xT_ready.sem, 1)
                    if not gated and e in (None, AT["exp"]):
                        act.wait_ge(shifted.sem, shifted.at(t))
                        nc.scalar.activation(ex[:, :, :], ex[:, :, :], ACT.Exp).then_inc(ex_done.sem, 1)
                    if not gated and e in (None, AT["wt"]):
                        act.wait_ge(wT_turned.sem, wT_turned.at(t))
                        nc.scalar.copy(wT[:, :], ln_bank[0:E, :]).then_inc(wT_ready.sem, 1)

                if not gated:
                    act.sem_inc(h_ready.sem, h_ready.credit)
                prepare(0, 0, None)
                with act.Fori(0, NG // UN) as i:
                    for u in range(UN):
                        t = i * UN + u
                        activate(t, 0)
                        for e in range(E):
                            if e + 1 < E:
                                activate(t, e + 1)
                            prepare(t + 1, 1 - u, e)

            @block.vector
            def _(dve):
                def choose(t):
                    dve.wait_ge(logits_ready.sem, logits_ready.at(t))
                    nc.vector.tensor_copy(lg[:, :, 0:E], lg_bank[:, 0:GB * E].rearrange("p (b e) -> p b e", b=GB))\
                        .then_inc(step.sem, 1)
                    dve.wait_ge(step.sem, step.at(t, 1))
                    nc.vector.memset(nx.spare[:, :], 0.0)
                    for b in range(GB):
                        ins = nc.vector.max(m8[:, b, :], lg[:, b, 0:E])
                    ins.then_inc(step.sem, 1)
                    dve.wait_ge(step.sem, step.at(t, 2))
                    if not gated:
                        nc.vector.tensor_tensor(ex[:, :, :], lg[:, :, 0:E], m8[:, :, 0:1].to_broadcast([P, GB, E]),
                                                ALU.subtract).then_inc(shifted.sem, 1)
                    nc.vector.memset(m8[:, :, TOP:8], SENT).then_inc(step.sem, 1)
                    dve.wait_ge(step.sem, step.at(t, 3))
                    nc.vector.memset(nx.spare[:, :], 0.0)
                    for b in range(GB):
                        ins = nc.vector.match_replace(rep[:, b, :], m8[:, b, :], lg[:, b, :], 0.5 * SENT)
                    ins.then_inc(step.sem, 1)
                    dve.wait_ge(step.sem, step.at(t, 4))
                    nc.vector.tensor_tensor(sel[:, :, :], rep[:, :, 0:E], lg[:, :, 0:E], ALU.not_equal)\
                        .then_inc(step.sem, 1)

                def weigh(t, u):
                    dve.wait_ge(step.sem, step.at(t, 5))
                    if gated:
                        nc.vector.tensor_scalar(wts[:, u, :, :], sel[:, :, :], gate, None, ALU.mult)\
                            .then_inc(wts_ready.sem, 1)
                        return
                    dve.wait_ge(ex_done.sem, ex_done.at(t))
                    nc.vector.tensor_tensor(sel[:, :, :], ex[:, :, :], sel[:, :, :], ALU.mult).then_inc(wstep.sem, 1)
                    dve.wait_ge(wstep.sem, wstep.at(t, 1))
                    nc.vector.tensor_reduce(wsum[:, :], sel[:, :, :], AX.X, ALU.add).then_inc(wstep.sem, 1)
                    dve.wait_ge(wstep.sem, wstep.at(t, 2))
                    nc.vector.reciprocal(wrec[:, :], wsum[:, :]).then_inc(wstep.sem, 1)
                    dve.wait_ge(wstep.sem, wstep.at(t, 3))
                    nc.vector.scalar_tensor_tensor(wts[:, u, :, :], sel[:, :, :], gate,
                                                   wrec[:, :].unsqueeze(2).to_broadcast([P, GB, E]),
                                                   ALU.mult, ALU.mult).then_inc(wts_ready.sem, 1)

                def add_bias(t):
                    dve.wait_ge(bias_ready.sem, bias_ready.at(t))
                    xg = x_group(t)
                    nc.vector.tensor_tensor(xg, ln_bank[:, :].rearrange("p (b d) -> p b d", b=GB), xg, ALU.add)\
                        .then_inc(bias_added.sem, 1)

                def prepare(t, u, e):
                    if e in (None, AT["stats"]):
                        nx.stats_dve(nc, dve, t, x_tile)
                    if e in (None, AT["apply"]):
                        nx.apply_dve(nc, dve, t, x_tile, first=e is None)
                    if e in (None, AT["choose"]):
                        choose(t)
                    if e in (None, AT["weights"]):
                        weigh(t, u)
                    if not gated and e in (None, AT["add"]):
                        add_bias(t)

                def hidden(t, e):
                    for f in range(FB):
                        k = e * FB + f
                        dve.wait_ge(sil_done.sem, sil_done.at(t, k + 1))
                        nc.vector.tensor_tensor(hT[:, e % 2, f, :], up_bank[1][k % R][:, :], sil[:, k % 2, :],
                                                ALU.mult).then_inc(h_ready.sem, 1)

                def add_expert(t, u, e):
                    if e == 0 and not gated:
                        dve.wait_ge(bias_added.sem, bias_added.at(t))
                    if e == 0 and gated:
                        dve.wait_ge(wts_ready.sem, wts_ready.at(t))
                    if e > 0:
                        dve.wait_ge(y_added.sem, y_added.at(t, e))
                    dve.wait_ge(y_ready.sem, y_ready.at(t, e + 1))
                    for b in range(GB):
                        xb = c.x[:, t * GB + b, :]
                        ins = nc.vector.scalar_tensor_tensor(xb, y_bank[e % 2][:, b * P:(b + 1) * P],
                                                             wts[:, u, b, e:e + 1], xb, ALU.mult, ALU.add)
                    ins.then_inc(y_added.sem, 1)

                if gated:
                    dve.sem_inc(h_ready.sem, h_ready.credit)
                dve.sem_inc(y_added.sem, y_added.credit)
                nc.vector.memset(lg[:, :, E:], SENT)
                if not gated:
                    nc.vector.memset(minus[:, :], -1.0)
                    nc.vector.scalar_tensor_tensor(k2[:, :], keys, 2.0, rw, ALU.mult, ALU.add).then_inc(kstep.sem, 1)
                    nc.vector.tensor_tensor(ksq[:, :], keys, keys, ALU.mult).then_inc(kstep.sem, 1)
                    dve.wait_ge(ksum.sem, ksum.at(0))
                    nc.vector.tensor_tensor(crow[0:1, :], lg_bank[0:1, 0:E], rb, ALU.add).then_inc(kstep.sem, 1)
                prepare(0, 0, None)
                with dve.Fori(0, NG // UN) as i:
                    for u in range(UN):
                        t = i * UN + u
                        if gated:
                            hidden(t, 0)
                        for e in range(E):
                            if gated and e + 1 < E:
                                hidden(t, e + 1)
                            add_expert(t, u, e)
                            prepare(t + 1, 1 - u, e)



def build(nc, d, out):
    with ExitStack() as ctx:
        def sb(name, shape, dt=F32):
            return ctx.enter_context(nc.sbuf_tensor(name, shape, dt))

        S = Signals(nc, ctx)
        c = Core()
        c.ctxT_dram, c.ctx_tok_dram = d["ctxT"], d["ctx_tok"]
        c.x = sb("x", [P, B + GB, D])
        c.ident = sb("ident", [P, P])
        c.ident_bf = sb("ident_bf", [P, P], BF16)
        c.ones = sb("ones", [P, P])
        c.pick = sb("pick", [P, 2, P], BF16)
        c.minus_half = sb("minus_half", [P, GB])
        gates = sb("gates", [P, 8])
        tg = sb("tg", [P, 8])
        c.headmask = sb("headmask", [P, 4])
        c.flip = sb("flip", [P, P])
        c.magic = sb("magic", [P, 1])
        mask = c.mask = sb("mask", [P, (B + GB) * P], BF16)
        valid1 = sb("valid1", [P, B + GB])
        rows = sb("rows", [P, 2, W])
        cols = sb("cols", [P, 8])
        b1_moe = sb("b1_moe", [P, 64])
        keys1 = sb("keys1", [P, 16])
        rw1 = sb("rw1", [P, 16])
        rb1 = sb("rb1", [1, 16])
        b2_moe = sb("b2_moe", [16, D])
        b1_bit = sb("b1_bit", [P, 512])
        b2_bit = sb("b2_bit", [P, D])
        b2_gated = sb("b2_gated", [P, D])
        keys3 = sb("keys3", [P, 8])
        near = sb("near", [P, 34 * 256])
        far = sb("far", [P, 2 * 16 * 512])

        def view(region, at, *dims):
            n = 1
            for k in dims:
                n *= k
            v = region[:, at:at + n]
            if len(dims) == 2:
                return v.rearrange("p (a b) -> p a b", a=dims[0])
            if len(dims) == 3:
                return v.rearrange("p (a b c) -> p a b c", a=dims[0], b=dims[1])
            return v

        def place(region, at, specs):
            views, pairs = [], []
            for name, dims in specs:
                n = d[name].shape[1]
                views.append(view(region, at, *dims))
                pairs.append((region[:, at:at + n], d[name]))
                at += n
            return views, pairs, at

        (wq0, wk0, wv0, wo0), loads0, at = place(near, 0, [
            ("L0_wq", (8, P)), ("L0_wk", (8, P)), ("L0_wv", (8, P)), ("L0_wo", (8, P))])
        (wg0, wu0, wd0), loads0f, at = place(near, at, [("L0_wg", (512,)), ("L0_wu", (512,)), ("L0_wd", (512,))])
        (wq1, wk1, wv1, wo1), loads1, at = place(near, at, [(f"L1_{k}", (D,)) for k in ("wq", "wk", "wv", "wo")])
        rel_bias = view(near, at, HEADS, P)
        assert at + HEADS * P <= near.shape[1]
        rel = d["L1_rel"]
        rel_flipped = view(near, 0, HEADS, P)
        rel_src = bass.AP(rel.tensor, rel.shape[1] // 2 - (P - 1), [[1, P], [rel.shape[1], HEADS], [1, P]])
        (w1_moe, w2_moe), loads1f, _ = place(far, 0, [("L1_w1", (16, 512)), ("L1_w2", (16, 4, D))])
        (wq2, wk2, wv2, wo2), loads2, at = place(near, 0, [
            ("L2_wq", (8, P)), ("L2_wk", (8, P)), ("L2_wv", (8, P)), ("L2_wo", (8, P))])
        (w1_bit, w2_bit), loads2f, at = place(near, at, [("L2_w1", (512,)), ("L2_w2", (512,))])
        (wq3, wk3, wv3, wo3), loads3, at = place(near, at, [(f"L3_{k}", (D,)) for k in ("wq", "wk", "wv", "wo")])
        (wg3, wu3, wd3), loads3f, _ = place(far, 0, [
            ("L3_gate_bank", (8, 256)), ("L3_up_bank", (8, 256)), ("L3_down_bank", (8, 2, D))])

        def row(k):
            return rows[k % 4 * 32:k % 4 * 32 + 1, k // 4, :]

        small_loads = [
            (gates[:, 0:4], d["g_xattn"].partition_broadcast(P)),
            (gates[:, 4:8], d["g_ffn"].partition_broadcast(P)),
            (c.headmask[:, :], d["headmask"]),
            (c.flip[:, :], d["flip"]),
            (cols[:, :], d["cols"]),
            (b1_moe[:, :], d["L1_b1"]), (keys1[:, :], d["L1_keys"]), (rw1[:, :], d["L1_rw"]), (rb1[:, :], d["L1_rb"]),
            (b2_moe[:, :], d["L1_b2"]),
            (b1_bit[:, :], d["L2_b1"].partition_broadcast(P)),
            (b2_bit[:, :], d["L2_b2"].partition_broadcast(P)),
            (keys3[:, :], d["L3_gate_w"]),
        ] + [(row(k), d["rows"][k:k + 1, :]) for k in range(5)]

        setup = S.new("setup_load", per=16 * (len(small_loads) + len(loads0) + 4), groups=1)
        consts = S.new("consts_set", per=2, groups=1)
        first_loads = small_loads + loads0

        with ExitStack() as mctx, nc.Block() as block:
            mask0_u8 = mctx.enter_context(nc.sbuf_tensor("mask0_u8", [P, B * P], U8))
            mask1_i = mctx.enter_context(nc.sbuf_tensor("mask1_i", [P, B * P], I32))
            valid1_i = mctx.enter_context(nc.sbuf_tensor("valid1_i", [P, B], I32))
            mask1_f = mctx.enter_context(nc.sbuf_tensor("mask1_f", [P, B * P], F32))
            all_loads = first_loads + [(mask0_u8[:, :], d["mask0"].partition_broadcast(P)), (mask1_i[:, :], d["mask1"].partition_broadcast(P)),
                                       (valid1_i[:, :], d["mask1_by_key"]),
                                       (c.x[:, 0:B, :].rearrange("p b d -> p (b d)"), d["x_tok"])]
            loaded = setup.at(0, 16 * len(all_loads))
            mstep = S.new("mask_step", per=1, groups=1)
            tstep = S.new("tanh_done", per=1, groups=1)

            @block.sync
            def _(sp):
                for dst, src in all_loads:
                    sp.dma_start(dst, src).then_inc(setup.sem, 16)
                sp.wait_ge(setup.sem, loaded)

            @block.gpsimd
            def _(pool):
                nc.gpsimd.memset(c.ident[:, :], 0.0).then_inc(consts.sem, 1)
                nc.gpsimd.memset(c.ones[:, :], 1.0)
                nc.gpsimd.memset(c.pick[:, :, :], 0.0)
                nc.gpsimd.memset(c.minus_half[:, :], -0.5)
                nc.gpsimd.memset(c.magic[:, :], MAGIC)
                nc.gpsimd.memset(mask[:, B * P:], 0.0)
                nc.gpsimd.memset(valid1[:, B:], 1.0)
                nc.gpsimd.memset(c.x[:, B:B + GB, :], 1.0)
                pool.wait_ge(consts.sem, consts.at(0, 1))
                nc.gpsimd.affine_select(out=c.ident[:, :], in_=c.ident[:, :], compare_op=ALU.not_equal, fill=1.0,
                                        base=0, pattern=[[-1, P]], channel_multiplier=1).then_inc(consts.sem, 1)
                pool.wait_ge(consts.sem, consts.at(0, 2))
                nc.gpsimd.tensor_copy(c.ident_bf[:, :], c.ident[:, :])
                nc.gpsimd.memset(c.pick[0:1, 0, :], 1.0)

            @block.scalar
            def _(act):
                act.wait_ge(setup.sem, loaded)
                nc.scalar.activation(tg[:, :], gates[:, :], ACT.Tanh).then_inc(tstep.sem, 1)

            @block.vector
            def _(dve):
                nc.vector.memset(row(5), 0.0)
                dve.wait_ge(consts.sem, consts.at(0, 2))
                nc.vector.memset(c.pick[32:33, 1, :], 1.0)
                dve.wait_ge(setup.sem, loaded)
                nc.vector.tensor_scalar(mask[:, 0:B * P], mask0_u8[:, :], 1.0, -NEG, ALU.subtract, ALU.mult)
                nc.vector.tensor_scalar(valid1[:, 0:B], valid1_i[:, :], 0.0, None, ALU.not_equal)
                nc.vector.tensor_scalar(mask1_f[:, :], mask1_i[:, :], 0.0, None, ALU.not_equal).then_inc(mstep.sem, 1)
                dve.wait_ge(mstep.sem, mstep.at(0))
                nc.vector.tensor_scalar(mask[32:64, 0:B * P], mask1_f[32:64, :], 1.0, -NEG, ALU.subtract, ALU.mult)
                dve.wait_ge(tstep.sem, tstep.at(0))
                nc.vector.tensor_scalar(b2_gated[:, :], b2_bit[:, :], tg[:, 6:7], None, ALU.mult)

        def col(k):
            return cols[:, k:k + 1]

        attention64(nc, c, S, "L0", 1, wq0, wk0, wv0, wo0, True, None, tg[:, 0:1], row(0),
                    loads=Loads(S, "late_load", loads0f + loads1 + loads1f))
        ternary_ffn(nc, c, S, "L0f", True, [wg0, wu0, wd0], tg[:, 4:5],
                    loads=Loads(S, "late_load", [(rel_flipped, rel_src)]))
        attention8(nc, c, S, "L1", wq1, wk1, wv1, wo1, col(0), col(1), row(1), row(2), tg[:, 1:2],
                   rel_bias=rel_bias, rel_flipped=rel_flipped, mask=mask, valid=valid1)
        experts_ffn(nc, c, S, "L1f", 16, 4, 4, False, [w1_moe], w2_moe, keys1[:, :], tg[:, 5:6],
                    b_up=b1_moe, b_down=b2_moe[:, :], rw=rw1[:, :], rb=rb1[0:1, :],
                    loads=Loads(S, "late_load", loads2 + loads2f + loads3))
        attention64(nc, c, S, "L2", 2, wq2, wk2, wv2, wo2, False, [(col(4), col(5)), (col(6), col(7))],
                    tg[:, 2:3], row(5), loads=Loads(S, "late_load", loads3f))
        ternary_ffn(nc, c, S, "L2f", False, [w1_bit, w2_bit], tg[:, 6:7], hidden_bias=b1_bit[:, :],
                    out_bias=b2_gated[:, :])
        attention8(nc, c, S, "L3", wq3, wk3, wv3, wo3, col(2), col(3), row(3), row(4), tg[:, 3:4])
        experts_ffn(nc, c, S, "L3f", 8, 2, 1, True, [wg3, wu3], wd3, keys3[:, :], tg[:, 7:8])

        saved = S.new("saved", per=16, groups=1)
        with nc.Block() as block:
            @block.sync
            def _(sp):
                sp.dma_start(out, c.x[:, 0:B, :].rearrange("p b d -> p (b d)")).then_inc(saved.sem, 16)
                sp.wait_ge(saved.sem, saved.at(0, 16))



def kernel(**inputs):
    import numpy as np
    import concourse.bacc as bacc
    from concourse.bass_utils import run_bass_kernel_spmd

    a = {k: np.asarray(v) for k, v in inputs.items()}

    def blocks(w):
        return w.reshape(-1, P, w.shape[1]).transpose(1, 0, 2).reshape(P, -1)

    def by_token(v):
        return v.transpose(1, 0, 2).reshape(P, -1)

    host = {
        "x_tok": by_token(a["x"]),
        "ctx_tok": by_token(a["ctx_1024"]),
        "ctxT": a["ctx_1024"].reshape(B * P, D).T,
        "g_xattn": a["g_xattn"],
        "g_ffn": a["g_ffn"],
        "mask0": a["mask_BxS2_bf1"].reshape(B * P).view(np.uint8),
        "mask1": a["mask_Bx1x1xS2_ik0"].reshape(B * P),
        "mask1_by_key": a["mask_Bx1x1xS2_ik0"].reshape(B, P).T,
        "headmask": (np.arange(P)[:, None] // 8 % 4 == np.arange(4)[None, :]).astype(np.float32),
        "flip": np.eye(P, dtype=np.float32)[::-1],
        "cols": np.stack([a[k] for k in ("L1_xattn_bq", "L1_xattn_bk", "L3_xattn_bq", "L3_xattn_bk",
                                         "L2_xattn_ln_m_g", "L2_xattn_ln_m_b", "L2_xattn_ln_l_g",
                                         "L2_xattn_ln_l_b")], axis=1),
        "rows": np.concatenate([np.tile(a[k], GB) for k in ("L0_xattn_b_out", "L1_xattn_bv", "L1_xattn_bo",
                                                            "L3_xattn_bv", "L3_xattn_bo")]).reshape(5, -1),
        "L0_wq": a["L0_xattn_Wq"].T,
        "L0_wk": a["L0_xattn_Wkv"][:HEADS * DH].T,
        "L0_wv": a["L0_xattn_Wkv"][HEADS * DH:].T,
        "L0_wo": blocks(a["L0_xattn_Wout"].T),
        "L0_wg": a["L0_ffn_w_gate"].T,
        "L0_wu": a["L0_ffn_w_up"].T,
        "L0_wd": blocks(a["L0_ffn_w_down"].T),
        "L1_wq": a["L1_xattn_Wq"].T,
        "L1_wk": a["L1_xattn_Wk"].T,
        "L1_wv": a["L1_xattn_Wv"].T,
        "L1_wo": a["L1_xattn_Wo"].T,
        "L1_rel": a["L1_xattn_rel_emb"].T,
        "L1_keys": a["L1_ffn_keys"].T,
        "L1_rw": a["L1_ffn_rw"].T,
        "L1_rb": a["L1_ffn_rb"].reshape(1, -1),
        "L1_w1": a["L1_ffn_w1"].transpose(2, 0, 1).reshape(D, -1),
        "L1_b1": a["L1_ffn_b1"].reshape(-1, P).T,
        "L1_w2": a["L1_ffn_w2"].transpose(0, 2, 1).reshape(-1, P, D).transpose(1, 0, 2).reshape(P, -1),
        "L1_b2": a["L1_ffn_b2"],
        "L2_wq": a["L2_xattn_Wq"],
        "L2_wk": a["L2_xattn_Wkv"][:, :HEADS * DH],
        "L2_wv": a["L2_xattn_Wkv"][:, HEADS * DH:],
        "L2_wo": blocks(a["L2_xattn_Wout"]),
        "L2_w1": a["L2_ffn_W1"].T,
        "L2_w2": blocks(a["L2_ffn_W2"].T),
        "L2_b1": a["L2_ffn_b1"],
        "L2_b2": a["L2_ffn_b2"],
        "L3_wq": a["L3_xattn_Wq"],
        "L3_wk": a["L3_xattn_Wk"],
        "L3_wv": a["L3_xattn_Wv"],
        "L3_wo": a["L3_xattn_Wo"],
        "L3_gate_w": a["L3_ffn_gate_w"].T,
        "L3_gate_bank": a["L3_ffn_gate_bank"].transpose(1, 0, 2).reshape(D, -1),
        "L3_up_bank": a["L3_ffn_up_bank"].transpose(1, 0, 2).reshape(D, -1),
        "L3_down_bank": a["L3_ffn_down_bank"].reshape(-1, P, D).transpose(1, 0, 2).reshape(P, -1),
    }
    host = {k: np.ascontiguousarray(v) for k, v in host.items()}
    nc = bacc.Bacc("TRN2", target_bir_lowering=False, num_devices=1)
    d = {k: nc.dram_tensor("in_" + k, v.shape, mybir.dt.from_np(v.dtype), kind="ExternalInput").ap() for k, v in host.items()}
    out = nc.dram_tensor("out_x", (P, B * D), F32, kind="ExternalOutput").ap()
    build(nc, d, out)
    r = run_bass_kernel_spmd(nc, [{"in_" + k: v for k, v in host.items()}], core_ids=[0])
    return r.results[0]["out_x"].reshape(P, B, D).transpose(1, 0, 2)
```

```python
from contextlib import ExitStack

import concourse.bass as bass
from concourse import mybir

P = 128
B = 32
D = 128
GB = 4
W = GB * P
NG = B // GB
UN = 2
DH = 64
HEADS = 16
NEG = -1.0e30
EPS = 1e-5
MAGIC = 12582912.0

ALU = mybir.AluOpType
ACT = mybir.ActivationFunctionType
BF16 = mybir.dt.bfloat16
F32 = mybir.dt.float32
I32 = mybir.dt.int32
U8 = mybir.dt.uint8
AX = mybir.AxisListType


class Signal:

    def __init__(self, sem, base, per, credit):
        self.sem, self.base, self.per, self.credit = sem, base, per, credit

    def at(self, t, n=1):
        return t * self.per + (self.base + self.credit + n)


class Signals:

    def __init__(self, nc, ctx):
        self.nc, self.ctx, self.sems, self.end = nc, ctx, {}, {}

    def new(self, name, per=1, credit=0, groups=NG, extra=0):
        if name not in self.sems:
            self.sems[name] = self.ctx.enter_context(self.nc.semaphore(name))
        base = self.end.get(name, 0)
        self.end[name] = base + credit + per * groups + extra
        return Signal(self.sems[name], base, per, credit)


class Core:
    pass


class Loads:

    def __init__(self, S, name, pairs):
        self.pairs = pairs
        self.landed = S.new(name, per=16 * len(pairs), groups=1)

    def start(self, sp):
        for dst, src in self.pairs:
            sp.dma_start(dst, src).then_inc(self.landed.sem, 16)

    def finish(self, sp):
        sp.wait_ge(self.landed.sem, self.landed.at(0, 16 * len(self.pairs)))


def ones_like(c, row):
    p = row.start_partition()
    return c.ones[p:p + 1, :]



class Norm:

    def __init__(self, nc, ctx, S, name, tag="", turns=True, groups=NG + 1):
        def sb(n, shape):
            return ctx.enter_context(nc.sbuf_tensor(f"{name}_{n}{tag}", shape, F32))

        self.st = sb("ln_st", [P, GB, 6])
        self.mv = sb("ln_mv", [P, GB, 2])
        self.ve = sb("ln_ve", [P, GB])
        self.rs = sb("ln_rs", [P, GB])
        self.xn = sb("ln_xn", [P, GB, D])
        self.spare = sb("ln_spare", [P, 1])
        self.stats = S.new("ln_stats_done" + tag, groups=groups)
        self.moments = S.new("ln_moments_done" + tag, groups=groups)
        self.veps = S.new("ln_veps_done" + tag, groups=groups)
        self.rstd = S.new("ln_rstd_done" + tag, groups=groups)
        self.normed = S.new("ln_normed" + tag, groups=groups)
        if not turns:
            return
        self.out = sb("ln_T", [P, UN, W])
        self.turned = S.new("ln_turned" + tag, groups=groups)

    def stats_dve(self, nc, dve, t, src):
        for j in range(GB):
            ins = nc.vector.bn_stats(self.st[:, j, :], src(t, j))
        ins.then_inc(self.stats.sem, 1)
        dve.wait_ge(self.stats.sem, self.stats.at(t))
        nc.vector.memset(self.spare[:, :], 0.0)
        for j in range(GB):
            ins = nc.vector.bn_aggr(self.mv[:, j, :], self.st[:, j, :])
        ins.then_inc(self.moments.sem, 1)
        dve.wait_ge(self.moments.sem, self.moments.at(t))
        nc.vector.tensor_scalar(self.ve[:, :], self.mv[:, :, 1], EPS, None, ALU.add).then_inc(self.veps.sem, 1)

    def rstd_pool(self, nc, pool, t, minus_half):
        pool.wait_ge(self.veps.sem, self.veps.at(t))
        nc.gpsimd.tensor_tensor(self.rs[:, :], self.ve[:, :], minus_half[:, 0:GB], ALU.pow)\
            .then_inc(self.rstd.sem, 1)

    def apply_dve(self, nc, dve, t, src, first=False):
        dve.wait_ge(self.rstd.sem, self.rstd.at(t))
        if not first:
            dve.wait_ge(self.turned.sem, self.turned.at(t, 0))
        for j in range(GB):
            ins = nc.vector.tensor_scalar(self.xn[:, j, :], src(t, j), self.mv[:, j, 0:1], self.rs[:, j:j + 1],
                                          ALU.subtract, ALU.mult)
        ins.then_inc(self.normed.sem, 1)

    def turn_pe(self, nc, pe, t, bank, ident):
        pe.wait_ge(self.normed.sem, self.normed.at(t))
        for j in range(GB):
            ins = nc.tensor.transpose(bank[:, j * P:(j + 1) * P], self.xn[:, j, :], ident)
        ins.then_inc(self.turned.sem, 1)



def attention64(nc, c, S, name, NS, wq, wk, wv, wo, masked, affine, gate, bias_row, loads=None):
    M = HEADS // 2
    BQ = GB // NS
    QM = 2 * NS
    NQ = M * QM
    UP = 1 + 2 * NS
    UG = M * UP + NS
    TG = M * (QM + 1)
    KL = NS * P
    LEAD = NS + UP
    LNQ = NQ // 2
    SCALE = float(DH) ** -0.5

    EARLY = {0: range(0, 2)} if NS == 1 else {0: range(0, 1), 1: range(2, 3), 2: range(3, 4), 3: range(4, 5)}
    LATE = {0: range(2, 3)} if NS == 1 else {0: range(1, 2)}

    use = {}
    for q in range(NQ):
        for part in (EARLY, LATE):
            for i in part.get(q % QM, ()):
                use[q // QM + 1, i] = len(use)
        if q == LNQ:
            for s in range(NS):
                use["norm", s] = len(use)
    assert len(use) == UG
    for i in range(UP):
        use[0, i] = use[M, i] - UG
        assert use[0, i] == i - UP

    def proj_use(m, i, last):
        return use[m, i] - (NS if last and use[m, i] > use["norm", 0] else 0)

    def proj_bank(u, k):
        return (LEAD + u * UG + k) % 2

    def turn_step(m):
        return QM * (m + 1) + 1

    def probs_use(q, first):
        if q < 2:
            return q - (0 if first else 1)
        return q + sum(1 for m in range(M) if turn_step(m) < q)

    def out_use(m, last=False):
        return turn_step(m) + 1 + m - (2 if last and m == M - 1 else 0)

    with ExitStack() as ctx:
        def sb(n, shape, dt=F32):
            return ctx.enter_context(nc.sbuf_tensor(f"{name}_{n}", shape, dt))

        def ps(n):
            return ctx.enter_context(nc.psum_tensor(f"{name}_{n}", [P, W], F32))

        pj = [ps(f"proj{i}") for i in range(2)]
        sc = [ps(f"scores{i}") for i in range(2)]
        pt = [ps(f"turned{i}") for i in range(2)]
        po = ps("pv")
        acc = ps("acc")
        QT = sb("QT", [P, 2, W])
        KT = sb("KT", [P, 2, 2, GB, NS * P])
        V = sb("V", [P, 2, GB, NS, 2, DH + 1])
        prob = sb("prob", [P, 2, W])
        probT = sb("probT", [P, 2, W])
        mx = sb("mx", [P, 2, BQ])
        rs = sb("rs", [P, 2, BQ])
        on = sb("on", [P, 2, GB, P])
        onT = sb("onT", [P, 2, W])
        if masked:
            pick = sb("pick", [P, UN, P], BF16)
        nx = Norm(nc, ctx, S, name, groups=NG)
        if NS == 1:
            ctxT = sb("ctxT", [P, 2, W])
            norms = [nx]
            sources = [ctxT]
        else:
            ctx_tok = sb("ctx_tok", [P, 2, GB, D])
            nctx = Norm(nc, ctx, S, name, "_ctx", groups=NG)
            norms = [nctx, nx]
            sources = [nctx.out, nx.out]

        proj_ready = S.new("a_proj_ready", per=M * UP)
        proj_used = S.new("a_proj_used", per=UG, credit=2)
        scores_ready = S.new("a_scores_ready", per=NQ)
        max_done = S.new("a_max_done", per=NQ)
        shifted = S.new("a_shifted", per=NQ, credit=2)
        exp_done = S.new("a_exp_done", per=NQ)
        turned = S.new("a_turned", per=TG)
        turned_used = S.new("a_turned_used", per=TG, credit=2)
        pv_ready = S.new("a_pv_ready", per=NQ)
        recip_done = S.new("a_recip_done", per=NQ)
        head_out = S.new("a_head_out", per=NQ, credit=1)
        out_ready = S.new("a_out_ready")
        x_updated = S.new("a_x_updated", credit=1)
        ones_set = S.new("a_ones_set", groups=1)
        mask_ready = S.new("a_mask_ready")
        load = [S.new(f"a_ctx_load{p}", per=16, groups=NG // UN) for p in range(UN)]

        def load_at(t, p):
            return t * (16 // UN) + (load[p].at(0, 16) - p * (16 // UN))

        def x_tile(t, j):
            return c.x[:, t * GB + j, :]

        def all_groups(eng, group):
            group(0, 0, True, False)
            with eng.Fori(0, (NG - 2) // UN) as i:
                group(i * UN + 1, 1, False, False)
                group(i * UN + 2, 0, False, False)
            group(NG - 1, 1, False, True)

        with nc.Block() as block:
            @block.sync
            def _(sp):
                def load_group(t, p):
                    if NS == 1:
                        sp.dma_start(ctxT[:, p, :], c.ctxT_dram[:, bass.ds(t * W, W)]).then_inc(load[p].sem, 16)
                    else:
                        sp.dma_start(ctx_tok[:, p, :, :].rearrange("p b d -> p (b d)"),
                                     c.ctx_tok_dram[:, bass.ds(t * W, W)]).then_inc(load[p].sem, 16)

                for p in range(UN):
                    load_group(p, p)
                if loads:
                    loads.start(sp)
                with sp.Fori(0, NG // UN - 1) as i:
                    for u in range(UN):
                        if NS == 1:
                            sp.wait_ge(out_ready.sem, out_ready.at(i * UN + u))
                        else:
                            sp.wait_ge(nctx.normed.sem, nctx.normed.at(i * UN + u))
                        load_group((i + 1) * UN + u, u)
                if loads:
                    loads.finish(sp)

            @block.gpsimd
            def _(pool):
                for n in norms:
                    n.rstd_pool(nc, pool, 0, c.minus_half)
                if masked:
                    nc.gpsimd.tensor_copy(pick[:, 0, :], c.ident[:, 0:1].to_broadcast([P, P]))\
                        .then_inc(mask_ready.sem, 1)

                def group(t, u, first, last):
                    if last:
                        return
                    for n in norms:
                        n.rstd_pool(nc, pool, t + 1, c.minus_half)
                    if masked:
                        column = c.ident[:, bass.ds(t + 1, 1)]
                        nc.gpsimd.tensor_copy(pick[:, 1 - u, :], column.to_broadcast([P, P]))\
                            .then_inc(mask_ready.sem, 1)

                all_groups(pool, group)

            @block.tensor
            def _(pe):
                def project(t, u, m, i, last=False):
                    v = 1 - u if m == M else u
                    k = proj_use(m, i, last)
                    bank = pj[proj_bank(u, k)]
                    if NS == 1 and m % M == 0 and i == 1:
                        n = t + 1 if m == M else t
                        pe.wait_ge(load[v].sem, load_at(n, v))
                    pe.wait_ge(proj_used.sem, proj_used.at(t, LEAD + k - 1))
                    if i == 0:
                        ins = nc.tensor.matmul(bank[:, :], wq[:, m % M, :], nx.out[:, v, :], start=True, stop=True)
                    elif i <= NS:
                        ins = nc.tensor.matmul(bank[:, :], wk[:, m % M, :], sources[i - 1][:, v, :],
                                               start=True, stop=True)
                    else:
                        for b in range(GB):
                            ins = nc.tensor.matmul(bank[:, b * P:(b + 1) * P],
                                                   sources[i - 1 - NS][:, v, b * P:(b + 1) * P], wv[:, m % M, :],
                                                   start=True, stop=True)
                    ins.then_inc(proj_ready.sem, 1)

                def scores(t, u, q, last=False):
                    m, h = q // QM, q % QM // NS
                    b0 = q % NS * BQ
                    if q % QM == 0:
                        pe.wait_ge(proj_used.sem, proj_used.at(t, LEAD + proj_use(m, NS, last) + 1))
                    if q == 0 and masked:
                        pe.wait_ge(mask_ready.sem, mask_ready.at(t))
                    pe.wait_ge(shifted.sem, shifted.at(t, q - 1))
                    bank = sc[q % 2]
                    if masked:
                        nc.tensor.matmul(bank[:, :], pick[:, u, :], c.masks[:, :],
                                         start=True, stop=False, skip_group_check=True)
                    for b in range(BQ):
                        ins = nc.tensor.matmul(bank[:, b * KL:(b + 1) * KL],
                                               QT[:, m % 2, (b0 + b) * P:(b0 + b + 1) * P],
                                               KT[:, m % 2, h, b0 + b, :],
                                               start=not masked, stop=True, skip_group_check=masked)
                    ins.then_inc(scores_ready.sem, 1)

                def turn_probs(t, u, q, first):
                    k = probs_use(q, first)
                    pe.wait_ge(exp_done.sem, exp_done.at(t, q + 1))
                    pe.wait_ge(turned_used.sem, turned_used.at(t, k - 1))
                    for b in range(GB):
                        ins = nc.tensor.transpose(pt[k % 2][:, b * P:(b + 1) * P],
                                                  prob[:, q % 2, b * P:(b + 1) * P], c.ident[:, :])
                    ins.then_inc(turned.sem, 1)

                def pv(t, q, first, last=False):
                    m, h = q // QM, q % QM // NS
                    b0 = q % NS * BQ
                    pe.wait_ge(turned_used.sem, turned_used.at(t, probs_use(q, first) + 1))
                    if q % QM == 0:
                        pe.wait_ge(proj_used.sem, proj_used.at(t, LEAD + proj_use(m, 2 * NS, last) + 1))
                    pe.wait_ge(head_out.sem, head_out.at(t, q))
                    for b in range(BQ):
                        for s in range(NS):
                            col = (b * NS + s) * P
                            ins = nc.tensor.matmul(po[:, b * (DH + 1):(b + 1) * (DH + 1)],
                                                   probT[:, q % 2, col:col + P], V[:, m % 2, b0 + b, s, h, :],
                                                   start=s == 0, stop=s == NS - 1)
                    ins.then_inc(pv_ready.sem, 1)

                def turn_out(t, m, last=False):
                    k = out_use(m, last)
                    pe.wait_ge(head_out.sem, head_out.at(t, QM * (m + 1)))
                    pe.wait_ge(turned_used.sem, turned_used.at(t, k - 1))
                    for b in range(GB):
                        ins = nc.tensor.transpose(pt[k % 2][:, b * P:(b + 1) * P],
                                                  on[:, m % 2, b, :], c.ident[:, :])
                    ins.then_inc(turned.sem, 1)

                def project_out(t, m, last=False):
                    if m == 0 and NS == 1 and isinstance(t, int) and t == 0:
                        pe.wait_ge(c.second_load.sem, c.second_loaded)
                    if m == 0:
                        pe.wait_ge(x_updated.sem, x_updated.at(t, 0))
                        nc.tensor.matmul(acc[:, :], ones_like(c, bias_row), bias_row, start=True, stop=False,
                                         skip_group_check=True)
                    pe.wait_ge(turned_used.sem, turned_used.at(t, out_use(m, last) + 1))
                    for b in range(GB):
                        ins = nc.tensor.matmul(acc[:, b * P:(b + 1) * P], onT[:, m % 2, b * P:(b + 1) * P],
                                               wo[:, m, :], start=False, stop=m == M - 1, skip_group_check=True)
                    if m == M - 1:
                        ins.then_inc(out_ready.sem, 1)

                for s, n in enumerate(norms):
                    pe.wait_ge(proj_used.sem, proj_used.at(0, s - 1))
                    n.turn_pe(nc, pe, 0, pj[s % 2], c.ident[:, :])
                pe.wait_ge(ones_set.sem, ones_set.at(0))
                pe.wait_ge(proj_used.sem, proj_used.at(0, NS))
                for i in range(UP):
                    project(0, 0, 0, i)
                scores(0, 0, 0)

                def group(t, u, first, last):
                    for q in range(NQ):
                        if q + 1 < NQ:
                            scores(t, u, q + 1, last)
                        elif not last:
                            scores(t + 1, 1 - u, 0)
                        m = q // QM + 1
                        if m < M or not last:
                            for i in EARLY.get(q % QM, ()):
                                project(t, u, m, i, last)
                        turn_probs(t, u, q, first)
                        if q >= 1:
                            pv(t, q - 1, first, last)
                        elif not first:
                            pv(t - 1, NQ - 1, False)
                        if m < M or not last:
                            for i in LATE.get(q % QM, ()):
                                project(t, u, m, i, last)
                        for m in range(M - 1):
                            if turn_step(m) == q:
                                turn_out(t, m)
                            if turn_step(m) + 1 == q:
                                project_out(t, m)
                        if q == turn_step(M - 1) - NQ and not first:
                            turn_out(t - 1, M - 1)
                        if q == turn_step(M - 2) + 1 - NQ and not first:
                            project_out(t - 1, M - 2)
                        if q == turn_step(M - 1) + 1 - NQ and not first:
                            project_out(t - 1, M - 1)
                        if q == LNQ and not last:
                            for s, n in enumerate(norms):
                                k = use["norm", s]
                                pe.wait_ge(proj_used.sem, proj_used.at(t, LEAD + k - 1))
                                n.turn_pe(nc, pe, t + 1, pj[proj_bank(u, k)], c.ident[:, :])
                    if last:
                        pv(t, NQ - 1, False, True)
                        if turn_step(M - 2) + 1 == NQ:
                            project_out(t, M - 2)
                        turn_out(t, M - 1, True)
                        project_out(t, M - 1, True)

                all_groups(pe, group)

            @block.scalar
            def _(act):
                def copy_projection(t, u, m, i, last=False):
                    act.wait_ge(proj_ready.sem, proj_ready.at(t, m * UP + i + 1))
                    bank = pj[proj_bank(u, proj_use(m, i, last))]
                    if i == 0:
                        ins = nc.scalar.copy(QT[:, m % 2, :], bank[:, :])
                    elif i <= NS:
                        s = i - 1
                        for h in range(2):
                            rows = slice(h * DH, (h + 1) * DH)
                            ins = nc.scalar.copy(KT[rows, m % 2, h, :, s * P:(s + 1) * P],
                                                 bank[rows, :].rearrange("p (b k) -> p b k", b=GB))
                    else:
                        ins = nc.scalar.copy(V[:, m % 2, :, i - 1 - NS, :, 0:DH],
                                             bank[:, :].rearrange("p (b h d) -> p b h d", b=GB, h=2))
                    ins.then_inc(proj_used.sem, 1)

                def copy_norm(t, u, s, n, bank):
                    act.wait_ge(n.turned.sem, n.turned.at(t))
                    if affine is None:
                        nc.scalar.copy(n.out[:, u, :], bank[:, :]).then_inc(proj_used.sem, 1)
                    else:
                        nc.scalar.activation(n.out[:, u, :], bank[:, :], ACT.Identity, bias=affine[s][1],
                                             scale=affine[s][0]).then_inc(proj_used.sem, 1)

                def copy_turned(t, k, dst):
                    act.wait_ge(turned.sem, turned.at(t, k + 1))
                    nc.scalar.copy(dst, pt[k % 2][:, :]).then_inc(turned_used.sem, 1)

                act.sem_inc(proj_used.sem, proj_used.credit)
                act.sem_inc(turned_used.sem, turned_used.credit)
                for s, n in enumerate(norms):
                    copy_norm(0, 0, s, n, pj[s % 2])
                for i in range(UP):
                    copy_projection(0, 0, 0, i)

                def group(t, u, first, last):
                    for q in range(NQ):
                        act.wait_ge(shifted.sem, shifted.at(t, q + 1))
                        nc.scalar.activation(prob[:, q % 2, :], prob[:, q % 2, :], ACT.Exp, scale=SCALE)\
                            .then_inc(exp_done.sem, 1)
                        m = q // QM + 1
                        if m < M or not last:
                            for i in EARLY.get(q % QM, ()):
                                copy_projection(t, u, m, i, last)
                        copy_turned(t, probs_use(q, first), probT[:, q % 2, :])
                        if m < M or not last:
                            for i in LATE.get(q % QM, ()):
                                copy_projection(t, u, m, i, last)
                        for m in range(M - 1):
                            if turn_step(m) == q:
                                copy_turned(t, out_use(m), onT[:, m % 2, :])
                        if q == turn_step(M - 1) - NQ and not first:
                            copy_turned(t - 1, out_use(M - 1), onT[:, (M - 1) % 2, :])
                        if q == LNQ and not last:
                            for s, n in enumerate(norms):
                                copy_norm(t + 1, 1 - u, s, n, pj[proj_bank(u, use["norm", s])])
                    if last:
                        copy_turned(t, out_use(M - 1, True), onT[:, (M - 1) % 2, :])

                all_groups(act, group)

            @block.vector
            def _(dve):
                def shift(t, q, first):
                    dve.wait_ge(scores_ready.sem, scores_ready.at(t, q + 1))
                    view = sc[q % 2][:, :].rearrange("p (b k) -> p b k", b=BQ)
                    nc.vector.tensor_reduce(mx[:, q % 2, :], view, AX.X, ALU.max).then_inc(max_done.sem, 1)
                    dve.wait_ge(max_done.sem, max_done.at(t, q + 1))
                    if q >= 2:
                        dve.wait_ge(turned.sem, turned.at(t, probs_use(q - 2, first) + 1))
                    elif not first:
                        dve.wait_ge(turned.sem, turned.at(t, probs_use(NQ + q - 2, False) + 1 - TG))
                    nc.vector.tensor_tensor(prob[:, q % 2, :].rearrange("p (b k) -> p b k", b=BQ), view,
                                            mx[:, q % 2, :].unsqueeze(2).to_broadcast([P, BQ, KL]), ALU.subtract)\
                        .then_inc(shifted.sem, 1)

                def normalise(t, q):
                    m, h = q // QM, q % QM // NS
                    b0 = q % NS * BQ
                    dve.wait_ge(pv_ready.sem, pv_ready.at(t, q + 1))
                    out = po[:, 0:BQ * (DH + 1)].rearrange("p (b e) -> p b e", b=BQ)
                    nc.vector.reciprocal(rs[:, q % 2, :], out[:, :, DH]).then_inc(recip_done.sem, 1)
                    dve.wait_ge(recip_done.sem, recip_done.at(t, q + 1))
                    nc.vector.tensor_tensor(on[:, m % 2, b0:b0 + BQ, h * DH:(h + 1) * DH], out[:, :, 0:DH],
                                            rs[:, q % 2, :].unsqueeze(2).to_broadcast([P, BQ, DH]), ALU.mult)\
                        .then_inc(head_out.sem, 1)

                def ctx_tile(u):
                    return lambda t, j: ctx_tok[:, u, j, :]

                nc.vector.memset(KT[0:DH, :, 1, :, :], 0.0)
                nc.vector.memset(KT[DH:P, :, 0, :, :], 0.0)
                nc.vector.memset(V[:, :, :, :, :, DH:DH + 1], 1.0).then_inc(ones_set.sem, 1)
                dve.sem_inc(shifted.sem, shifted.credit)
                dve.sem_inc(head_out.sem, head_out.credit)
                dve.sem_inc(x_updated.sem, x_updated.credit)
                if NS == 2:
                    dve.wait_ge(load[0].sem, load[0].at(0, 16))
                    nctx.stats_dve(nc, dve, 0, ctx_tile(0))
                    nctx.apply_dve(nc, dve, 0, ctx_tile(0), first=True)
                nx.stats_dve(nc, dve, 0, x_tile)
                nx.apply_dve(nc, dve, 0, x_tile, first=True)
                shift(0, 0, True)

                def update_x(t):
                    dve.wait_ge(out_ready.sem, out_ready.at(t))
                    xg = c.x[:, bass.ds(t * GB, GB), :].rearrange("p b d -> p (b d)")
                    nc.vector.scalar_tensor_tensor(xg, acc[:, :], gate, xg, ALU.mult, ALU.add)\
                        .then_inc(x_updated.sem, 1)

                def group(t, u, first, last):
                    for q in range(NQ):
                        if q + 1 < NQ:
                            shift(t, q + 1, first)
                        elif not last:
                            shift(t + 1, 0, False)
                        if q >= 1:
                            normalise(t, q - 1)
                        elif not first:
                            normalise(t - 1, NQ - 1)
                        if q == 3 and not first:
                            update_x(t - 1)
                        if last:
                            continue
                        if NS == 2 and q == LNQ // 2 - 3:
                            dve.wait_ge(load[1 - u].sem, load_at(t + 1, 1 - u))
                            nctx.stats_dve(nc, dve, t + 1, ctx_tile(1 - u))
                        if NS == 2 and q == LNQ // 2 - 1:
                            nctx.apply_dve(nc, dve, t + 1, ctx_tile(1 - u))
                        if q == LNQ // 2 - 1 and NS == 1 and first:
                            dve.wait_ge(c.second_load.sem, c.second_loaded)
                        if q == LNQ // 2 - 1:
                            nx.stats_dve(nc, dve, t + 1, x_tile)
                        if q == LNQ // 2 + 1:
                            nx.apply_dve(nc, dve, t + 1, x_tile)
                    if last:
                        normalise(t, NQ - 1)
                        update_x(t)

                all_groups(dve, group)



def ternary_ffn(nc, c, S, name, gated, weights, gate, hidden_bias=None, out_bias=None, loads=None):
    F = 512
    FB = F // P
    NW = len(weights)
    LA = 1 if gated else 2
    X_STEP = GB - LA - 1
    with ExitStack() as ctx:
        def sb(n, shape, dt=F32):
            return ctx.enter_context(nc.sbuf_tensor(f"{name}_{n}", shape, dt))

        def ps(n, dt=F32):
            return ctx.enter_context(nc.psum_tensor(f"{name}_{n}", [P, W], dt))

        up_bank = [[ps(f"up{k}{i}") for i in range(2)] for k in range(NW - 1)]
        xt_bank = ps("xt", BF16)
        ht_bank = ps("ht", BF16)
        y_bank = [ps(f"y{i}") for i in range(UN)]
        wt = sb("wt", [P, NW, F])
        wb = sb("wb", [P, NW, F], BF16)
        wsum = sb("wsum", [P, NW])
        wmean = sb("wmean", [P, NW])
        wtmp = sb("wtmp", [P, NW])
        winv = sb("winv", [P, NW])
        xam = sb("xam", [P, GB])
        xa = sb("xa", [P, GB])
        xs = sb("xs", [P, GB])
        xdq = sb("xdq", [P, UN, NW - 1, GB])
        xr = sb("xr", [P, GB, D])
        xq = sb("xq", [P, GB, D], BF16)
        xqT = sb("xqT", [P, UN, W], BF16)
        pre = sb("pre", [P, 2, F])
        h = sb("h", [P, 2, F])
        ham = sb("ham", [P, 2])
        ha = sb("ha", [P, 2])
        hs = sb("hs", [P, 2])
        hdq = sb("hdq", [P, UN, GB])
        hr = sb("hr", [P, 2, F])
        hq = sb("hq", [P, 2, F], BF16)
        hqT = sb("hqT", [P, 2, F], BF16)
        wtg = sb("wtg", [P, 1])
        y = sb("y_sb", [P, GB, D])
        nx = Norm(nc, ctx, S, name, turns=False, groups=NG)

        w_step = S.new("b_weight_step", per=NW + 6, groups=1)
        w_total = S.new("b_weight_total", groups=1)
        x_step = S.new("b_x_step", per=5)
        xq_ready = S.new("b_xq_ready")
        x_turned = S.new("b_x_turned")
        xT_ready = S.new("b_xT_ready")
        up_ready = S.new("b_up_ready", per=GB)
        act_done = S.new("b_act_done", per=GB)
        a1_done = S.new("b_a1_done", per=GB, credit=2)
        am_done = S.new("b_am_done", per=GB)
        ha_done = S.new("b_ha_done", per=GB)
        hs_done = S.new("b_hs_done", per=GB)
        rounded = S.new("b_rounded", per=GB)
        hq_ready = S.new("b_hq_ready", per=GB)
        h_turned = S.new("b_h_turned", per=GB)
        hT_ready = S.new("b_hT_ready", per=GB, credit=1)
        y_ready = S.new("b_y_ready")
        y_done = S.new("b_y_done", per=0 if out_bias is None else 1)
        x_updated = S.new("b_x_updated", credit=UN)
        hdq_done = S.new("b_hdq_done")

        def x_tile(t, j):
            return c.x[:, t * GB + j, :]

        def all_groups(eng, group):
            group(0, 0, True, False)
            with eng.Fori(0, (NG - 2) // UN) as i:
                group(i * UN + 1, 1, False, False)
                group(i * UN + 2, 0, False, False)
            group(NG - 1, 1, False, True)

        def ahead(t, u, b, last):
            if b < GB:
                return t, u, b
            return None if last else (t + 1, 1 - u, b - GB)

        def behind(t, u, b, first):
            if b >= 0:
                return t, u, b
            return None if first else (t - 1, 1 - u, b + GB)

        with nc.Block() as block:
            if loads:
                @block.sync
                def _(sp):
                    loads.start(sp)
                    loads.finish(sp)

            @block.gpsimd
            def _(pool):
                nx.rstd_pool(nc, pool, 0, c.minus_half)

                def group(t, u, first, last):
                    if not last:
                        nx.rstd_pool(nc, pool, t + 1, c.minus_half)

                all_groups(pool, group)

            @block.tensor
            def _(pe):
                def turn_x(t):
                    pe.wait_ge(xq_ready.sem, xq_ready.at(t))
                    for b in range(GB):
                        ins = nc.tensor.transpose(xt_bank[:, b * P:(b + 1) * P], xq[:, b, :], c.ident_bf[:, :])
                    ins.then_inc(x_turned.sem, 1)

                def up(t, u, b):
                    if b == 0:
                        pe.wait_ge(xT_ready.sem, xT_ready.at(t))
                    pe.wait_ge(a1_done.sem, a1_done.at(t, b - 1))
                    for k in range(NW - 1):
                        ins = nc.tensor.matmul(up_bank[k][b % 2][:, :], xqT[:, u, b * P:(b + 1) * P], wb[:, k, :],
                                               start=True, stop=True)
                    ins.then_inc(up_ready.sem, 1)

                def turn_h(t, u, b):
                    pe.wait_ge(hq_ready.sem, hq_ready.at(t, b + 1))
                    pe.wait_ge(hT_ready.sem, hT_ready.at(t, b))
                    for f in range(FB):
                        ins = nc.tensor.transpose(ht_bank[:, f * P:(f + 1) * P], hq[:, b % 2, f * P:(f + 1) * P],
                                                  c.ident_bf[:, :])
                    ins.then_inc(h_turned.sem, 1)

                def down(t, u, b):
                    if b == 0:
                        pe.wait_ge(x_updated.sem, x_updated.at(t, -1))
                    pe.wait_ge(hT_ready.sem, hT_ready.at(t, b + 1))
                    for f in range(FB):
                        ins = nc.tensor.matmul(y_bank[u][:, b * P:(b + 1) * P], hqT[:, b % 2, f * P:(f + 1) * P],
                                               wb[:, NW - 1, f * P:(f + 1) * P], start=f == 0, stop=f == FB - 1)
                    if b == GB - 1:
                        ins.then_inc(y_ready.sem, 1)

                pe.wait_ge(w_step.sem, w_step.at(0, NW))
                nc.tensor.matmul(y_bank[1][:, 0:NW], c.ones[:, :], wsum[:, :], start=True, stop=True)\
                    .then_inc(w_total.sem, 1)
                turn_x(0)
                pe.wait_ge(w_step.sem, w_step.at(0, NW + 6))
                for b in range(LA + 1):
                    up(0, 0, b)

                def group(t, u, first, last):
                    for b in range(GB):
                        if b == X_STEP and not last:
                            turn_x(t + 1)
                        n = ahead(t, u, b + LA + 1, last)
                        if n:
                            up(*n)
                        n = behind(t, u, b - 1, first)
                        if n:
                            turn_h(*n)
                            down(*n)
                    if last:
                        turn_h(t, u, GB - 1)
                        down(t, u, GB - 1)

                all_groups(pe, group)

            @block.scalar
            def _(act):
                def copy_x(t, u):
                    act.wait_ge(x_turned.sem, x_turned.at(t))
                    nc.scalar.copy(xqT[:, u, :], xt_bank[:, :]).then_inc(xT_ready.sem, 1)

                def activate(t, u, b, fresh=False):
                    if gated:
                        act.wait_ge(up_ready.sem, up_ready.at(t, b + 1))
                        nc.scalar.activation(pre[:, b % 2, :], up_bank[0][b % 2][:, :], ACT.Silu,
                                             scale=xdq[:, u, 0, b:b + 1]).then_inc(act_done.sem, 1)
                    else:
                        act.wait_ge(a1_done.sem, a1_done.at(t, b + 1))
                        if not fresh:
                            act.wait_ge(rounded.sem, rounded.at(t, b - 1))
                        nc.scalar.activation(h[:, b % 2, :], pre[:, b % 2, :], ACT.Gelu).then_inc(act_done.sem, 1)

                def round_up(t, b):
                    act.wait_ge(hs_done.sem, hs_done.at(t, b + 1))
                    nc.scalar.activation(hr[:, b % 2, :], h[:, b % 2, :], ACT.Identity, bias=c.magic[:, :],
                                         scale=hs[:, b % 2:b % 2 + 1]).then_inc(rounded.sem, 1)

                act.sem_inc(hT_ready.sem, hT_ready.credit)
                copy_x(0, 0)
                for b in range(2):
                    activate(0, 0, b, fresh=True)

                def copy_h(t, u, b):
                    act.wait_ge(h_turned.sem, h_turned.at(t, b + 1))
                    nc.scalar.copy(hqT[:, b % 2, :], ht_bank[:, :]).then_inc(hT_ready.sem, 1)

                def group(t, u, first, last):
                    for b in range(GB):
                        round_up(t, b)
                        if b == X_STEP and not last:
                            copy_x(t + 1, 1 - u)
                        n = ahead(t, u, b + 2, last)
                        if n:
                            activate(*n)
                        n = behind(t, u, b - 1, first)
                        if n:
                            copy_h(*n)
                    if last:
                        copy_h(t, u, GB - 1)

                all_groups(act, group)

            @block.vector
            def _(dve):
                def quantise_x(t, u, first=False):
                    dve.wait_ge(nx.normed.sem, nx.normed.at(t))
                    nc.vector.tensor_reduce(xam[:, :], nx.xn[:, :, :], AX.X, ALU.max, apply_absolute_value=True)\
                        .then_inc(x_step.sem, 1)
                    dve.wait_ge(x_step.sem, x_step.at(t, 1))
                    nc.vector.tensor_scalar(xa[:, :], xam[:, :], 1e-5, 1.0 / 127.0, ALU.max, ALU.mult)\
                        .then_inc(x_step.sem, 1)
                    dve.wait_ge(x_step.sem, x_step.at(t, 2))
                    nc.vector.reciprocal(xs[:, :], xa[:, :]).then_inc(x_step.sem, 1)
                    for k in range(NW - 1):
                        ins = nc.vector.tensor_scalar(xdq[:, u, k, :], xa[:, :], wmean[:, k:k + 1], None, ALU.mult)
                    ins.then_inc(x_step.sem, 1)
                    dve.wait_ge(x_step.sem, x_step.at(t, 4))
                    for b in range(GB):
                        ins = nc.vector.tensor_scalar(xr[:, b, :], nx.xn[:, b, :], xs[:, b:b + 1], MAGIC,
                                                      ALU.mult, ALU.add)
                    ins.then_inc(x_step.sem, 1)
                    dve.wait_ge(x_step.sem, x_step.at(t, 5))
                    if not first:
                        dve.wait_ge(xT_ready.sem, xT_ready.at(t, 0))
                    nc.vector.tensor_scalar(xq[:, :, :], xr[:, :, :], MAGIC, 127.0, ALU.subtract, ALU.min)\
                        .then_inc(xq_ready.sem, 1)

                def hidden(t, u, b):
                    k = b % 2
                    if gated:
                        dve.wait_ge(act_done.sem, act_done.at(t, b + 1))
                        nc.vector.scalar_tensor_tensor(h[:, k, :], up_bank[1][k][:, :], xdq[:, u, 1, b:b + 1],
                                                       pre[:, k, :], ALU.mult, ALU.mult).then_inc(a1_done.sem, 1)
                    else:
                        dve.wait_ge(up_ready.sem, up_ready.at(t, b + 1))
                        nc.vector.scalar_tensor_tensor(pre[:, k, :], up_bank[0][k][:, :], xdq[:, u, 0, b:b + 1],
                                                       hidden_bias, ALU.mult, ALU.add).then_inc(a1_done.sem, 1)

                def scale_h(t, u, b):
                    k = b % 2
                    if gated:
                        dve.wait_ge(a1_done.sem, a1_done.at(t, b + 1))
                    else:
                        dve.wait_ge(act_done.sem, act_done.at(t, b + 1))
                    nc.vector.tensor_reduce(ham[:, k:k + 1], h[:, k, :], AX.X, ALU.max, apply_absolute_value=True)\
                        .then_inc(am_done.sem, 1)
                    dve.wait_ge(am_done.sem, am_done.at(t, b + 1))
                    nc.vector.tensor_scalar(ha[:, k:k + 1], ham[:, k:k + 1], 1e-5, 1.0 / 127.0, ALU.max, ALU.mult)\
                        .then_inc(ha_done.sem, 1)
                    dve.wait_ge(ha_done.sem, ha_done.at(t, b + 1))
                    nc.vector.reciprocal(hs[:, k:k + 1], ha[:, k:k + 1]).then_inc(hs_done.sem, 1)
                    ins = nc.vector.tensor_scalar(hdq[:, u, b:b + 1], ha[:, k:k + 1], wtg[:, :], None, ALU.mult)
                    if b == GB - 1:
                        ins.then_inc(hdq_done.sem, 1)

                def quantise_h(t, u, b, fresh=False):
                    if not fresh:
                        dve.wait_ge(h_turned.sem, h_turned.at(t, b - 1))
                    dve.wait_ge(rounded.sem, rounded.at(t, b + 1))
                    nc.vector.tensor_scalar(hq[:, b % 2, :], hr[:, b % 2, :], MAGIC, 127.0, ALU.subtract, ALU.min)\
                        .then_inc(hq_ready.sem, 1)

                dve.sem_inc(a1_done.sem, a1_done.credit)
                dve.sem_inc(x_updated.sem, x_updated.credit)
                for k, w in enumerate(weights):
                    nc.vector.tensor_reduce(wsum[:, k:k + 1], w, AX.X, ALU.add, apply_absolute_value=True)\
                        .then_inc(w_step.sem, 1)
                nx.stats_dve(nc, dve, 0, x_tile)
                dve.wait_ge(w_total.sem, w_total.at(0))
                nc.vector.tensor_scalar(wmean[:, :], y_bank[1][:, 0:NW], 1.0 / (P * F), 1e-5, ALU.mult, ALU.max)\
                    .then_inc(w_step.sem, 1)
                dve.wait_ge(w_step.sem, w_step.at(0, NW + 1))
                nc.vector.reciprocal(winv[:, :], wmean[:, :]).then_inc(w_step.sem, 1)
                nc.vector.tensor_tensor(wtg[:, :], wmean[:, NW - 1:NW], gate, ALU.mult).then_inc(w_step.sem, 1)
                dve.wait_ge(w_step.sem, w_step.at(0, NW + 3))
                for k, w in enumerate(weights):
                    ins = nc.vector.tensor_scalar(wt[:, k, :], w, winv[:, k:k + 1], MAGIC, ALU.mult, ALU.add)
                ins.then_inc(w_step.sem, 1)
                dve.wait_ge(w_step.sem, w_step.at(0, NW + 4))
                nc.vector.tensor_scalar(wt[:, :, :], wt[:, :, :], MAGIC, 1.0, ALU.subtract, ALU.min)\
                    .then_inc(w_step.sem, 1)
                dve.wait_ge(w_step.sem, w_step.at(0, NW + 5))
                nc.vector.tensor_scalar(wb[:, :, :], wt[:, :, :], -1.0, None, ALU.max).then_inc(w_step.sem, 1)
                nx.apply_dve(nc, dve, 0, x_tile, first=True)
                quantise_x(0, 0, first=True)
                for b in range(LA):
                    hidden(0, 0, b)

                def update_x(t, u):
                    dve.wait_ge(y_ready.sem, y_ready.at(t))
                    dve.wait_ge(hdq_done.sem, hdq_done.at(t))
                    for b in range(GB):
                        xb = c.x[:, t * GB + b, :]
                        dst, addend = (xb, xb) if out_bias is None else (y[:, b, :], out_bias)
                        ins = nc.vector.scalar_tensor_tensor(dst, y_bank[u][:, b * P:(b + 1) * P],
                                                             hdq[:, u, b:b + 1], addend, ALU.mult, ALU.add)
                    if out_bias is not None:
                        ins.then_inc(y_done.sem, 1)
                        dve.wait_ge(y_done.sem, y_done.at(t))
                        xg = c.x[:, bass.ds(t * GB, GB), :]
                        ins = nc.vector.tensor_tensor(xg, y[:, :, :], xg, ALU.add)
                    ins.then_inc(x_updated.sem, 1)

                def group(t, u, first, last):
                    for b in range(GB):
                        if b == 0 and not last:
                            nx.stats_dve(nc, dve, t + 1, x_tile)
                        scale_h(t, u, b)
                        n = behind(t, u, b - 1, first)
                        if n:
                            quantise_h(*n, fresh=first and b < 3)
                        n = ahead(t, u, b + LA, last)
                        if n:
                            hidden(*n)
                        if b == 0 and not last:
                            nx.apply_dve(nc, dve, t + 1, x_tile, first=True)
                            quantise_x(t + 1, 1 - u)
                        if b == 1 and not first:
                            update_x(t - 1, 1 - u)
                    if last:
                        quantise_h(t, u, GB - 1)
                        update_x(t, u)

                all_groups(dve, group)



def attention8(nc, c, S, name, wq, wk, wv, wo, bq, bk, bv_row, bo_row, gate, rel_bias=None, rel_flipped=None,
               mask_row=None, valid=None):
    DK = D // HEADS
    NR = 4
    NQ = HEADS
    HQ = 8
    NS = 4
    AHEAD = 2
    TG = NQ + 1
    UG = 3
    SCALE = float(DK) ** -0.5
    TINY = 1e-30
    STATS, APPLY, NORM, QUERIES, KEYS, VALUES = 1, 3, 5, 7, 10, 10
    TURN_OUT, OUT, ADD = 2, 4, 5

    def probs_use(q, first):
        return q - 1 if q <= TURN_OUT and not first else q

    with ExitStack() as ctx:
        def sb(n, shape, dt=F32):
            return ctx.enter_context(nc.sbuf_tensor(f"{name}_{n}", shape, dt))

        def ps(n):
            return ctx.enter_context(nc.psum_tensor(f"{name}_{n}", [P, W], F32))

        pj = ps("proj")
        sc = [ps(f"scores{i}") for i in range(NS)]
        pt = ps("turned")
        po = ps("pv")
        va = ps("va")
        QT = sb("QT", [P, UN, NR, W])
        Kx = sb("Kx", [P, UN, NR, W])
        V = sb("V", [P, UN, GB, HEADS, DK + 1])
        bqs = sb("bqs", [P, 1])
        bks = sb("bks", [P, NR])
        prob = sb("prob", [P, 2, W])
        probT = sb("probT", [P, 2, W])
        mx = sb("mx", [P, 2, GB])
        den = sb("den", [P, NQ // HQ, GB, HQ])
        rs = sb("rs", [P, NQ // HQ, GB, HQ])
        on = sb("on", [P, GB, D])
        onT = sb("onT", [P, W])
        ctxT = sb("ctxT", [P, UN, W])
        if mask_row is not None:
            pick = sb("pick", [P, UN, P], BF16)
            vg = sb("vg", [P, UN, GB])
        nx = Norm(nc, ctx, S, name, groups=NG)

        zeros_set = S.new("c_zeros_set", groups=1)
        biases_set = S.new("c_biases_set", groups=1)
        proj_ready = S.new("c_proj_ready", per=2)
        proj_used = S.new("c_proj_used", per=UG, credit=1)
        v_ready = S.new("c_v_ready")
        vg_ready = S.new("c_vg_ready")
        va_used = S.new("c_va_used", per=2, credit=1)
        scores_ready = S.new("c_scores_ready", per=NQ)
        biased = S.new("c_biased", per=NQ if rel_bias is not None else 0)
        max_done = S.new("c_max_done", per=NQ)
        shifted = S.new("c_shifted", per=NQ, credit=NS)
        exp_done = S.new("c_exp_done", per=NQ)
        turned = S.new("c_turned", per=TG)
        turned_used = S.new("c_turned_used", per=TG, credit=1)
        pv_ready = S.new("c_pv_ready", per=NQ // HQ)
        den_done = S.new("c_den_done", per=NQ // HQ)
        recip_done = S.new("c_recip_done", per=NQ // HQ)
        head_out = S.new("c_head_out", per=NQ // HQ, credit=1)
        out_ready = S.new("c_out_ready")
        flip_ready = S.new("c_flip_ready", per=HEADS * P // W, groups=1)
        flip_used = S.new("c_flip_used", per=HEADS * P // W, groups=1)
        mask_ready = S.new("c_mask_ready")
        load = [S.new(f"c_ctx_load{p}", per=16, groups=NG // UN) for p in range(UN)]

        def load_at(t, p):
            return t * (16 // UN) + (load[p].at(0, 16) - p * (16 // UN))

        def x_tile(t, j):
            return c.x[:, t * GB + j, :]

        def sequences(t):
            return slice(t * GB, (t + 1) * GB) if isinstance(t, int) else bass.ds(t * GB, GB)

        def all_groups(eng, group):
            group(0, 0, True, False)
            with eng.Fori(0, (NG - 2) // UN) as i:
                group(i * UN + 1, 1, False, False)
                group(i * UN + 2, 0, False, False)
            group(NG - 1, 1, False, True)

        with nc.Block() as block:
            @block.sync
            def _(sp):
                def load_group(t, p):
                    sp.dma_start(ctxT[:, p, :], c.ctxT_dram[:, bass.ds(t * W, W)]).then_inc(load[p].sem, 16)

                for p in range(UN):
                    load_group(p, p)
                with sp.Fori(0, NG // UN - 1) as i:
                    for u in range(UN):
                        sp.wait_ge(v_ready.sem, v_ready.at(i * UN + u))
                        load_group((i + 1) * UN + u, u)

            @block.gpsimd
            def _(pool):
                nc.gpsimd.memset(QT[:, :, :, :], 0.0).then_inc(zeros_set.sem, 1)
                nx.rstd_pool(nc, pool, 0, c.minus_half)
                if mask_row is not None:
                    nc.gpsimd.tensor_copy(pick[:, 0, :], c.ident[:, mask_row:mask_row + 1].to_broadcast([P, P]))\
                        .then_inc(mask_ready.sem, 1)

                def group(t, u, first, last):
                    if last:
                        return
                    nx.rstd_pool(nc, pool, t + 1, c.minus_half)
                    if mask_row is not None:
                        column = c.ident[:, bass.ds(t + (mask_row + 1), 1)]
                        nc.gpsimd.tensor_copy(pick[:, 1 - u, :], column.to_broadcast([P, P]))\
                            .then_inc(mask_ready.sem, 1)

                all_groups(pool, group)

            @block.tensor
            def _(pe):
                def project_q(t, u, n):
                    pe.wait_ge(proj_used.sem, n)
                    nc.tensor.matmul(pj[:, :], wq, nx.out[:, u, :], start=True, stop=True)\
                        .then_inc(proj_ready.sem, 1)

                def project_k(t, u, n):
                    pe.wait_ge(load[u].sem, load_at(t, u))
                    pe.wait_ge(proj_used.sem, n)
                    nc.tensor.matmul(pj[:, :], wk, ctxT[:, u, :], start=True, stop=True)\
                        .then_inc(proj_ready.sem, 1)

                def project_v(t, u, n):
                    pe.wait_ge(va_used.sem, n)
                    nc.tensor.matmul(va[:, :], ones_like(c, bv_row), bv_row, start=True, stop=False,
                                     skip_group_check=True)
                    for b in range(GB):
                        ins = nc.tensor.matmul(va[:, b * P:(b + 1) * P], ctxT[:, u, b * P:(b + 1) * P], wv,
                                               start=False, stop=True, skip_group_check=True)
                    ins.then_inc(v_ready.sem, 1)

                def scores(t, u, q):
                    r, j = q // NR, q % NR
                    if q == 0:
                        pe.wait_ge(proj_used.sem, proj_used.at(t, UG))
                        if mask_row is not None:
                            pe.wait_ge(mask_ready.sem, mask_ready.at(t))
                    pe.wait_ge(shifted.sem, shifted.at(t, q - NS + 1))
                    bank = sc[q % NS]
                    if mask_row is not None:
                        nc.tensor.matmul(bank[:, :], pick[:, u, :], c.masks[:, :], start=True, stop=False,
                                         skip_group_check=True)
                    for b in range(GB):
                        ins = nc.tensor.matmul(bank[:, b * P:(b + 1) * P],
                                               QT[:, u, j, b * P:(b + 1) * P], Kx[:, u, r, b * P:(b + 1) * P],
                                               start=mask_row is None, stop=True, skip_group_check=mask_row is not None)
                    ins.then_inc(scores_ready.sem, 1)

                def turn_probs(t, q, first):
                    k = probs_use(q, first)
                    pe.wait_ge(exp_done.sem, exp_done.at(t, q + 1))
                    pe.wait_ge(turned_used.sem, turned_used.at(t, k))
                    for b in range(GB):
                        ins = nc.tensor.transpose(pt[:, b * P:(b + 1) * P],
                                                  prob[:, q % 2, b * P:(b + 1) * P], c.ident[:, :])
                    ins.then_inc(turned.sem, 1)

                def pv(t, u, q, first):
                    r, j = q // NR, q % NR
                    pe.wait_ge(turned_used.sem, turned_used.at(t, probs_use(q, first) + 1))
                    if q % HQ == 0:
                        pe.wait_ge(head_out.sem, head_out.at(t, q // HQ))
                    for b in range(GB):
                        col = (b * HQ + q % HQ) * (DK + 1)
                        ins = nc.tensor.matmul(po[:, col:col + DK + 1], probT[:, q % 2, b * P:(b + 1) * P],
                                               V[:, u, b, 4 * j + r, :], start=True, stop=True)
                    if q % HQ == HQ - 1:
                        ins.then_inc(pv_ready.sem, 1)

                def turn_out(t, n):
                    pe.wait_ge(head_out.sem, head_out.at(t, NQ // HQ))
                    pe.wait_ge(turned_used.sem, n)
                    for b in range(GB):
                        ins = nc.tensor.transpose(pt[:, b * P:(b + 1) * P], on[:, b, :], c.ident[:, :])
                    ins.then_inc(turned.sem, 1)

                def project_out(t, n_free, n_turned):
                    pe.wait_ge(va_used.sem, n_free)
                    nc.tensor.matmul(va[:, :], ones_like(c, bo_row), bo_row, start=True, stop=False,
                                     skip_group_check=True)
                    pe.wait_ge(turned_used.sem, n_turned)
                    for b in range(GB):
                        ins = nc.tensor.matmul(va[:, b * P:(b + 1) * P], onT[:, b * P:(b + 1) * P], wo,
                                               start=False, stop=True, skip_group_check=True)
                    ins.then_inc(out_ready.sem, 1)

                if rel_bias is not None:
                    for k in range(HEADS * P // W):
                        if k >= 2:
                            pe.wait_ge(flip_used.sem, flip_used.at(0, k - 1))
                        nc.tensor.matmul(sc[k % 2][:, :], c.flip[:, :], rel_flipped[:, k * 4:(k + 1) * 4, :],
                                         start=True, stop=True).then_inc(flip_ready.sem, 1)
                    pe.wait_ge(flip_used.sem, flip_used.at(0, HEADS * P // W))
                pe.wait_ge(proj_used.sem, proj_used.at(0, 0))
                nx.turn_pe(nc, pe, 0, pj, c.ident[:, :])
                project_q(0, 0, proj_used.at(0, 1))
                project_k(0, 0, proj_used.at(0, 2))
                project_v(0, 0, va_used.at(0, 0))
                for q in range(AHEAD):
                    scores(0, 0, q)

                def group(t, u, first, last):
                    for q in range(NQ):
                        turn_probs(t, q, first)
                        if q + AHEAD < NQ:
                            scores(t, u, q + AHEAD)
                        elif not last:
                            scores(t + 1, 1 - u, q + AHEAD - NQ)
                        if q >= 1:
                            pv(t, u, q - 1, first)
                        elif not first:
                            pv(t - 1, 1 - u, NQ - 1, False)
                        if q == TURN_OUT and not first:
                            turn_out(t - 1, turned_used.at(t, TURN_OUT))
                        if q == OUT and not first:
                            project_out(t - 1, va_used.at(t, 0), turned_used.at(t, TURN_OUT + 1))
                        if q == NORM and not last:
                            pe.wait_ge(proj_used.sem, proj_used.at(t, UG))
                            nx.turn_pe(nc, pe, t + 1, pj, c.ident[:, :])
                        if q == QUERIES and not last:
                            project_q(t + 1, 1 - u, proj_used.at(t, UG + 1))
                        if q == KEYS and not last:
                            project_k(t + 1, 1 - u, proj_used.at(t, UG + 2))
                        if q == VALUES and not last:
                            project_v(t + 1, 1 - u, va_used.at(t, 1))
                    if last:
                        pv(t, u, NQ - 1, False)
                        turn_out(t, turned_used.at(t, NQ))
                        project_out(t, va_used.at(t, 1), turned_used.at(t, NQ + 1))

                all_groups(pe, group)

            @block.scalar
            def _(act):
                def copy_norm(t, u):
                    act.wait_ge(nx.turned.sem, nx.turned.at(t))
                    nc.scalar.copy(nx.out[:, u, :], pj[:, :]).then_inc(proj_used.sem, 1)

                def copy_q(t, u, quadrants=range(NR)):
                    act.wait_ge(proj_ready.sem, proj_ready.at(t, 1))
                    for j in quadrants:
                        quadrant = slice(32 * j, 32 * j + 32)
                        ins = nc.scalar.activation(QT[quadrant, u, j, :], pj[quadrant, :], ACT.Identity,
                                                   bias=bqs[quadrant, :], scale=SCALE)
                        if j == NR - 1:
                            ins.then_inc(proj_used.sem, 1)

                def copy_k(t, u, masks=range(NR)):
                    act.wait_ge(proj_ready.sem, proj_ready.at(t, 2))
                    for r in masks:
                        ins = nc.scalar.activation(Kx[:, u, r, :], pj[:, :], ACT.Identity, bias=bks[:, r:r + 1],
                                                   scale=c.headmask[:, r:r + 1])
                        if r == NR - 1:
                            ins.then_inc(proj_used.sem, 1)

                def copy_turned(t, k, dst):
                    act.wait_ge(turned.sem, turned.at(t, k + 1))
                    nc.scalar.copy(dst, pt[:, :]).then_inc(turned_used.sem, 1)

                act.sem_inc(proj_used.sem, proj_used.credit)
                act.sem_inc(turned_used.sem, turned_used.credit)
                if rel_bias is not None:
                    for k in range(HEADS * P // W):
                        act.wait_ge(flip_ready.sem, flip_ready.at(0, k + 1))
                        nc.scalar.copy(rel_bias[:, k * 4:(k + 1) * 4, :].rearrange("p h k -> p (h k)"),
                                       sc[k % 2][:, :]).then_inc(flip_used.sem, 1)
                copy_norm(0, 0)
                act.wait_ge(zeros_set.sem, zeros_set.at(0))
                act.wait_ge(biases_set.sem, biases_set.at(0))
                copy_q(0, 0)
                copy_k(0, 0)

                def exp(t, q):
                    act.wait_ge(shifted.sem, shifted.at(t, q + 1))
                    nc.scalar.activation(prob[:, q % 2, :], prob[:, q % 2, :], ACT.Exp).then_inc(exp_done.sem, 1)

                exp(0, 0)

                def group(t, u, first, last):
                    for q in range(NQ):
                        copy_turned(t, probs_use(q, first), probT[:, q % 2, :])
                        if q + 1 < NQ:
                            exp(t, q + 1)
                        elif not last:
                            exp(t + 1, 0)
                        if q == TURN_OUT and not first:
                            copy_turned(t, TURN_OUT, onT[:, :])
                        if q == NORM and not last:
                            copy_norm(t + 1, 1 - u)
                        for k in range(2):
                            if q == QUERIES + k and not last:
                                copy_q(t + 1, 1 - u, range(2 * k, 2 * k + 2))
                            if q == KEYS + k and not last:
                                copy_k(t + 1, 1 - u, range(2 * k, 2 * k + 2))
                    if last:
                        copy_turned(t, NQ, onT[:, :])

                all_groups(act, group)

            @block.vector
            def _(dve):
                def take_values(t, u):
                    view = va[:, :].rearrange("p (b h d) -> p b h d", b=GB, h=HEADS)
                    if valid is None:
                        dve.wait_ge(v_ready.sem, v_ready.at(t))
                        ins = nc.vector.tensor_copy(V[:, u, :, :, 0:DK], view)
                    else:
                        nc.vector.tensor_copy(vg[:, u, :], valid[:, sequences(t)]).then_inc(vg_ready.sem, 1)
                        dve.wait_ge(vg_ready.sem, vg_ready.at(t))
                        nc.vector.tensor_copy(V[:, u, :, :, DK], vg[:, u, :].unsqueeze(2).to_broadcast([P, GB, HEADS]))
                        dve.wait_ge(v_ready.sem, v_ready.at(t))
                        for b in range(GB):
                            ins = nc.vector.tensor_scalar(V[:, u, b, :, 0:DK], view[:, b, :, :], vg[:, u, b:b + 1],
                                                          None, ALU.mult)
                    ins.then_inc(va_used.sem, 1)

                def shift(t, q, first):
                    h = 4 * (q % NR) + q // NR
                    dve.wait_ge(scores_ready.sem, scores_ready.at(t, q + 1))
                    view = sc[q % NS][:, :].rearrange("p (b k) -> p b k", b=GB)
                    dst = prob[:, q % 2, :].rearrange("p (b k) -> p b k", b=GB)
                    if rel_bias is not None:
                        nc.vector.tensor_tensor(view, view, rel_bias[:, h, :].unsqueeze(1).to_broadcast([P, GB, P]),
                                                ALU.add).then_inc(biased.sem, 1)
                        dve.wait_ge(biased.sem, biased.at(t, q + 1))
                    nc.vector.tensor_reduce(mx[:, q % 2, :], view, AX.X, ALU.max).then_inc(max_done.sem, 1)
                    dve.wait_ge(max_done.sem, max_done.at(t, q + 1))
                    if q >= 2:
                        dve.wait_ge(turned.sem, turned.at(t, probs_use(q - 2, first) + 1))
                    elif not first:
                        dve.wait_ge(turned.sem, turned.at(t, NQ + q - 2 + 1 - TG))
                    nc.vector.tensor_tensor(dst, view, mx[:, q % 2, :].unsqueeze(2).to_broadcast([P, GB, P]),
                                            ALU.subtract).then_inc(shifted.sem, 1)

                def normalise(t, half):
                    dve.wait_ge(pv_ready.sem, pv_ready.at(t, half + 1))
                    out = po[:, 0:GB * HQ * (DK + 1)].rearrange("p (b r j e) -> p b r j e", b=GB, r=HQ // NR, j=NR)
                    flat = po[:, 0:GB * HQ * (DK + 1)].rearrange("p (b l e) -> p b l e", b=GB, l=HQ)
                    nc.vector.tensor_scalar(den[:, half, :, :], flat[:, :, :, DK], TINY, None, ALU.max)\
                        .then_inc(den_done.sem, 1)
                    dve.wait_ge(den_done.sem, den_done.at(t, half + 1))
                    nc.vector.reciprocal(rs[:, half, :, :], den[:, half, :, :]).then_inc(recip_done.sem, 1)
                    dve.wait_ge(recip_done.sem, recip_done.at(t, half + 1))
                    for r2 in range(HQ // NR):
                        r = half * (HQ // NR) + r2
                        dst = on[:, :, :].rearrange("p b (j r d) -> p b j r d", j=NR, r=NR)[:, :, :, r, :]
                        ins = nc.vector.tensor_tensor(
                            dst, out[:, :, r2, :, 0:DK],
                            rs[:, half, :, r2 * NR:(r2 + 1) * NR].unsqueeze(3).to_broadcast([P, GB, NR, DK]), ALU.mult)
                    ins.then_inc(head_out.sem, 1)

                dve.sem_inc(shifted.sem, shifted.credit)
                dve.sem_inc(head_out.sem, head_out.credit)
                dve.sem_inc(va_used.sem, va_used.credit)
                nc.vector.tensor_scalar(bqs[:, :], bq, SCALE, None, ALU.mult)
                nc.vector.tensor_scalar(bks[:, :], c.headmask[:, :], bk, None, ALU.mult).then_inc(biases_set.sem, 1)
                if valid is None:
                    nc.vector.memset(V[:, :, :, :, DK:DK + 1], 1.0)
                nx.stats_dve(nc, dve, 0, x_tile)
                nx.apply_dve(nc, dve, 0, x_tile, first=True)
                take_values(0, 0)
                for q in range(AHEAD):
                    shift(0, q, True)

                def update_x(t):
                    dve.wait_ge(out_ready.sem, out_ready.at(t))
                    xg = c.x[:, bass.ds(t * GB, GB), :].rearrange("p b d -> p (b d)")
                    nc.vector.scalar_tensor_tensor(xg, va[:, :], gate, xg, ALU.mult, ALU.add)\
                        .then_inc(va_used.sem, 1)

                def group(t, u, first, last):
                    for q in range(NQ):
                        if q + AHEAD < NQ:
                            shift(t, q + AHEAD, first)
                        elif not last:
                            shift(t + 1, q + AHEAD - NQ, False)
                        if q == 0 and not first:
                            normalise(t - 1, NQ // HQ - 1)
                        if q > 0 and q % HQ == 0:
                            normalise(t, q // HQ - 1)
                        if q == ADD and not first:
                            update_x(t - 1)
                        if q == STATS and not last:
                            nx.stats_dve(nc, dve, t + 1, x_tile)
                        if q == APPLY and not last:
                            nx.apply_dve(nc, dve, t + 1, x_tile)
                        if q == VALUES and not last:
                            take_values(t + 1, 1 - u)
                    if last:
                        normalise(t, NQ // HQ - 1)
                        update_x(t)

                all_groups(dve, group)



def experts_ffn(nc, c, S, name, E, FB, TOP, gated, w_up, w_down, keys, gate, b_up=None, b_down=None,
                rw=None, rb=None, loads=None):
    NU = E * FB
    R = 2 if gated else 4
    SENT = -3.0e38
    if gated:
        AT = dict(stats=0, apply=1, turn=2, logits=3, choose=3, exp=3, weights=3, wt=4, bias=4, add=4)
    else:
        AT = dict(stats=1, apply=2, turn=3, logits=5, choose=5, exp=6, weights=7, wt=8, bias=9, add=10)
    with ExitStack() as ctx:
        def sb(n, shape, dt=F32):
            return ctx.enter_context(nc.sbuf_tensor(f"{name}_{n}", shape, dt))

        def ps(n):
            return ctx.enter_context(nc.psum_tensor(f"{name}_{n}", [P, W], F32))

        up_bank = [[ps(f"up{k}{i}") for i in range(R)] for k in range(len(w_up))]
        y_bank = [ps(f"y{i}") for i in range(2)]
        ln_bank = ps("ln")
        lg_bank = ps("lg")
        hT = sb("hT", [P, 2, FB, W])
        sil = sb("sil", [P, 2, W]) if gated else None
        lg = sb("lg_sb", [P, GB, E + 8])
        rep = sb("rep", [P, GB, E + 8])
        m8 = sb("m8", [P, GB, 8])
        sel = sb("sel", [P, GB, E])
        ex = sb("ex", [P, GB, E])
        wsum = sb("wsum", [P, GB])
        wrec = sb("wrec", [P, GB])
        wts = sb("wts", [P, UN, GB, E])
        nx = Norm(nc, ctx, S, name)
        if not gated:
            xsq = sb("xsq", [P, W])
            k2 = sb("k2", [P, E])
            ksq = sb("ksq", [P, E])
            minus = sb("minus", [P, E])
            crow = sb("crow", [1, E])
            wT = sb("wT", [E, W])

        up_ready = S.new("m_up_ready", per=NU)
        sil_done = S.new("m_sil_done", per=NU if gated else 0)
        h_ready = S.new("m_h_ready", per=NU, credit=R)
        y_ready = S.new("m_y_ready", per=E)
        y_added = S.new("m_y_added", per=E, credit=2)
        xT_ready = S.new("m_xT_ready", groups=NG + 1)
        logits_ready = S.new("m_logits_ready", groups=NG + 1)
        step = S.new("m_choice_step", per=5, groups=NG + 1)
        shifted = S.new("m_shifted", groups=NG + 1)
        ex_done = S.new("m_exp_done", groups=NG + 1 if not gated else 0)
        wstep = S.new("m_weight_step", per=3, groups=NG + 1)
        wts_ready = S.new("m_wts_ready", groups=NG + 1)
        wT_turned = S.new("m_wT_turned", groups=NG + 1)
        wT_ready = S.new("m_wT_ready", groups=NG + 1)
        bias_ready = S.new("m_bias_ready", groups=NG + 1)
        bias_added = S.new("m_bias_added", groups=NG + 1)
        kstep = S.new("m_key_step", per=3, groups=1)
        ksum = S.new("m_key_sum", groups=1)

        def x_tile(t, j):
            return c.x[:, t * GB + j, :]

        def x_group(t):
            return c.x[:, t * GB:(t + 1) * GB, :] if isinstance(t, int) else c.x[:, bass.ds(t * GB, GB), :]

        with nc.Block() as block:
            if loads:
                @block.sync
                def _(sp):
                    loads.start(sp)
                    loads.finish(sp)

            @block.gpsimd
            def _(pool):
                nx.rstd_pool(nc, pool, 0, c.minus_half)
                with pool.Fori(0, NG // UN) as i:
                    for u in range(UN):
                        nx.rstd_pool(nc, pool, i * UN + u + 1, c.minus_half)

            @block.tensor
            def _(pe):
                def up(t, u, e):
                    for f in range(FB):
                        k = e * FB + f
                        pe.wait_ge(h_ready.sem, h_ready.at(t, k - R + 1))
                        for j, w in enumerate(w_up):
                            ins = nc.tensor.matmul(up_bank[j][k % R][:, :], w[:, e, f * P:(f + 1) * P],
                                                   nx.out[:, u, :], start=True, stop=True)
                        ins.then_inc(up_ready.sem, 1)

                def down(t, e):
                    pe.wait_ge(y_added.sem, y_added.at(t, e - 1))
                    pe.wait_ge(h_ready.sem, h_ready.at(t, (e + 1) * FB))
                    for b in range(GB):
                        for f in range(FB):
                            ins = nc.tensor.matmul(y_bank[e % 2][:, b * P:(b + 1) * P],
                                                   hT[:, e % 2, f, b * P:(b + 1) * P], w_down[:, e, f, :],
                                                   start=f == 0, stop=f == FB - 1)
                    ins.then_inc(y_ready.sem, 1)

                def logits(t, u):
                    pe.wait_ge(xT_ready.sem, xT_ready.at(t))
                    for b in range(GB):
                        cols = slice(b * P, (b + 1) * P)
                        dst = lg_bank[:, b * E:(b + 1) * E]
                        ins = nc.tensor.matmul(dst, nx.out[:, u, cols], keys if gated else k2[:, :],
                                               start=True, stop=gated)
                        if not gated:
                            nc.tensor.matmul(dst, xsq[:, cols], minus[:, :], start=False, stop=False)
                            ins = nc.tensor.matmul(dst, c.ones[0:1, :], crow[0:1, :], start=False, stop=True)
                    ins.then_inc(logits_ready.sem, 1)

                def turn_weights(t, u):
                    pe.wait_ge(wts_ready.sem, wts_ready.at(t))
                    for b in range(GB):
                        ins = nc.tensor.transpose(ln_bank[0:E, b * P:(b + 1) * P], wts[:, u, b, :], c.ident[:, :])
                    ins.then_inc(wT_turned.sem, 1)

                def add_bias(t):
                    pe.wait_ge(wT_ready.sem, wT_ready.at(t))
                    for b in range(GB):
                        ins = nc.tensor.matmul(ln_bank[:, b * P:(b + 1) * P], wT[:, b * P:(b + 1) * P], b_down,
                                               start=True, stop=True)
                    ins.then_inc(bias_ready.sem, 1)

                def prepare(t, u, e):
                    if e in (None, AT["turn"]):
                        nx.turn_pe(nc, pe, t, ln_bank, c.ident[:, :])
                    if e in (None, AT["logits"]):
                        logits(t, u)
                    if not gated and e in (None, AT["wt"]):
                        turn_weights(t, u)
                    if not gated and e in (None, AT["bias"]):
                        add_bias(t)

                if not gated:
                    pe.wait_ge(kstep.sem, kstep.at(0, 2))
                    nc.tensor.matmul(lg_bank[0:1, 0:E], minus[:, 0:1], ksq[:, :], start=True, stop=True)\
                        .then_inc(ksum.sem, 1)
                    pe.wait_ge(kstep.sem, kstep.at(0, 3))
                prepare(0, 0, None)
                with pe.Fori(0, NG // UN) as i:
                    for u in range(UN):
                        t = i * UN + u
                        up(t, u, 0)
                        for e in range(E):
                            if e + 1 < E:
                                up(t, u, e + 1)
                            down(t, e)
                            prepare(t + 1, 1 - u, e)

            @block.scalar
            def _(act):
                def activate(t, e):
                    for f in range(FB):
                        k = e * FB + f
                        act.wait_ge(up_ready.sem, up_ready.at(t, k + 1))
                        if gated:
                            nc.scalar.activation(sil[:, k % 2, :], up_bank[0][k % R][:, :], ACT.Silu)\
                                .then_inc(sil_done.sem, 1)
                        else:
                            nc.scalar.activation(hT[:, e % 2, f, :], up_bank[0][k % R][:, :], ACT.Gelu,
                                                 bias=b_up[:, e * FB + f:e * FB + f + 1]).then_inc(h_ready.sem, 1)

                def prepare(t, u, e):
                    if e in (None, AT["turn"]):
                        act.wait_ge(nx.turned.sem, nx.turned.at(t))
                        ins = nc.scalar.copy(nx.out[:, u, :], ln_bank[:, :])
                        if not gated:
                            ins = nc.scalar.activation(xsq[:, :], ln_bank[:, :], ACT.Square)
                        ins.then_inc(xT_ready.sem, 1)
                    if not gated and e in (None, AT["exp"]):
                        act.wait_ge(shifted.sem, shifted.at(t))
                        nc.scalar.activation(ex[:, :, :], ex[:, :, :], ACT.Exp).then_inc(ex_done.sem, 1)
                    if not gated and e in (None, AT["wt"]):
                        act.wait_ge(wT_turned.sem, wT_turned.at(t))
                        nc.scalar.copy(wT[:, :], ln_bank[0:E, :]).then_inc(wT_ready.sem, 1)

                if not gated:
                    act.sem_inc(h_ready.sem, h_ready.credit)
                prepare(0, 0, None)
                with act.Fori(0, NG // UN) as i:
                    for u in range(UN):
                        t = i * UN + u
                        activate(t, 0)
                        for e in range(E):
                            if e + 1 < E:
                                activate(t, e + 1)
                            prepare(t + 1, 1 - u, e)

            @block.vector
            def _(dve):
                def choose(t):
                    dve.wait_ge(logits_ready.sem, logits_ready.at(t))
                    nc.vector.tensor_copy(lg[:, :, 0:E], lg_bank[:, 0:GB * E].rearrange("p (b e) -> p b e", b=GB))\
                        .then_inc(step.sem, 1)
                    dve.wait_ge(step.sem, step.at(t, 1))
                    nc.vector.memset(nx.spare[:, :], 0.0)
                    for b in range(GB):
                        ins = nc.vector.max(m8[:, b, :], lg[:, b, 0:E])
                    ins.then_inc(step.sem, 1)
                    dve.wait_ge(step.sem, step.at(t, 2))
                    if not gated:
                        nc.vector.tensor_tensor(ex[:, :, :], lg[:, :, 0:E], m8[:, :, 0:1].to_broadcast([P, GB, E]),
                                                ALU.subtract).then_inc(shifted.sem, 1)
                    nc.vector.memset(m8[:, :, TOP:8], SENT).then_inc(step.sem, 1)
                    dve.wait_ge(step.sem, step.at(t, 3))
                    nc.vector.memset(nx.spare[:, :], 0.0)
                    for b in range(GB):
                        ins = nc.vector.match_replace(rep[:, b, :], m8[:, b, :], lg[:, b, :], 0.5 * SENT)
                    ins.then_inc(step.sem, 1)
                    dve.wait_ge(step.sem, step.at(t, 4))
                    nc.vector.tensor_tensor(sel[:, :, :], rep[:, :, 0:E], lg[:, :, 0:E], ALU.not_equal)\
                        .then_inc(step.sem, 1)

                def weigh(t, u):
                    dve.wait_ge(step.sem, step.at(t, 5))
                    if gated:
                        nc.vector.tensor_scalar(wts[:, u, :, :], sel[:, :, :], gate, None, ALU.mult)\
                            .then_inc(wts_ready.sem, 1)
                        return
                    dve.wait_ge(ex_done.sem, ex_done.at(t))
                    nc.vector.tensor_tensor(sel[:, :, :], ex[:, :, :], sel[:, :, :], ALU.mult).then_inc(wstep.sem, 1)
                    dve.wait_ge(wstep.sem, wstep.at(t, 1))
                    nc.vector.tensor_reduce(wsum[:, :], sel[:, :, :], AX.X, ALU.add).then_inc(wstep.sem, 1)
                    dve.wait_ge(wstep.sem, wstep.at(t, 2))
                    nc.vector.reciprocal(wrec[:, :], wsum[:, :]).then_inc(wstep.sem, 1)
                    dve.wait_ge(wstep.sem, wstep.at(t, 3))
                    nc.vector.scalar_tensor_tensor(wts[:, u, :, :], sel[:, :, :], gate,
                                                   wrec[:, :].unsqueeze(2).to_broadcast([P, GB, E]),
                                                   ALU.mult, ALU.mult).then_inc(wts_ready.sem, 1)

                def add_bias(t):
                    dve.wait_ge(bias_ready.sem, bias_ready.at(t))
                    xg = x_group(t)
                    nc.vector.tensor_tensor(xg, ln_bank[:, :].rearrange("p (b d) -> p b d", b=GB), xg, ALU.add)\
                        .then_inc(bias_added.sem, 1)

                def prepare(t, u, e):
                    if e in (None, AT["stats"]):
                        nx.stats_dve(nc, dve, t, x_tile)
                    if e in (None, AT["apply"]):
                        nx.apply_dve(nc, dve, t, x_tile, first=e is None)
                    if e in (None, AT["choose"]):
                        choose(t)
                    if e in (None, AT["weights"]):
                        weigh(t, u)
                    if not gated and e in (None, AT["add"]):
                        add_bias(t)

                def hidden(t, e):
                    for f in range(FB):
                        k = e * FB + f
                        dve.wait_ge(sil_done.sem, sil_done.at(t, k + 1))
                        nc.vector.tensor_tensor(hT[:, e % 2, f, :], up_bank[1][k % R][:, :], sil[:, k % 2, :],
                                                ALU.mult).then_inc(h_ready.sem, 1)

                def add_expert(t, u, e):
                    if e == 0 and not gated:
                        dve.wait_ge(bias_added.sem, bias_added.at(t))
                    if e == 0 and gated:
                        dve.wait_ge(wts_ready.sem, wts_ready.at(t))
                    if e > 0:
                        dve.wait_ge(y_added.sem, y_added.at(t, e))
                    dve.wait_ge(y_ready.sem, y_ready.at(t, e + 1))
                    for b in range(GB):
                        xb = c.x[:, t * GB + b, :]
                        ins = nc.vector.scalar_tensor_tensor(xb, y_bank[e % 2][:, b * P:(b + 1) * P],
                                                             wts[:, u, b, e:e + 1], xb, ALU.mult, ALU.add)
                    ins.then_inc(y_added.sem, 1)

                if gated:
                    dve.sem_inc(h_ready.sem, h_ready.credit)
                dve.sem_inc(y_added.sem, y_added.credit)
                nc.vector.memset(lg[:, :, E:], SENT)
                if not gated:
                    nc.vector.memset(minus[:, :], -1.0)
                    nc.vector.scalar_tensor_tensor(k2[:, :], keys, 2.0, rw, ALU.mult, ALU.add).then_inc(kstep.sem, 1)
                    nc.vector.tensor_tensor(ksq[:, :], keys, keys, ALU.mult).then_inc(kstep.sem, 1)
                    dve.wait_ge(ksum.sem, ksum.at(0))
                    nc.vector.tensor_tensor(crow[0:1, :], lg_bank[0:1, 0:E], rb, ALU.add).then_inc(kstep.sem, 1)
                prepare(0, 0, None)
                with dve.Fori(0, NG // UN) as i:
                    for u in range(UN):
                        t = i * UN + u
                        if gated:
                            hidden(t, 0)
                        for e in range(E):
                            if gated and e + 1 < E:
                                hidden(t, e + 1)
                            add_expert(t, u, e)
                            prepare(t + 1, 1 - u, e)



def build(nc, d, out):
    with ExitStack() as ctx:
        def sb(name, shape, dt=F32):
            return ctx.enter_context(nc.sbuf_tensor(name, shape, dt))

        S = Signals(nc, ctx)
        c = Core()
        c.ctxT_dram, c.ctx_tok_dram = d["ctxT"], d["ctx_tok"]
        c.x = sb("x", [P, B + GB, D])
        c.ident = sb("ident", [P, P])
        c.ident_bf = sb("ident_bf", [P, P], BF16)
        c.ones = sb("ones", [P, P])
        c.minus_half = sb("minus_half", [P, GB])
        gates = sb("gates", [P, 8])
        tg = sb("tg", [P, 8])
        c.headmask = sb("headmask", [P, 4])
        c.flip = sb("flip", [P, P])
        c.magic = sb("magic", [P, 1])
        c.masks = sb("masks", [P, W], BF16)
        valid1 = sb("valid1", [P, B + GB])
        rows = sb("rows", [P, 2, W])
        cols = sb("cols", [P, 8])
        b1_moe = sb("b1_moe", [P, 64])
        keys1 = sb("keys1", [P, 16])
        rw1 = sb("rw1", [P, 16])
        rb1 = sb("rb1", [1, 16])
        b2_moe = sb("b2_moe", [16, D])
        b1_bit = sb("b1_bit", [P, 512])
        b2_bit = sb("b2_bit", [P, D])
        b2_gated = sb("b2_gated", [P, D])
        keys3 = sb("keys3", [P, 8])
        near = sb("near", [P, 34 * 256])
        far = sb("far", [P, 2 * 16 * 512])

        def view(region, at, *dims):
            n = 1
            for k in dims:
                n *= k
            v = region[:, at:at + n]
            if len(dims) == 2:
                return v.rearrange("p (a b) -> p a b", a=dims[0])
            if len(dims) == 3:
                return v.rearrange("p (a b c) -> p a b c", a=dims[0], b=dims[1])
            return v

        def place(region, at, specs):
            views, pairs = [], []
            for name, dims in specs:
                n = d[name].shape[1]
                views.append(view(region, at, *dims))
                pairs.append((region[:, at:at + n], d[name]))
                at += n
            return views, pairs, at

        (wq0, wk0, wv0, wo0), loads0, at = place(near, 0, [
            ("L0_wq", (8, P)), ("L0_wk", (8, P)), ("L0_wv", (8, P)), ("L0_wo", (8, P))])
        (wg0, wu0, wd0), loads0f, at = place(near, at, [("L0_wg", (512,)), ("L0_wu", (512,)), ("L0_wd", (512,))])
        (wq1, wk1, wv1, wo1), loads1, at = place(near, at, [(f"L1_{k}", (D,)) for k in ("wq", "wk", "wv", "wo")])
        rel_bias = view(near, at, HEADS, P)
        assert at + HEADS * P <= near.shape[1]
        rel = d["L1_rel"]
        rel_flipped = view(near, 0, HEADS, P)
        rel_src = bass.AP(rel.tensor, rel.shape[1] // 2 - (P - 1), [[1, P], [rel.shape[1], HEADS], [1, P]])
        (w1_moe, w2_moe), loads1f, _ = place(far, 0, [("L1_w1", (16, 512)), ("L1_w2", (16, 4, D))])
        (wq2, wk2, wv2, wo2), loads2, at = place(near, 0, [
            ("L2_wq", (8, P)), ("L2_wk", (8, P)), ("L2_wv", (8, P)), ("L2_wo", (8, P))])
        (w1_bit, w2_bit), loads2f, at = place(near, at, [("L2_w1", (512,)), ("L2_w2", (512,))])
        (wq3, wk3, wv3, wo3), loads3, at = place(near, at, [(f"L3_{k}", (D,)) for k in ("wq", "wk", "wv", "wo")])
        (wg3, wu3, wd3), loads3f, _ = place(far, 0, [
            ("L3_gate_bank", (8, 256)), ("L3_up_bank", (8, 256)), ("L3_down_bank", (8, 2, D))])

        def row(k):
            return rows[k % 4 * 32:k % 4 * 32 + 1, k // 4, :]

        small_loads = [
            (gates[:, 0:4], d["g_xattn"].partition_broadcast(P)),
            (gates[:, 4:8], d["g_ffn"].partition_broadcast(P)),
            (c.headmask[:, :], d["headmask"]),
            (c.flip[:, :], d["flip"]),
            (cols[:, :], d["cols"]),
            (b1_moe[:, :], d["L1_b1"]), (keys1[:, :], d["L1_keys"]), (rw1[:, :], d["L1_rw"]), (rb1[:, :], d["L1_rb"]),
            (b2_moe[:, :], d["L1_b2"]),
            (b1_bit[:, :], d["L2_b1"].partition_broadcast(P)),
            (b2_bit[:, :], d["L2_b2"].partition_broadcast(P)),
            (keys3[:, :], d["L3_gate_w"]),
        ] + [(row(k), d["rows"][k:k + 1, :]) for k in range(5)]

        consts = S.new("consts_set", per=2, groups=1)
        x_flat = c.x[:, 0:B, :].rearrange("p b d -> p (b d)")
        first_loads = [(x_flat[:, 0:W], d["x_tok"][:, 0:W])] + loads0[0:3] + small_loads
        second_loads = [(x_flat[:, W:], d["x_tok"][:, W:])] + loads0[3:]

        with ExitStack() as mctx, nc.Block() as block:
            mask0_u8 = mctx.enter_context(nc.sbuf_tensor("mask0_u8", [NG, W], U8))
            mask1_i = mctx.enter_context(nc.sbuf_tensor("mask1_i", [32 + NG, W], I32))
            mask1_f = mctx.enter_context(nc.sbuf_tensor("mask1_f", [32 + NG, W], F32))
            valid1_i = mctx.enter_context(nc.sbuf_tensor("valid1_i", [P, B], I32))
            all_loads = [(mask0_u8[:, :], d["mask0"]), (mask1_i[32:32 + NG, :], d["mask1"]),
                         (valid1_i[:, :], d["mask1_by_key"])] + first_loads
            setup = S.new("setup_load", per=16 * len(all_loads), groups=1)
            c.second_load = S.new("second_load", per=16 * len(second_loads), groups=1)
            c.second_loaded = c.second_load.at(0, 16 * len(second_loads))
            loaded = setup.at(0, 16 * len(all_loads))
            mstep = S.new("mask_step", per=1, groups=1)
            tstep = S.new("tanh_done", per=1, groups=1)

            @block.sync
            def _(sp):
                for dst, src in all_loads:
                    sp.dma_start(dst, src).then_inc(setup.sem, 16)
                for dst, src in second_loads:
                    sp.dma_start(dst, src).then_inc(c.second_load.sem, 16)
                sp.wait_ge(setup.sem, loaded)

            @block.gpsimd
            def _(pool):
                nc.gpsimd.memset(c.ident[:, :], 0.0).then_inc(consts.sem, 1)
                nc.gpsimd.memset(c.ones[:, :], 1.0)
                nc.gpsimd.memset(c.masks[:, :], 0.0)
                nc.gpsimd.memset(c.minus_half[:, :], -0.5)
                nc.gpsimd.memset(c.magic[:, :], MAGIC)
                nc.gpsimd.memset(valid1[:, B:], 1.0)
                nc.gpsimd.memset(c.x[:, B:B + GB, :], 1.0)
                pool.wait_ge(consts.sem, consts.at(0, 1))
                nc.gpsimd.affine_select(out=c.ident[:, :], in_=c.ident[:, :], compare_op=ALU.not_equal, fill=1.0,
                                        base=0, pattern=[[-1, P]], channel_multiplier=1).then_inc(consts.sem, 1)
                pool.wait_ge(consts.sem, consts.at(0, 2))
                nc.gpsimd.tensor_copy(c.ident_bf[:, :], c.ident[:, :])

            @block.scalar
            def _(act):
                act.wait_ge(setup.sem, loaded)
                nc.scalar.activation(tg[:, :], gates[:, :], ACT.Tanh).then_inc(tstep.sem, 1)

            @block.vector
            def _(dve):
                nc.vector.memset(row(5), 0.0)
                dve.wait_ge(setup.sem, loaded)
                dve.wait_ge(consts.sem, consts.at(0, 2))
                nc.vector.tensor_scalar(c.masks[0:NG, :], mask0_u8[:, :], 1.0, -NEG, ALU.subtract, ALU.mult)
                nc.vector.tensor_scalar(valid1[:, 0:B], valid1_i[:, :], 0.0, None, ALU.not_equal)
                nc.vector.tensor_scalar(mask1_f[32:32 + NG, :], mask1_i[32:32 + NG, :], 0.0, None, ALU.not_equal)\
                    .then_inc(mstep.sem, 1)
                dve.wait_ge(mstep.sem, mstep.at(0))
                nc.vector.tensor_scalar(c.masks[32:32 + NG, :], mask1_f[32:32 + NG, :], 1.0, -NEG,
                                        ALU.subtract, ALU.mult)
                dve.wait_ge(tstep.sem, tstep.at(0))
                nc.vector.tensor_scalar(b2_gated[:, :], b2_bit[:, :], tg[:, 6:7], None, ALU.mult)

        def col(k):
            return cols[:, k:k + 1]

        attention64(nc, c, S, "L0", 1, wq0, wk0, wv0, wo0, True, None, tg[:, 0:1], row(0),
                    loads=Loads(S, "late_load", loads0f + loads1 + loads1f))
        ternary_ffn(nc, c, S, "L0f", True, [wg0, wu0, wd0], tg[:, 4:5],
                    loads=Loads(S, "late_load", [(rel_flipped, rel_src)]))
        attention8(nc, c, S, "L1", wq1, wk1, wv1, wo1, col(0), col(1), row(1), row(2), tg[:, 1:2],
                   rel_bias=rel_bias, rel_flipped=rel_flipped, mask_row=32, valid=valid1)
        experts_ffn(nc, c, S, "L1f", 16, 4, 4, False, [w1_moe], w2_moe, keys1[:, :], tg[:, 5:6],
                    b_up=b1_moe, b_down=b2_moe[:, :], rw=rw1[:, :], rb=rb1[0:1, :],
                    loads=Loads(S, "late_load", loads2 + loads2f + loads3))
        attention64(nc, c, S, "L2", 2, wq2, wk2, wv2, wo2, False, [(col(4), col(5)), (col(6), col(7))],
                    tg[:, 2:3], row(5), loads=Loads(S, "late_load", loads3f))
        ternary_ffn(nc, c, S, "L2f", False, [w1_bit, w2_bit], tg[:, 6:7], hidden_bias=b1_bit[:, :],
                    out_bias=b2_gated[:, :])
        attention8(nc, c, S, "L3", wq3, wk3, wv3, wo3, col(2), col(3), row(3), row(4), tg[:, 3:4])
        experts_ffn(nc, c, S, "L3f", 8, 2, 1, True, [wg3, wu3], wd3, keys3[:, :], tg[:, 7:8])

        saved = S.new("saved", per=16, groups=1)
        with nc.Block() as block:
            @block.sync
            def _(sp):
                sp.dma_start(out, c.x[:, 0:B, :].rearrange("p b d -> p (b d)")).then_inc(saved.sem, 16)
                sp.wait_ge(saved.sem, saved.at(0, 16))



def kernel(**inputs):
    import numpy as np
    import concourse.bacc as bacc
    from concourse.bass_utils import run_bass_kernel_spmd

    a = {k: np.asarray(v) for k, v in inputs.items()}

    def blocks(w):
        return w.reshape(-1, P, w.shape[1]).transpose(1, 0, 2).reshape(P, -1)

    def by_token(v):
        return v.transpose(1, 0, 2).reshape(P, -1)

    host = {
        "x_tok": by_token(a["x"]),
        "ctx_tok": by_token(a["ctx_1024"]),
        "ctxT": a["ctx_1024"].reshape(B * P, D).T,
        "g_xattn": a["g_xattn"],
        "g_ffn": a["g_ffn"],
        "mask0": a["mask_BxS2_bf1"].reshape(NG, W).view(np.uint8),
        "mask1": a["mask_Bx1x1xS2_ik0"].reshape(NG, W),
        "mask1_by_key": a["mask_Bx1x1xS2_ik0"].reshape(B, P).T,
        "headmask": (np.arange(P)[:, None] // 8 % 4 == np.arange(4)[None, :]).astype(np.float32),
        "flip": np.eye(P, dtype=np.float32)[::-1],
        "cols": np.stack([a[k] for k in ("L1_xattn_bq", "L1_xattn_bk", "L3_xattn_bq", "L3_xattn_bk",
                                         "L2_xattn_ln_m_g", "L2_xattn_ln_m_b", "L2_xattn_ln_l_g",
                                         "L2_xattn_ln_l_b")], axis=1),
        "rows": np.concatenate([np.tile(a[k], GB) for k in ("L0_xattn_b_out", "L1_xattn_bv", "L1_xattn_bo",
                                                            "L3_xattn_bv", "L3_xattn_bo")]).reshape(5, -1),
        "L0_wq": a["L0_xattn_Wq"].T,
        "L0_wk": a["L0_xattn_Wkv"][:HEADS * DH].T,
        "L0_wv": a["L0_xattn_Wkv"][HEADS * DH:].T,
        "L0_wo": blocks(a["L0_xattn_Wout"].T),
        "L0_wg": a["L0_ffn_w_gate"].T,
        "L0_wu": a["L0_ffn_w_up"].T,
        "L0_wd": blocks(a["L0_ffn_w_down"].T),
        "L1_wq": a["L1_xattn_Wq"].T,
        "L1_wk": a["L1_xattn_Wk"].T,
        "L1_wv": a["L1_xattn_Wv"].T,
        "L1_wo": a["L1_xattn_Wo"].T,
        "L1_rel": a["L1_xattn_rel_emb"].T,
        "L1_keys": a["L1_ffn_keys"].T,
        "L1_rw": a["L1_ffn_rw"].T,
        "L1_rb": a["L1_ffn_rb"].reshape(1, -1),
        "L1_w1": a["L1_ffn_w1"].transpose(2, 0, 1).reshape(D, -1),
        "L1_b1": a["L1_ffn_b1"].reshape(-1, P).T,
        "L1_w2": a["L1_ffn_w2"].transpose(0, 2, 1).reshape(-1, P, D).transpose(1, 0, 2).reshape(P, -1),
        "L1_b2": a["L1_ffn_b2"],
        "L2_wq": a["L2_xattn_Wq"],
        "L2_wk": a["L2_xattn_Wkv"][:, :HEADS * DH],
        "L2_wv": a["L2_xattn_Wkv"][:, HEADS * DH:],
        "L2_wo": blocks(a["L2_xattn_Wout"]),
        "L2_w1": a["L2_ffn_W1"].T,
        "L2_w2": blocks(a["L2_ffn_W2"].T),
        "L2_b1": a["L2_ffn_b1"],
        "L2_b2": a["L2_ffn_b2"],
        "L3_wq": a["L3_xattn_Wq"],
        "L3_wk": a["L3_xattn_Wk"],
        "L3_wv": a["L3_xattn_Wv"],
        "L3_wo": a["L3_xattn_Wo"],
        "L3_gate_w": a["L3_ffn_gate_w"].T,
        "L3_gate_bank": a["L3_ffn_gate_bank"].transpose(1, 0, 2).reshape(D, -1),
        "L3_up_bank": a["L3_ffn_up_bank"].transpose(1, 0, 2).reshape(D, -1),
        "L3_down_bank": a["L3_ffn_down_bank"].reshape(-1, P, D).transpose(1, 0, 2).reshape(P, -1),
    }
    host = {k: np.ascontiguousarray(v) for k, v in host.items()}
    nc = bacc.Bacc("TRN2", target_bir_lowering=False, num_devices=1)
    d = {k: nc.dram_tensor("in_" + k, v.shape, mybir.dt.from_np(v.dtype), kind="ExternalInput").ap() for k, v in host.items()}
    out = nc.dram_tensor("out_x", (P, B * D), F32, kind="ExternalOutput").ap()
    build(nc, d, out)
    r = run_bass_kernel_spmd(nc, [{"in_" + k: v for k, v in host.items()}], core_ids=[0])
    return r.results[0]["out_x"].reshape(P, B, D).transpose(1, 0, 2)
```
